# Optimizing a Trainium2 kernel written in Bass

```python
import numpy as np
import jax
import jax.numpy as jnp

def _softmax(x, axis=-1):
    return jax.nn.softmax(x, axis=axis)

def _gelu(x):
    return jax.nn.gelu(x, approximate=True)

def _silu(x):
    return jax.nn.silu(x)

def _sigmoid(x):
    return jax.nn.sigmoid(x)

def _layernorm(x, axis=-1, eps=1e-05):
    m = jnp.mean(x, axis=axis, keepdims=True)
    v = jnp.var(x, axis=axis, keepdims=True)
    return (x - m) / jnp.sqrt(v + eps)

def _scatter_add(tgt, idx, src, axis=0):
    return tgt.at[idx].add(src)

def _segment_sum(src, seg, n):
    return jax.ops.segment_sum(src, seg, n)
kernel_name = 'mk_conv_attn_hybrid_d2_conv_nchw256_r2_79b051'

def setup_inputs(seed: int=0):
    np.random.seed(seed)
    _w = jnp.asarray

    def _rec_inputs():
        import jax
        import jax.numpy as jnp
        _gk = jax.random.key(seed)
        x = -0.0003929 + 0.9999 * jax.random.normal(jax.random.fold_in(_gk, 1), (16, 128, 32, 32), jnp.float32)
        return x
    x = _rec_inputs()

    def _L0_conv_setup():
        import jax, jax.numpy as jnp
        import numpy as np
        import itertools
        EPS = 1e-05
        WS = 7
        NH = 4
        KD = 16
        DV = 32

        def _bias_idxs(res):
            pts = list(itertools.product(range(res), range(res)))
            offs, idxs = ({}, [])
            for p1 in pts:
                for p2 in pts:
                    o = (abs(p1[0] - p2[0]), abs(p1[1] - p2[1]))
                    if o not in offs:
                        offs[o] = len(offs)
                    idxs.append(offs[o])
            return np.array(idxs, np.int32).reshape(res * res, res * res)
        IDXS = _bias_idxs(WS)

        def bn(x, p):
            g, b, m, v = p
            sh = (1, -1) + (1,) * (x.ndim - 2)
            return (x - m.reshape(sh)) * (g.reshape(sh) / jnp.sqrt(v.reshape(sh) + EPS)) + b.reshape(sh)

        def dwconv(x, w, pad):
            return jax.lax.conv_general_dilated(x, w, (1, 1), [(pad, pad)] * 2, dimension_numbers=('NCHW', 'OIHW', 'NCHW'), feature_group_count=x.shape[1])

        def pw(x, w, p):
            return bn(jnp.einsum('oc,bcxy->boxy', w, x), p)

        def ffn(x, w1, p1, w2, p2):
            return x + pw(jax.nn.relu(pw(x, w1, p1)), w2, p2)

        def cga(x, qkv_w, qkv_bn, qdw_w, qdw_bn, attn_bias, proj_w, proj_bn):
            Bw, C, H, W = x.shape
            N = H * W
            s = x.reshape(Bw, NH, C // NH, H, W).transpose(0, 2, 1, 3, 4).reshape(Bw, C, H, W)
            heads = s.reshape(Bw, NH, C // NH, H, W)
            f = jnp.einsum('bhcxy,hoc->bhoxy', heads, qkv_w)
            g, b, m, v = (qkv_bn[:, 0], qkv_bn[:, 1], qkv_bn[:, 2], qkv_bn[:, 3])
            sh = (1, NH, 2 * KD + DV, 1, 1)
            f = (f - m.reshape(sh)) * (g.reshape(sh) / jnp.sqrt(v.reshape(sh) + EPS)) + b.reshape(sh)
            q, k, val = (f[:, :, :KD], f[:, :, KD:2 * KD], f[:, :, 2 * KD:])
            q = bn(dwconv(q.reshape(Bw, NH * KD, H, W), qdw_w, 2), qdw_bn).reshape(Bw, NH, KD, H, W)
            qf = q.reshape(Bw, NH, KD, N)
            kf = k.reshape(Bw, NH, KD, N)
            vf = val.reshape(Bw, NH, DV, N)
            bias = attn_bias[:, IDXS]
            attn = jnp.einsum('bhcn,bhcm->bhnm', qf, kf) * KD ** (-0.5) + bias[None]
            attn = jax.nn.softmax(attn, axis=-1)
            out = jnp.einsum('bhdm,bhnm->bhdn', vf, attn).reshape(Bw, NH * DV, H, W)
            return pw(jax.nn.relu(out), proj_w, proj_bn)

        def window_attn(x, qkv_w, qkv_bn, qdw_w, qdw_bn, attn_bias, proj_w, proj_bn):
            B, C, H, W = x.shape
            pad_b, pad_r = (-H % WS, -W % WS)
            xt = jnp.transpose(x, (0, 2, 3, 1))
            xt = jnp.pad(xt, ((0, 0), (0, pad_b), (0, pad_r), (0, 0)))
            pH, pW = (H + pad_b, W + pad_r)
            nH, nW = (pH // WS, pW // WS)
            xw = xt.reshape(B, nH, WS, nW, WS, C).transpose(0, 1, 3, 2, 4, 5)
            xw = xw.reshape(B * nH * nW, WS, WS, C).transpose(0, 3, 1, 2)
            xw = cga(xw, qkv_w, qkv_bn, qdw_w, qdw_bn, attn_bias, proj_w, proj_bn)
            xt = xw.transpose(0, 2, 3, 1).reshape(B, nH, nW, WS, WS, C).transpose(0, 1, 3, 2, 4, 5)
            xt = xt.reshape(B, pH, pW, C)
            return jnp.transpose(xt[:, :H, :W], (0, 3, 1, 2))

        def _bn_params(k, C):
            k1, k2, k3, k4 = jax.random.split(k, 4)
            return jnp.stack([1.0 + 0.1 * jax.random.normal(k1, (C,)), 0.1 * jax.random.normal(k2, (C,)), 0.1 * jax.random.normal(k3, (C,)), jax.random.uniform(k4, (C,), minval=0.5, maxval=1.5)])
        key = jax.random.key(seed)
        ks = jax.random.split(key, 24)
        B, C, H, W = (16, 128, 32, 32)
        d = {}
        d['x'] = jax.random.normal(ks[0], (B, C, H, W), jnp.float32)
        d['dw0_w'] = jax.random.normal(ks[1], (C, 1, 3, 3), jnp.float32) / 3.0
        d['dw0_bn'] = _bn_params(ks[2], C)
        d['ffn0_w1'] = jax.random.normal(ks[3], (2 * C, C), jnp.float32) * C ** (-0.5)
        d['ffn0_bn1'] = _bn_params(ks[4], 2 * C)
        d['ffn0_w2'] = jax.random.normal(ks[5], (C, 2 * C), jnp.float32) * (2 * C) ** (-0.5)
        d['ffn0_bn2'] = _bn_params(ks[6], C)
        d['qkv_w'] = jax.random.normal(ks[7], (NH, 2 * KD + DV, C // NH), jnp.float32) * (C // NH) ** (-0.5)
        d['qkv_bn'] = jnp.stack([_bn_params(jax.random.fold_in(ks[8], i), 2 * KD + DV) for i in range(NH)])
        d['qdw_w'] = jax.random.normal(ks[9], (NH * KD, 1, 5, 5), jnp.float32) / 5.0
        d['qdw_bn'] = _bn_params(ks[10], NH * KD)
        d['attn_bias'] = 0.1 * jax.random.normal(ks[11], (NH, 49), jnp.float32)
        d['proj_w'] = jax.random.normal(ks[12], (C, NH * DV), jnp.float32) * (NH * DV) ** (-0.5)
        d['proj_bn'] = _bn_params(ks[13], C)
        d['dw1_w'] = jax.random.normal(ks[14], (C, 1, 3, 3), jnp.float32) / 3.0
        d['dw1_bn'] = _bn_params(ks[15], C)
        d['ffn1_w1'] = jax.random.normal(ks[16], (2 * C, C), jnp.float32) * C ** (-0.5)
        d['ffn1_bn1'] = _bn_params(ks[17], 2 * C)
        d['ffn1_w2'] = jax.random.normal(ks[18], (C, 2 * C), jnp.float32) * (2 * C) ** (-0.5)
        d['ffn1_bn2'] = _bn_params(ks[19], C)
        return d
    _L0_conv_all = _L0_conv_setup()
    _L0_conv_in = {k: v for k, v in _L0_conv_all.items() if k in ('dw0_w', 'dw0_bn', 'ffn0_w1', 'ffn0_bn1', 'ffn0_w2', 'ffn0_bn2', 'qkv_w', 'qkv_bn', 'qdw_w', 'qdw_bn', 'attn_bias', 'proj_w', 'proj_bn', 'dw1_w', 'dw1_bn', 'ffn1_w1', 'ffn1_bn1', 'ffn1_w2', 'ffn1_bn2')}
    del _L0_conv_all

    def _L1_attn_setup():
        import jax, jax.numpy as jnp
        import numpy as np
        NUM_HEADS = 4
        LN_EPS = 1e-05

        def positional_encoding(length, d_model):
            pos = jnp.arange(length, dtype=jnp.float32)[:, None]
            div = jnp.exp(jnp.arange(0, d_model, 2, dtype=jnp.float32) * (-np.log(10000.0) / d_model))
            pe = jnp.zeros((length, d_model), dtype=jnp.float32)
            pe = pe.at[:, 0::2].set(jnp.sin(pos * div))
            pe = pe.at[:, 1::2].set(jnp.cos(pos * div))
            return pe

        def rel_shift(pos_score):
            B, H, S, _ = pos_score.shape
            padded = jnp.pad(pos_score, ((0, 0), (0, 0), (0, 0), (1, 0)))
            padded = padded.reshape(B, H, S + 1, S)
            return padded[:, :, 1:].reshape(B, H, S, S)
        key = jax.random.key(seed)
        ks = jax.random.split(key, 8)
        B, S, D, H = (8, 1024, 128, NUM_HEADS)
        dh = D // H
        s = 0.02
        return {'inputs': jax.random.normal(ks[0], (B, S, D), dtype=jnp.float32), 'ln_gamma': jnp.ones((D,), jnp.float32), 'ln_beta': jnp.zeros((D,), jnp.float32), 'Wq': jax.random.normal(ks[1], (D, D), jnp.float32) * s, 'bq': jnp.zeros((D,), jnp.float32), 'Wk': jax.random.normal(ks[2], (D, D), jnp.float32) * s, 'bk': jnp.zeros((D,), jnp.float32), 'Wv': jax.random.normal(ks[3], (D, D), jnp.float32) * s, 'bv': jnp.zeros((D,), jnp.float32), 'Wpos': jax.random.normal(ks[4], (D, D), jnp.float32) * s, 'u_bias': jax.random.normal(ks[5], (H, dh), jnp.float32) * s, 'v_bias': jax.random.normal(ks[6], (H, dh), jnp.float32) * s, 'Wout': jax.random.normal(ks[7], (D, D), jnp.float32) * s, 'bout': jnp.zeros((D,), jnp.float32)}
    _L1_attn_all = _L1_attn_setup()
    _L1_attn_in = {k: v for k, v in _L1_attn_all.items() if k in ('ln_gamma', 'ln_beta', 'Wq', 'bq', 'Wk', 'bk', 'Wv', 'bv', 'Wpos', 'u_bias', 'v_bias', 'Wout', 'bout')}
    del _L1_attn_all

    def _L1_ffn_setup():
        import jax, jax.numpy as jnp
        import numpy as np
        TOP_K = 2
        key = jax.random.key(seed)
        ks = jax.random.split(key, 4)
        B, L, D, H, E = (8, 2048, 128, 512, 8)
        s = 0.02
        return {'x': jax.random.normal(ks[0], (B, L, D), jnp.float32), 'Wg': jax.random.normal(ks[1], (D, E), jnp.float32) * s, 'bg': jnp.zeros((E,), jnp.float32), 'W1': jax.random.normal(ks[2], (E, D, H), jnp.float32) * s, 'b1': jnp.zeros((E, H), jnp.float32), 'W2': jax.random.normal(ks[3], (E, H, D), jnp.float32) * s, 'b2': jnp.zeros((E, D), jnp.float32)}
    _L1_ffn_all = _L1_ffn_setup()
    _L1_ffn_in = {k: v for k, v in _L1_ffn_all.items() if k in ('Wg', 'bg', 'W1', 'b1', 'W2', 'b2')}
    del _L1_ffn_all
    return {'x': x, 'L0_conv_dw0_w': _L0_conv_in['dw0_w'], 'L0_conv_dw0_bn': _L0_conv_in['dw0_bn'], 'L0_conv_ffn0_w1': _L0_conv_in['ffn0_w1'], 'L0_conv_ffn0_bn1': _L0_conv_in['ffn0_bn1'], 'L0_conv_ffn0_w2': _L0_conv_in['ffn0_w2'], 'L0_conv_ffn0_bn2': _L0_conv_in['ffn0_bn2'], 'L0_conv_qkv_w': _L0_conv_in['qkv_w'], 'L0_conv_qkv_bn': _L0_conv_in['qkv_bn'], 'L0_conv_qdw_w': _L0_conv_in['qdw_w'], 'L0_conv_qdw_bn': _L0_conv_in['qdw_bn'], 'L0_conv_attn_bias': _L0_conv_in['attn_bias'], 'L0_conv_proj_w': _L0_conv_in['proj_w'], 'L0_conv_proj_bn': _L0_conv_in['proj_bn'], 'L0_conv_dw1_w': _L0_conv_in['dw1_w'], 'L0_conv_dw1_bn': _L0_conv_in['dw1_bn'], 'L0_conv_ffn1_w1': _L0_conv_in['ffn1_w1'], 'L0_conv_ffn1_bn1': _L0_conv_in['ffn1_bn1'], 'L0_conv_ffn1_w2': _L0_conv_in['ffn1_w2'], 'L0_conv_ffn1_bn2': _L0_conv_in['ffn1_bn2'], 'L1_attn_ln_gamma': _L1_attn_in['ln_gamma'], 'L1_attn_ln_beta': _L1_attn_in['ln_beta'], 'L1_attn_Wq': _L1_attn_in['Wq'], 'L1_attn_bq': _L1_attn_in['bq'], 'L1_attn_Wk': _L1_attn_in['Wk'], 'L1_attn_bk': _L1_attn_in['bk'], 'L1_attn_Wv': _L1_attn_in['Wv'], 'L1_attn_bv': _L1_attn_in['bv'], 'L1_attn_Wpos': _L1_attn_in['Wpos'], 'L1_attn_u_bias': _L1_attn_in['u_bias'], 'L1_attn_v_bias': _L1_attn_in['v_bias'], 'L1_attn_Wout': _L1_attn_in['Wout'], 'L1_attn_bout': _L1_attn_in['bout'], 'L1_ffn_Wg': _L1_ffn_in['Wg'], 'L1_ffn_bg': _L1_ffn_in['bg'], 'L1_ffn_W1': _L1_ffn_in['W1'], 'L1_ffn_b1': _L1_ffn_in['b1'], 'L1_ffn_W2': _L1_ffn_in['W2'], 'L1_ffn_b2': _L1_ffn_in['b2']}

def reference(x, L0_conv_dw0_w, L0_conv_dw0_bn, L0_conv_ffn0_w1, L0_conv_ffn0_bn1, L0_conv_ffn0_w2, L0_conv_ffn0_bn2, L0_conv_qkv_w, L0_conv_qkv_bn, L0_conv_qdw_w, L0_conv_qdw_bn, L0_conv_attn_bias, L0_conv_proj_w, L0_conv_proj_bn, L0_conv_dw1_w, L0_conv_dw1_bn, L0_conv_ffn1_w1, L0_conv_ffn1_bn1, L0_conv_ffn1_w2, L0_conv_ffn1_bn2, L1_attn_ln_gamma, L1_attn_ln_beta, L1_attn_Wq, L1_attn_bq, L1_attn_Wk, L1_attn_bk, L1_attn_Wv, L1_attn_bv, L1_attn_Wpos, L1_attn_u_bias, L1_attn_v_bias, L1_attn_Wout, L1_attn_bout, L1_ffn_Wg, L1_ffn_bg, L1_ffn_W1, L1_ffn_b1, L1_ffn_W2, L1_ffn_b2):
    import jax
    import jax.numpy as jnp

    def _L0_conv_ref(x, dw0_w, dw0_bn, ffn0_w1, ffn0_bn1, ffn0_w2, ffn0_bn2, qkv_w, qkv_bn, qdw_w, qdw_bn, attn_bias, proj_w, proj_bn, dw1_w, dw1_bn, ffn1_w1, ffn1_bn1, ffn1_w2, ffn1_bn2):
        import jax, jax.numpy as jnp
        import numpy as np
        import itertools
        EPS = 1e-05
        WS = 7
        NH = 4
        KD = 16
        DV = 32

        def _bias_idxs(res):
            pts = list(itertools.product(range(res), range(res)))
            offs, idxs = ({}, [])
            for p1 in pts:
                for p2 in pts:
                    o = (abs(p1[0] - p2[0]), abs(p1[1] - p2[1]))
                    if o not in offs:
                        offs[o] = len(offs)
                    idxs.append(offs[o])
            return np.array(idxs, np.int32).reshape(res * res, res * res)
        IDXS = _bias_idxs(WS)

        def bn(x, p):
            g, b, m, v = p
            sh = (1, -1) + (1,) * (x.ndim - 2)
            return (x - m.reshape(sh)) * (g.reshape(sh) / jnp.sqrt(v.reshape(sh) + EPS)) + b.reshape(sh)

        def dwconv(x, w, pad):
            return jax.lax.conv_general_dilated(x, w, (1, 1), [(pad, pad)] * 2, dimension_numbers=('NCHW', 'OIHW', 'NCHW'), feature_group_count=x.shape[1])

        def pw(x, w, p):
            return bn(jnp.einsum('oc,bcxy->boxy', w, x), p)

        def ffn(x, w1, p1, w2, p2):
            return x + pw(jax.nn.relu(pw(x, w1, p1)), w2, p2)

        def cga(x, qkv_w, qkv_bn, qdw_w, qdw_bn, attn_bias, proj_w, proj_bn):
            Bw, C, H, W = x.shape
            N = H * W
            s = x.reshape(Bw, NH, C // NH, H, W).transpose(0, 2, 1, 3, 4).reshape(Bw, C, H, W)
            heads = s.reshape(Bw, NH, C // NH, H, W)
            f = jnp.einsum('bhcxy,hoc->bhoxy', heads, qkv_w)
            g, b, m, v = (qkv_bn[:, 0], qkv_bn[:, 1], qkv_bn[:, 2], qkv_bn[:, 3])
            sh = (1, NH, 2 * KD + DV, 1, 1)
            f = (f - m.reshape(sh)) * (g.reshape(sh) / jnp.sqrt(v.reshape(sh) + EPS)) + b.reshape(sh)
            q, k, val = (f[:, :, :KD], f[:, :, KD:2 * KD], f[:, :, 2 * KD:])
            q = bn(dwconv(q.reshape(Bw, NH * KD, H, W), qdw_w, 2), qdw_bn).reshape(Bw, NH, KD, H, W)
            qf = q.reshape(Bw, NH, KD, N)
            kf = k.reshape(Bw, NH, KD, N)
            vf = val.reshape(Bw, NH, DV, N)
            bias = attn_bias[:, IDXS]
            attn = jnp.einsum('bhcn,bhcm->bhnm', qf, kf) * KD ** (-0.5) + bias[None]
            attn = jax.nn.softmax(attn, axis=-1)
            out = jnp.einsum('bhdm,bhnm->bhdn', vf, attn).reshape(Bw, NH * DV, H, W)
            return pw(jax.nn.relu(out), proj_w, proj_bn)

        def window_attn(x, qkv_w, qkv_bn, qdw_w, qdw_bn, attn_bias, proj_w, proj_bn):
            B, C, H, W = x.shape
            pad_b, pad_r = (-H % WS, -W % WS)
            xt = jnp.transpose(x, (0, 2, 3, 1))
            xt = jnp.pad(xt, ((0, 0), (0, pad_b), (0, pad_r), (0, 0)))
            pH, pW = (H + pad_b, W + pad_r)
            nH, nW = (pH // WS, pW // WS)
            xw = xt.reshape(B, nH, WS, nW, WS, C).transpose(0, 1, 3, 2, 4, 5)
            xw = xw.reshape(B * nH * nW, WS, WS, C).transpose(0, 3, 1, 2)
            xw = cga(xw, qkv_w, qkv_bn, qdw_w, qdw_bn, attn_bias, proj_w, proj_bn)
            xt = xw.transpose(0, 2, 3, 1).reshape(B, nH, nW, WS, WS, C).transpose(0, 1, 3, 2, 4, 5)
            xt = xt.reshape(B, pH, pW, C)
            return jnp.transpose(xt[:, :H, :W], (0, 3, 1, 2))

        def _bn_params(k, C):
            k1, k2, k3, k4 = jax.random.split(k, 4)
            return jnp.stack([1.0 + 0.1 * jax.random.normal(k1, (C,)), 0.1 * jax.random.normal(k2, (C,)), 0.1 * jax.random.normal(k3, (C,)), jax.random.uniform(k4, (C,), minval=0.5, maxval=1.5)])
        x = x + bn(dwconv(x, dw0_w, 1), dw0_bn)
        x = ffn(x, ffn0_w1, ffn0_bn1, ffn0_w2, ffn0_bn2)
        x = x + window_attn(x, qkv_w, qkv_bn, qdw_w, qdw_bn, attn_bias, proj_w, proj_bn)
        x = x + bn(dwconv(x, dw1_w, 1), dw1_bn)
        x = ffn(x, ffn1_w1, ffn1_bn1, ffn1_w2, ffn1_bn2)
        return x

    def _L1_attn_ref(inputs, ln_gamma, ln_beta, Wq, bq, Wk, bk, Wv, bv, Wpos, u_bias, v_bias, Wout, bout):
        import jax, jax.numpy as jnp
        import numpy as np
        NUM_HEADS = 4
        LN_EPS = 1e-05

        def positional_encoding(length, d_model):
            pos = jnp.arange(length, dtype=jnp.float32)[:, None]
            div = jnp.exp(jnp.arange(0, d_model, 2, dtype=jnp.float32) * (-np.log(10000.0) / d_model))
            pe = jnp.zeros((length, d_model), dtype=jnp.float32)
            pe = pe.at[:, 0::2].set(jnp.sin(pos * div))
            pe = pe.at[:, 1::2].set(jnp.cos(pos * div))
            return pe

        def rel_shift(pos_score):
            B, H, S, _ = pos_score.shape
            padded = jnp.pad(pos_score, ((0, 0), (0, 0), (0, 0), (1, 0)))
            padded = padded.reshape(B, H, S + 1, S)
            return padded[:, :, 1:].reshape(B, H, S, S)
        B, S, D = inputs.shape
        H = NUM_HEADS
        dh = D // H
        mu = jnp.mean(inputs, axis=-1, keepdims=True)
        var = jnp.mean(jnp.square(inputs - mu), axis=-1, keepdims=True)
        x = (inputs - mu) / jnp.sqrt(var + LN_EPS) * ln_gamma + ln_beta
        pe = positional_encoding(S, D)
        q = (x @ Wq + bq).reshape(B, S, H, dh)
        k = (x @ Wk + bk).reshape(B, S, H, dh)
        v = (x @ Wv + bv).reshape(B, S, H, dh)
        p = (pe @ Wpos).reshape(S, H, dh)
        content_score = jnp.einsum('bshd,bthd->bhst', q + u_bias, k)
        pos_score = jnp.einsum('bshd,thd->bhst', q + v_bias, p)
        pos_score = rel_shift(pos_score)
        score = (content_score + pos_score) / np.sqrt(D).astype(np.float32)
        attn = jax.nn.softmax(score, axis=-1)
        ctx = jnp.einsum('bhst,bthd->bshd', attn, v).reshape(B, S, D)
        return ctx @ Wout + bout

    def _L1_ffn_ref(x, Wg, bg, W1, b1, W2, b2):
        import jax, jax.numpy as jnp
        import numpy as np
        TOP_K = 2
        B, L, D = x.shape
        E = W1.shape[0]
        xf = x.reshape(-1, D)
        gate_logits = xf @ Wg + bg
        top_w, top_i = jax.lax.top_k(gate_logits, TOP_K)
        top_w = jax.nn.softmax(top_w, axis=-1)
        w_dense = jnp.sum(jax.nn.one_hot(top_i, E, dtype=xf.dtype) * top_w[..., None], axis=1)
        out = jnp.zeros_like(xf)
        for e in range(E):
            h = jax.nn.gelu(xf @ W1[e] + b1[e], approximate=False)
            out = out + w_dense[:, e:e + 1] * (h @ W2[e] + b2[e])
        return out.reshape(B, L, D)

    def _gn(v, G=32, eps=1e-05):
        B_, C_, H_, W_ = v.shape
        g = v.reshape(B_, G, C_ // G, H_, W_)
        m = jnp.mean(g, axis=(2, 3, 4), keepdims=True)
        s = jnp.var(g, axis=(2, 3, 4), keepdims=True)
        return ((g - m) / jnp.sqrt(s + eps)).reshape(v.shape)

    def _ln_c(v, eps=1e-06):
        m = jnp.mean(v, axis=1, keepdims=True)
        s = jnp.var(v, axis=1, keepdims=True)
        return (v - m) / jnp.sqrt(s + eps)

    def _ln_t(v, eps=1e-05):
        m = jnp.mean(v, axis=-1, keepdims=True)
        s = jnp.var(v, axis=-1, keepdims=True)
        return (v - m) / jnp.sqrt(s + eps)

    def _to_tokens(v):
        B_, C_, H_, W_ = v.shape
        return v.reshape(B_, C_, H_ * W_).transpose(0, 2, 1)

    def _from_tokens(t, like):
        B_, C_, H_, W_ = like.shape
        return t.transpose(0, 2, 1).reshape(B_, C_, H_, W_)
    x = x + _L0_conv_ref(_gn(x), L0_conv_dw0_w, L0_conv_dw0_bn, L0_conv_ffn0_w1, L0_conv_ffn0_bn1, L0_conv_ffn0_w2, L0_conv_ffn0_bn2, L0_conv_qkv_w, L0_conv_qkv_bn, L0_conv_qdw_w, L0_conv_qdw_bn, L0_conv_attn_bias, L0_conv_proj_w, L0_conv_proj_bn, L0_conv_dw1_w, L0_conv_dw1_bn, L0_conv_ffn1_w1, L0_conv_ffn1_bn1, L0_conv_ffn1_w2, L0_conv_ffn1_bn2)
    t = _to_tokens(x)
    t = t + _L1_attn_ref(_ln_t(t), L1_attn_ln_gamma, L1_attn_ln_beta, L1_attn_Wq, L1_attn_bq, L1_attn_Wk, L1_attn_bk, L1_attn_Wv, L1_attn_bv, L1_attn_Wpos, L1_attn_u_bias, L1_attn_v_bias, L1_attn_Wout, L1_attn_bout)
    t = t + _L1_ffn_ref(_ln_t(t), L1_ffn_Wg, L1_ffn_bg, L1_ffn_W1, L1_ffn_b1, L1_ffn_W2, L1_ffn_b2)
    x = _from_tokens(t, x)
    return x

_drawn_inputs = setup_inputs


def setup_inputs(seed=0):
    import zlib

    import numpy as np

    out = dict(_drawn_inputs(seed))
    spreads = {'L1_attn_ln_gamma': (1.0, 0.6),
     'L1_attn_ln_beta': (0.0, 0.8),
     'L1_attn_bq': (0.0, 0.8),
     'L1_attn_bk': (0.0, 0.8),
     'L1_attn_bv': (0.0, 0.8),
     'L1_attn_bout': (0.0, 0.307),
     'L1_ffn_bg': (0.0, 0.641),
     'L1_ffn_b1': (0.0, 0.8),
     'L1_ffn_b2': (0.0, 0.47)}
    factors = {'L0_conv_attn_bias': 3.398,
     'L1_attn_Wq': 8.0,
     'L1_attn_Wk': 8.0,
     'L1_attn_Wv': 8.0,
     'L1_attn_Wpos': 8.0,
     'L1_attn_u_bias': 8.0,
     'L1_attn_v_bias': 8.0,
     'L1_attn_Wout': 7.451,
     'L1_ffn_Wg': 3.261,
     'L1_ffn_W1': 6.374,
     'L1_ffn_W2': 5.787}
    for name, (base, spread) in spreads.items():
        noise = np.random.default_rng([zlib.crc32(name.encode()), seed]).standard_normal(out[name].shape)
        drawn = base * np.exp(spread * noise) if base else spread * noise
        out[name] = jnp.asarray(drawn.astype(out[name].dtype))
    for name, factor in factors.items():
        out[name] = (out[name] * factor).astype(out[name].dtype)
    return out
```

```python
from contextlib import ExitStack

import numpy as np

import concourse.bass as bass
from concourse import mybir

F32 = mybir.dt.float32
F32R = mybir.dt.float32r
ALU = mybir.AluOpType
ACT = mybir.ActivationFunctionType
AX = mybir.AxisListType

C = 128
T = 1024
P = 128
TT = T // P
HALF = 512
E = 8
HID = 512
MC = HID // P


class Chain:

    def __init__(self, sem, per):
        self.sem, self.per = sem, per

    def begin(self, eng, n):
        self.eng, self.base, self.k = eng, n * self.per, 0

    def step(self, instruction):
        instruction.then_inc(self.sem, 1)
        self.k += 1
        self.eng.wait_ge(self.sem, self.base + self.k)

    def end(self):
        assert self.k == self.per, (self.k, self.per)


def flat(ap):
    return ap.rearrange("p a b -> p (a b)")


def raw(ap):
    return ap.bitcast(F32)


def col_bcast(stat, n):
    return stat.unsqueeze(2).to_broadcast([stat.shape[0], stat.shape[1], n])

def moe_phase(nc, NB, x_dram, out_dram, wg, bg, w1, b1, w2, b2, ident_dram, lower_dram):
    gate_rows = nc.dram_tensor("gate_rows", [NB, E, T], F32, kind="Internal").ap()
    LAG = 2
    NH, NS = 3, 2 * MC
    GROUPS = 2 + 2 * E
    CHUNKS = 2 * E * MC

    with ExitStack() as ctx:
        def sb(name, shape, dt=F32):
            return ctx.enter_context(nc.sbuf_tensor("moe_" + name, shape, dt))

        def sem(name):
            return ctx.enter_context(nc.semaphore("moe_" + name))

        def psum(name, shape):
            return ctx.enter_context(nc.psum_tensor("moe_" + name, shape, F32))

        ident = sb("ident", [P, P])
        lower = sb("lower", [P, E * E])
        w1f = sb("w1f", [P, HID])
        w1h = sb("w1h", [P, E, HID], F32R)
        w1l = sb("w1l", [P, E, HID], F32R)
        w2s = sb("w2s", [P, E, MC, C])
        wgf = sb("wgf", [P, E])
        wgh = sb("wgh", [P, E], F32R)
        wgl = sb("wgl", [P, E], F32R)
        bgb = sb("bgb", [P, E])
        b1s = sb("b1s", [P, E, MC])
        b2s = sb("b2s", [E, C])
        euler = sb("euler", [P, TT * E])
        minus_half = sb("minus_half", [P, TT])
        x = [sb(f"x{k}", [P, T]) for k in range(2)]
        xc = sb("xc", [P, TT, C])
        sq = sb("sq", [P, TT, C])
        total, mean, var, rstd = (sb(s, [P, TT]) for s in ("total", "mean", "var", "rstd"))
        xnh = [sb(f"xnh{k}", [P, T], F32R) for k in range(2)]
        xnl = [sb(f"xnl{k}", [P, T], F32R) for k in range(2)]
        logit = sb("logit", [P, TT, E])
        diff = sb("diff", [P, TT, E])
        above = sb("above", [P, TT, E, E])
        equal = sb("equal", [P, TT, E, E])
        rank = sb("rank", [P, TT * E])
        best = sb("best", [P, TT])
        gate = sb("gate", [P, TT, E])
        gateT = [sb(f"gateT{k}", [E, T]) for k in range(2)]
        gate_all = sb("gate_all", [P, E, T])
        hid = sb("hid", [P, NS, HALF])
        scaled = sb("scaled", [P, HALF])
        acc = [sb(f"acc{k}", [P, T]) for k in range(2)]

        turn_ps = psum("turn_ps", [P, 2, HALF])
        logit_ps = psum("logit_ps", [P, HALF])
        hid_ps = psum("hid_ps", [P, NH, HALF])
        out_ps = psum("out_ps", [P, 2, HALF])
        turn = flat(turn_ps[:])
        turn_tiles = turn.rearrange("p (t c) -> p t c", t=TT)
        logit_tiles = logit_ps[:, 0:TT * E].rearrange("p (t e) -> p t e", t=TT)

        w1_loaded, weights_loaded, w1_used = sem("w1_loaded"), sem("weights_loaded"), sem("w1_used")
        weights_split, consts_set = sem("weights_split"), sem("consts_set")
        x_loaded, x_turned, centred, squared = sem("x_loaded"), sem("x_turned"), sem("centred"), sem("squared")
        var_ready, rstd_ready, normed, norm_turned = sem("var_ready"), sem("rstd_ready"), sem("normed"), sem("norm_turned")
        high_ready, low_ready, logits_ready = sem("high_ready"), sem("low_ready"), sem("logits_ready")
        diff_ready, exp_ready, gates_ready = sem("diff_ready"), sem("exp_ready"), sem("gates_ready")
        gates_turned, gateT_ready, rows_stored = sem("gates_turned"), sem("gateT_ready"), sem("rows_stored")
        gate_spread = [sem(f"gate{e}_spread") for e in range(E)]
        hid_done, gelu_done = sem("hid_done"), sem("gelu_done")
        out_done, out_used = sem("out_done"), sem("out_used")
        stored = [sem(f"stored{k}") for k in range(2)]
        norm_chain = Chain(sem("norm_step"), 3)
        gate_chain = Chain(sem("gate_step"), 9)
        summed = sem("summed")
        block = ctx.enter_context(nc.Block())

        def image_loop(eng, pieces, run):
            for at in sorted(pieces):
                pieces[at](0, 0, True)

            def ahead(n, k):
                return lambda at: pieces[at](n, k, False) if at in pieces else None

            if NB > 2:
                with eng.Fori(0, NB - 2, 2) as n:
                    run(n, 0, ahead(n + 1, 1))
                    run(n + 1, 1, ahead(n + 2, 0))
            run(NB - 2, 0, ahead(NB - 1, 1))
            run(NB - 1, 1, lambda at: None)

        @block.sync
        def _(sp):
            sp.dma_start(ident[:], ident_dram).then_inc(weights_loaded, 16)
            sp.dma_start(lower[:], lower_dram).then_inc(weights_loaded, 16)
            sp.dma_start(wgf[:], wg).then_inc(weights_loaded, 16)
            sp.dma_start(bgb[:], bg.partition_broadcast(P)).then_inc(weights_loaded, 16)
            sp.dma_start(b2s[:], b2).then_inc(weights_loaded, 16)
            sp.dma_start(b1s[:], b1).then_inc(weights_loaded, 16)
            sp.dma_start(w2s[:], w2.rearrange("e (m p) c -> p e m c", p=P)).then_inc(weights_loaded, 16)
            for e in range(E):
                if e:
                    sp.wait_ge(w1_used, e)
                sp.dma_start(w1f[:], w1[e]).then_inc(w1_loaded, 16)

            def load(n, k, first):
                sp.dma_start(x[k][:], x_dram[n]).then_inc(x_loaded, 16)

            def store_rows(n, k, first):
                sp.wait_ge(gateT_ready, n + 1)
                sp.dma_start(gate_rows[n], gateT[k][:]).then_inc(rows_stored, 16)
                sp.wait_ge(rows_stored, 16 * n + 16)
                if first:
                    for e in range(E):
                        sp.dma_start(gate_all[:, e, :], gate_rows[n, e].partition_broadcast(P)).then_inc(gate_spread[e], 16)

            def run(n, k, ahead):
                more = not (isinstance(n, int) and n == NB - 1)
                ahead(0)
                ahead(1)
                for e in range(E if more else 0):
                    sp.wait_ge(out_used, GROUPS * n + 2 + 2 * e + 2)
                    sp.dma_start(gate_all[:, e, :], gate_rows[n + 1, e].partition_broadcast(P)).then_inc(gate_spread[e], 16)
                sp.wait_ge(summed, 2 * E * (n + 1))
                sp.dma_start(out_dram[n], acc[k][:]).then_inc(stored[k], 16)

            image_loop(sp, {0: load, 1: store_rows}, run)
            for k in range(2):
                sp.wait_ge(stored[k], 16 * (NB // 2))

        @block.gpsimd
        def _(pool):
            pool.memset(euler[:], float(np.e)).then_inc(consts_set, 1)
            pool.memset(minus_half[:], -0.5).then_inc(consts_set, 1)
            pool.wait_ge(consts_set, 2)

            def powers(n, k, first):
                pool.wait_ge(var_ready, n + 1)
                pool.tensor_tensor(rstd[:], var[:], minus_half[:], ALU.pow).then_inc(rstd_ready, 1)
                pool.wait_ge(diff_ready, n + 1)
                pool.tensor_tensor(flat(gate[:]), euler[:], flat(diff[:]), ALU.pow).then_inc(exp_ready, 1)

            image_loop(pool, {0: powers}, lambda n, k, ahead: ahead(0))

        @block.scalar
        def _(act):
            def square(n, k, first):
                act.wait_ge(centred, n + 1)
                act.activation(flat(sq[:]), flat(xc[:]), ACT.Square).then_inc(squared, 1)

            def high(n, k, first):
                act.wait_ge(norm_turned, n + 1)
                act.activation(xnh[k][:], turn, ACT.Copy).then_inc(high_ready, 1)

            def gates(n, k, first):
                act.wait_ge(gates_turned, n + 1)
                if not first:
                    act.wait_ge(rows_stored, 16 * (n - 1))
                act.activation(gateT[k][:], turn[0:E, :], ACT.Copy).then_inc(gateT_ready, 1)

            def run(n, k, ahead):
                for g in range(CHUNKS):
                    e, m = g // (2 * MC), g % MC
                    act.wait_ge(hid_done, CHUNKS * n + g + 1)
                    if g % MC == 0:
                        act.wait_ge(out_done, GROUPS * n + (g // MC + 1 if g >= NS else 0))
                    act.activation(hid[:, g % NS, :], hid_ps[:, g % NH, :], ACT.Gelu,
                                   bias=b1s[:, e, m:m + 1]).then_inc(gelu_done, 1)
                    ahead(g)

            act.wait_ge(weights_loaded, 7 * 16)
            image_loop(act, {10: square, 28: high, 50: gates}, run)

        @block.vector
        def _(dve):
            for e in range(E):
                dve.wait_ge(w1_loaded, 16 * (e + 1))
                dve.tensor_copy(w1h[:, e, :], w1f[:]).then_inc(weights_split, 1)
                dve.wait_ge(weights_split, e + 1)
                dve.tensor_tensor(w1l[:, e, :], w1f[:], raw(w1h[:, e, :]), ALU.subtract).then_inc(w1_used, 1)
            dve.wait_ge(weights_loaded, 7 * 16)
            dve.tensor_copy(wgh[:], wgf[:]).then_inc(weights_split, 1)
            dve.wait_ge(weights_split, E + 1)
            dve.tensor_tensor(wgl[:], wgf[:], raw(wgh[:]), ALU.subtract).then_inc(weights_split, 1)

            def centre(n, k, first):
                norm_chain.begin(dve, n)
                dve.wait_ge(x_turned, n + 1)
                norm_chain.step(dve.tensor_reduce(total[:], turn_tiles, AX.X, ALU.add))
                norm_chain.step(dve.tensor_scalar(mean[:], total[:], 1.0 / C, None, ALU.mult))
                dve.tensor_tensor(xc[:], turn_tiles, col_bcast(mean[:], C), ALU.subtract).then_inc(centred, 1)

            def normalise(n, k, first):
                dve.wait_ge(squared, n + 1)
                norm_chain.step(dve.tensor_reduce(total[:], sq[:], AX.X, ALU.add))
                norm_chain.end()
                dve.tensor_scalar(var[:], total[:], 1.0 / C, 1e-5, ALU.mult, ALU.add).then_inc(var_ready, 1)
                dve.wait_ge(rstd_ready, n + 1)
                dve.wait_ge(centred, n + 1)
                dve.tensor_tensor(xc[:], xc[:], col_bcast(rstd[:], C), ALU.mult).then_inc(normed, 1)

            def low(n, k, first):
                dve.wait_ge(norm_turned, n + 1)
                dve.wait_ge(high_ready, n + 1)
                dve.tensor_tensor(xnl[k][:], turn, raw(xnh[k][:]), ALU.subtract).then_inc(low_ready, 1)

            def gating(n, k, first):
                gate_chain.begin(dve, n)
                dve.wait_ge(logits_ready, n + 1)
                gate_chain.step(dve.tensor_tensor(logit[:], logit_tiles, bgb[:].unsqueeze(1).to_broadcast([P, TT, E]), ALU.add))
                other = logit[:].unsqueeze(2).to_broadcast([P, TT, E, E])
                own = logit[:].unsqueeze(3).to_broadcast([P, TT, E, E])
                dve.tensor_tensor(above[:], other, own, ALU.is_gt)
                gate_chain.step(dve.tensor_tensor(equal[:], other, own, ALU.is_equal))
                pairs = equal[:].rearrange("p t e f -> p t (e f)")
                gate_chain.step(dve.tensor_tensor(pairs, pairs, lower[:].unsqueeze(1).to_broadcast([P, TT, E * E]), ALU.mult))
                gate_chain.step(dve.tensor_tensor(above[:], above[:], equal[:], ALU.add))
                dve.tensor_reduce(rank[:], above[:].rearrange("p t e f -> p (t e) f"), AX.X, ALU.add)
                gate_chain.step(dve.tensor_reduce(best[:], logit[:], AX.X, ALU.max))
                dve.tensor_tensor(diff[:], logit[:], col_bcast(best[:], E), ALU.subtract).then_inc(diff_ready, 1)
                dve.wait_ge(exp_ready, n + 1)
                gate_chain.step(dve.scalar_tensor_tensor(flat(gate[:]), rank[:], 1.5, flat(gate[:]), ALU.is_lt, ALU.mult))
                gate_chain.step(dve.tensor_reduce(total[:], gate[:], AX.X, ALU.add))
                gate_chain.step(dve.reciprocal(mean[:], total[:]))
                gate_chain.step(dve.tensor_tensor(gate[:], gate[:], col_bcast(mean[:], E), ALU.mult))
                gate_chain.end()
                dve.tensor_copy(logit[:], gate[:]).then_inc(gates_ready, 1)

            def run(n, k, ahead):
                dve.wait_ge(stored[k], 8 * n if k == 0 else 8 * (n - 1))
                for half in range(2):
                    part = slice(half * HALF, (half + 1) * HALF)
                    dve.wait_ge(out_done, GROUPS * n + half + 1)
                    dve.tensor_tensor(acc[k][:, part], out_ps[:, half, :], x[k][:, part], ALU.add).then_inc(out_used, 1)
                for q in range(2 * E):
                    e, half = divmod(q, 2)
                    part = slice(half * HALF, (half + 1) * HALF)
                    dve.wait_ge(out_done, GROUPS * n + 2 + q + 1)
                    if half == 0:
                        dve.wait_ge(gate_spread[e], 16 * n + 16)
                    if q:
                        dve.wait_ge(summed, 2 * E * n + q)
                    else:
                        dve.wait_ge(out_used, GROUPS * n + 2)
                    dve.tensor_tensor(scaled[:], out_ps[:, half, :], gate_all[:, e, part], ALU.mult).then_inc(out_used, 1)
                    dve.wait_ge(out_used, GROUPS * n + 2 + q + 1)
                    dve.tensor_tensor(acc[k][:, part], acc[k][:, part], scaled[:], ALU.add).then_inc(summed, 1)
                    ahead(q)

            image_loop(dve, {0: centre, 3: normalise, 6: low, 8: gating}, run)

        @block.tensor
        def _(pe):
            def turn_x(n, k, first):
                pe.wait_ge(x_loaded, 16 * n + 16)
                if not first:
                    pe.wait_ge(gateT_ready, n)
                for t in range(TT):
                    last = pe.transpose(turn[:, t * P:(t + 1) * P], x[k][:, t * P:(t + 1) * P], ident[:])
                last.then_inc(x_turned, 1)

            def turn_norm(n, k, first):
                pe.wait_ge(normed, n + 1)
                for t in range(TT):
                    last = pe.transpose(turn[:, t * P:(t + 1) * P], xc[:, t, :], ident[:])
                last.then_inc(norm_turned, 1)

            def logits(n, k, first):
                pe.wait_ge(high_ready, n + 1)
                pe.wait_ge(low_ready, n + 1)
                if not first:
                    pe.wait_ge(gates_ready, n)
                for t in range(TT):
                    cols = slice(t * P, (t + 1) * P)
                    for j, (a, w) in enumerate(((xnh[k], wgh), (xnh[k], wgl), (xnl[k], wgh))):
                        last = pe.matmul(logit_ps[:, t * E:(t + 1) * E], a[:, cols], w[:], start=(j == 0), stop=(j == 2))
                last.then_inc(logits_ready, 1)

            def turn_gates(n, k, first):
                pe.wait_ge(gates_ready, n + 1)
                for t in range(TT):
                    last = pe.transpose(turn[0:E, t * P:(t + 1) * P], logit[:, t, :], ident[:])
                last.then_inc(gates_turned, 1)

            def run(n, k, ahead):
                pe.wait_ge(gateT_ready, n + 1)
                for half in range(2):
                    part = slice(half * HALF, (half + 1) * HALF)
                    pe.wait_ge(out_used, GROUPS * n + half)
                    pe.matmul(out_ps[:, half, :], b2s[:], gateT[k][:, part], start=True, stop=True).then_inc(out_done, 1)

                def first_product(g):
                    e, half, m = g // (2 * MC), g // MC % 2, g % MC
                    part = slice(half * HALF, (half + 1) * HALF)
                    rows = slice(m * P, (m + 1) * P)
                    pe.wait_ge(gelu_done, CHUNKS * n + max(g - NH + 1, 0))
                    for j, (w, a) in enumerate(((w1h, xnh[k]), (w1l, xnh[k]), (w1h, xnl[k]))):
                        last = pe.matmul(hid_ps[:, g % NH, :], w[:, e, rows], a[:, part], start=(j == 0), stop=(j == 2))
                    last.then_inc(hid_done, 1)

                def second_product(g):
                    e, half, m = g // (2 * MC), g // MC % 2, g % MC
                    pe.wait_ge(gelu_done, CHUNKS * n + g + 1)
                    if m == 0:
                        pe.wait_ge(out_used, GROUPS * n + 2 + g // MC - 1)
                    last = pe.matmul(out_ps[:, half, :], w2s[:, e, m, :], hid[:, g % NS, :], start=(m == 0), stop=(m == MC - 1))
                    if m == MC - 1:
                        last.then_inc(out_done, 1)

                for g in range(CHUNKS + LAG):
                    if g < CHUNKS:
                        first_product(g)
                    if g >= LAG:
                        second_product(g - LAG)
                    ahead(g)

            pe.wait_ge(weights_loaded, 7 * 16)
            pe.wait_ge(weights_split, E + 2)
            pe.wait_ge(w1_used, E)
            image_loop(pe, {4: turn_x, 26: turn_norm, 34: logits, 48: turn_gates}, run)


HEADS = 4
DH = C // HEADS
STEPS = TT
BAND = P + 2
NEG = -1e30


def band_of_keys(i):
    return (max(i * P - 2, 0), (i + 1) * P)


def band_of_queries(i):
    return (i * P, min((i + 1) * P + 2, T))


def attention_phase(nc, NB, x_dram, y_dram, gamma, beta, w_qkv, bq, bk, bv, u_bias, v_bias, pos_stack, pos_t,
                    w_out, b_out, ident_dram, rot_dram, keys_dram, masks_dram, heads_dram):
    SCALE = 1.0 / float(np.sqrt(C))

    with ExitStack() as ctx:
        def sb(name, shape, dt=F32):
            return ctx.enter_context(nc.sbuf_tensor("att_" + name, shape, dt))

        def sem(name):
            return ctx.enter_context(nc.semaphore("att_" + name))

        def psum(name, shape):
            return ctx.enter_context(nc.psum_tensor("att_" + name, shape, F32))

        ident = sb("ident", [P, P])
        identr = sb("identr", [P, P], F32R)
        masks = sb("masks", [P, 6, BAND], F32R)
        cos_t, sin_t = sb("cos_t", [P, T]), sb("sin_t", [P, T])
        keys_h = sb("keys_h", [P, 2, T], F32R)
        keys_l = sb("keys_l", [P, 2, T], F32R)
        wh, wl = sb("wh", [P, 3, C], F32R), sb("wl", [P, 3, C], F32R)
        posw = sb("posw", [3 * DH, HEADS, 2, C], F32R)
        pos_part = sb("pos_part", [3 * DH, HEADS, 2, C], F32R)
        wpos = sb("wpos", [P, 2, C])
        wout = sb("wout", [P, C])
        vec = sb("vec", [P, 8])
        bias_q, bias_out = sb("bias_q", [P, 1]), sb("bias_out", [P, 1])
        head_of, v_less_u = sb("head_of", [P, HEADS]), sb("v_less_u", [P, HEADS])
        mask_u = sb("mask_u", [P, HEADS])
        pos_bias = sb("pos_bias", [P, 2, HEADS])
        minus_half = sb("minus_half", [P, TT])
        x, xres = sb("x", [P, T]), sb("xres", [P, T])
        xc = sb("xc", [P, TT, C])
        sq = sb("sq", [P, TT, C])
        total, mean, var, rstd = (sb(s, [P, TT]) for s in ("total", "mean", "var", "rstd"))
        z = sb("z", [P, T])
        zh, zl = sb("zh", [P, T], F32R), sb("zl", [P, T], F32R)
        q, k = sb("q", [P, T]), sb("k", [P, T])
        qh, ql, kh, kl = (sb(s, [P, T], F32R) for s in ("qh", "ql", "kh", "kl"))
        qs = sb("qs", [3 * DH + 1, HEADS, T], F32R)
        ks = sb("ks", [3 * DH + 1, HEADS, T], F32R)
        vals = sb("vals", [P, TT, HEADS, 2 * DH])
        turned = sb("turned", [P, 2, HALF])
        rotated_f = sb("rotated_f", [P, HALF])
        rot_h = [sb(f"rot_h{j}", [P, T + 2], F32R) for j in range(2)]
        rot_l = [sb(f"rot_l{j}", [P, T + 2], F32R) for j in range(2)]
        neg_max = sb("neg_max", [P, TT])
        weights = [sb(f"weights{j}", [P, T + 2 * BAND]) for j in range(2)]
        recip = sb("recip", [DH, T])
        context = sb("context", [P, T])
        y = sb("y", [P, T])

        score_ps = psum("score_ps", [P, 3 * HALF])
        scratch = psum("scratch", [P, 3 * HALF])
        sum_ps = psum("sum_ps", [P, T])
        scratch_tiles = scratch[:, 0:T].rearrange("p (t c) -> p t c", t=TT)

        consts_set, loaded, staged, split_step, setup_ps, setup_step = (
            sem(s) for s in ("consts_set", "loaded", "staged", "split_step", "setup_ps", "setup_step"))
        keys_staged = sem("keys_staged")
        x_loaded, squared, var_ready, rstd_ready, normed = (
            sem(s) for s in ("x_loaded", "squared", "var_ready", "rstd_ready", "normed"))
        z_high, q_high, k_high = sem("z_high"), sem("q_high"), sem("k_high")
        z_low, q_low, k_low = sem("z_low"), sem("q_low"), sem("k_low")
        stack_loaded = [sem(f"stack{h}_loaded") for h in range(HEADS)]
        scratch_filled, scratch_read = sem("scratch_filled"), sem("scratch_read")
        rotated, scores_done, exps_done, band_step, weights_ready = (
            sem(s) for s in ("rotated", "scores_done", "exps_done", "band_step", "weights_ready"))
        sums_done, context_ready, xres_loaded, stored = (
            sem(s) for s in ("sums_done", "context_ready", "xres_loaded", "stored"))
        norm_chain = Chain(sem("norm_step"), 3)
        rot_chain = Chain(sem("rot_step"), 3)
        context_chain = Chain(sem("context_step"), 1)
        block = ctx.enter_context(nc.Block())

        before = {0: ["R0"], 1: ["R1"], 2: ["M1"], 3: ["M2"], 4: ["M3"], 5: ["M4"], 6: ["M6"], 7: ["X"]}
        after = {1: ["M0"], 5: ["M5"], 6: ["M7"]}
        image_items = {(0, 0): "V", (0, 2): "O", (0, 3): "TX", (1, 3): "TN", (2, 0): "Q", (2, 2): "K"}
        first_items = ["TX", "TN", "Q", "K", "R0", "R1"] + [f"M{i}" for i in range(TT)] + ["X"]

        order = []
        for h in range(HEADS):
            for i in range(STEPS):
                for name in before[i] + after.get(i, []):
                    order.append((name, h))
                if (h, i) in image_items:
                    order.append((image_items[h, i], None))
        OF_NEXT_IMAGE = ("TX", "TN", "Q", "K")
        FIRST = len(first_items)

        def is_first(n):
            return isinstance(n, int) and n == 0

        def is_last(n):
            return isinstance(n, int) and n == NB - 1

        def number_of(n, name, h=None):
            ahead = order[:order.index((name, h))]
            if is_first(n):
                return FIRST + sum(other != "O" for other, _ in ahead)
            if is_last(n):
                ahead = [other for other in ahead if other[0] not in OF_NEXT_IMAGE]
            return FIRST - 1 + len(order) * n + len(ahead)

        def prepared_number(n, name):
            return first_items.index(name) if is_first(n) else number_of(n - 1, name)

        left_out = len(OF_NEXT_IMAGE) + 2 + TT + 1
        LAST_O = FIRST - 1 + len(order) * NB - left_out

        def image_loop(eng, prologue, step):
            for number, item in enumerate(first_items):
                prologue(item, number)

            def image(n):
                number = number_of(n, *order[0])
                for h in range(HEADS):
                    for i in range(STEPS):
                        placed = []
                        for names in (before[i], after.get(i, []) + ([image_items[h, i]] if (h, i) in image_items else [])):
                            numbered = []
                            for name in names:
                                by_head = name not in ("V", "O") + OF_NEXT_IMAGE
                                if is_last(n) and (name in OF_NEXT_IMAGE or (by_head and h == HEADS - 1)):
                                    continue
                                if is_first(n) and name == "O":
                                    continue
                                image_of = n - 1 if name == "O" else n + 1 if name in OF_NEXT_IMAGE or (by_head and h == HEADS - 1) else n
                                numbered.append((name, number, image_of, (h + 1) % HEADS))
                                number = number + 1
                            placed.append(numbered)
                        step(n, h, i, *placed)

            image(0)
            if NB > 2:
                with eng.Fori(1, NB - 1) as n:
                    image(n)
            image(NB - 1)

        @block.sync
        def _(sp):
            sp.dma_start(ident[:], ident_dram).then_inc(loaded, 16)
            sp.dma_start(cos_t[:], rot_dram[0]).then_inc(loaded, 16)
            sp.dma_start(sin_t[:], rot_dram[1]).then_inc(loaded, 16)
            sp.dma_start(z[:, 0:6 * BAND], masks_dram).then_inc(loaded, 16)
            sp.dma_start(sq[:, 0:3, :], w_qkv).then_inc(loaded, 16)
            sp.dma_start(flat(xc[0:3 * DH, :, :]), pos_stack).then_inc(loaded, 16)
            sp.dma_start(wpos[:], pos_t).then_inc(loaded, 16)
            sp.dma_start(wout[:], w_out).then_inc(loaded, 16)
            sp.dma_start(head_of[:], heads_dram).then_inc(loaded, 16)
            for j, v in enumerate((gamma, beta, bq, bk, bv, u_bias, v_bias, b_out)):
                sp.dma_start(vec[:, j:j + 1], v).then_inc(loaded, 16)
            sp.dma_start(q[:], keys_dram[0]).then_inc(keys_staged, 16)
            sp.dma_start(k[:], keys_dram[1]).then_inc(keys_staged, 16)

            def load_stack(h):
                rows = slice(h * DH, (h + 1) * DH)
                for j, (a, b) in enumerate(((qh, kh), (ql, kh), (qh, kl))):
                    to = slice(j * DH, (j + 1) * DH)
                    sp.dma_start(raw(qs[to, h, :]), raw(a[rows, :])).then_inc(stack_loaded[h], 16)
                    sp.dma_start(raw(ks[to, h, :]), raw(b[rows, :])).then_inc(stack_loaded[h], 16)

            sp.dma_start(x[:], x_dram[0]).then_inc(x_loaded, 16)
            sp.wait_ge(q_low, 1)
            sp.wait_ge(k_low, 1)
            for h in range(HEADS):
                load_stack(h)

            def image(n):
                if not is_first(n):
                    sp.wait_ge(scores_done, HEADS * STEPS * n)
                    load_stack(HEADS - 1)
                    sp.dma_start(xres[:], x_dram[n - 1]).then_inc(xres_loaded, 16)
                    sp.wait_ge(scratch_read, number_of(n, "O") + 1)
                    sp.dma_start(y_dram[n - 1], y[:]).then_inc(stored, 16)
                if not is_last(n):
                    sp.wait_ge(scratch_filled, prepared_number(n, "TX") + 1)
                    sp.dma_start(x[:], x_dram[n + 1]).then_inc(x_loaded, 16)
                    sp.wait_ge(k_low, n + 2)
                    for h in range(HEADS - 1):
                        if h:
                            sp.wait_ge(scores_done, HEADS * STEPS * n + STEPS * (h + 1))
                        load_stack(h)

            image(0)
            if NB > 2:
                with sp.Fori(1, NB - 1) as n:
                    image(n)
            image(NB - 1)
            sp.dma_start(xres[:], x_dram[NB - 1]).then_inc(xres_loaded, 16)
            sp.wait_ge(scratch_read, LAST_O + 1)
            sp.dma_start(y_dram[NB - 1], y[:]).then_inc(stored, 16)
            sp.wait_ge(stored, 16 * NB)

        @block.gpsimd
        def _(pool):
            pool.memset(minus_half[:], -0.5).then_inc(consts_set, 1)
            pool.memset(vals[:, :, :, DH:2 * DH], 1.0).then_inc(consts_set, 1)
            pool.wait_ge(consts_set, 2)
            pool.memset(raw(ks[3 * DH:3 * DH + 1, :, :]), 1.0).then_inc(consts_set, 1)
            pool.wait_ge(consts_set, 3)
            for j in range(2):
                pool.memset(raw(rot_h[j][:, T:T + 2]), 0.0).then_inc(consts_set, 1)
                pool.memset(raw(rot_l[j][:, T:T + 2]), 0.0).then_inc(consts_set, 1)
            pool.wait_ge(consts_set, 7)

            def rstd_of(n):
                pool.wait_ge(var_ready, n + 1)
                pool.tensor_tensor(rstd[:], var[:], minus_half[:], ALU.pow).then_inc(rstd_ready, 1)

            def prologue(item, number):
                if item == "TX":
                    rstd_of(0)

            def step(n, h, i, before, after):
                J = HEADS * STEPS * n + STEPS * h + i
                w = weights[i % 2]
                a, b = band_of_keys(i)
                pool.wait_ge(exps_done, J + 1)
                pool.tensor_tensor(w[:, a:b], w[:, a:b], w[:, T:T + b - a], ALU.add).then_inc(band_step, 1)
                pool.wait_ge(band_step, J + 1)
                pool.tensor_tensor(w[:, a:b], w[:, a:b], w[:, T + b - a:T + 2 * (b - a)], ALU.add).then_inc(weights_ready, 1)
                if (h, i) == (0, 5) and not is_last(n):
                    rstd_of(n + 1)

            image_loop(pool, prologue, step)

        @block.scalar
        def _(act):
            act.wait_ge(loaded, 17 * 16)
            act.wait_ge(setup_step, 5)
            act.wait_ge(consts_set, 7)

            def consume(item, number, image, head):
                if item in ("V", "TN", "Q", "K", "X"):
                    act.wait_ge(scratch_filled, number + 1)
                if item == "V":
                    act.activation(vals[:, :, :, 0:DH], scratch[:, 0:T].rearrange("p (t h d) -> p t h d", t=TT, h=HEADS),
                                   ACT.Copy).then_inc(scratch_read, 1)
                elif item == "TN":
                    act.activation(z[:], scratch[:, 0:T], ACT.Identity, bias=vec[:, 1:2], scale=vec[:, 0:1]).then_inc(scratch_read, 1)
                elif item == "Q":
                    act.activation(q[:], scratch[:, 0:T], ACT.Identity, bias=bias_q[:]).then_inc(scratch_read, 1)
                elif item == "K":
                    act.activation(k[:], scratch[:, 0:T], ACT.Identity, bias=vec[:, 3:4]).then_inc(scratch_read, 1)
                elif item == "X":
                    act.activation(qs[3 * DH:3 * DH + 1, head, :], scratch[0:1, 0:T], ACT.Copy).then_inc(scratch_read, 1)

            def square(n):
                act.wait_ge(scratch_read, prepared_number(n, "TX") + 1)
                act.activation(flat(sq[:]), flat(xc[:]), ACT.Square).then_inc(squared, 1)

            def prologue(item, number):
                consume(item, number, 0, 0)
                if item == "TX":
                    square(0)

            def step(n, h, i, before, after):
                J = HEADS * STEPS * n + STEPS * h + i
                act.wait_ge(scores_done, J + 1)
                if not is_first(n) or STEPS * h + i >= 2:
                    act.wait_ge(sums_done, J - 1)
                a, b = band_of_keys(i)
                width = T + 2 * (b - a)
                act.activation(weights[i % 2][:, 0:width], score_ps[:, 0:width], ACT.Exp, scale=SCALE).then_inc(exps_done, 1)
                for item in before + after:
                    consume(*item)
                if (h, i) == (0, 4) and not is_last(n):
                    square(n + 1)

            image_loop(act, prologue, step)

        @block.vector
        def _(dve):
            dve.wait_ge(loaded, 17 * 16)
            dve.tensor_copy(identr[:], ident[:])
            dve.tensor_copy(flat(masks[:]), z[:, 0:6 * BAND])
            dve.tensor_copy(wh[:], sq[:, 0:3, :]).then_inc(split_step, 1)
            dve.wait_ge(split_step, 1)
            dve.tensor_tensor(wl[:], sq[:, 0:3, :], raw(wh[:]), ALU.subtract).then_inc(split_step, 1)
            pos_flat = posw[:].rearrange("p h s c -> p (h s c)")
            part_flat = pos_part[:].rearrange("p h s c -> p (h s c)")
            source = flat(xc[0:3 * DH, :, :])
            low_rows = slice(2 * DH, 3 * DH)
            dve.tensor_copy(pos_flat[0:2 * DH, :], source[0:2 * DH, :])
            dve.tensor_copy(part_flat[low_rows, :], source[low_rows, :]).then_inc(split_step, 1)
            dve.wait_ge(split_step, 3)
            dve.tensor_tensor(pos_flat[low_rows, :], source[low_rows, :], raw(part_flat[low_rows, :]), ALU.subtract).then_inc(split_step, 1)
            dve.wait_ge(keys_staged, 32)
            for j, source_of in enumerate((q, k)):
                dve.tensor_copy(keys_h[:, j, :], source_of[:]).then_inc(split_step, 1)
                dve.wait_ge(split_step, 5 + j)
                dve.tensor_tensor(keys_l[:, j, :], source_of[:], raw(keys_h[:, j, :]), ALU.subtract).then_inc(setup_step, 1)
            dve.tensor_scalar(v_less_u[:], head_of[:], vec[:, 6:7], None, ALU.mult).then_inc(split_step, 1)
            dve.tensor_scalar(mask_u[:], head_of[:], vec[:, 5:6], None, ALU.mult).then_inc(split_step, 1)
            dve.wait_ge(split_step, 8)
            dve.tensor_tensor(v_less_u[:], v_less_u[:], mask_u[:], ALU.subtract).then_inc(setup_step, 1)
            dve.tensor_tensor(bias_q[:], vec[:, 2:3], vec[:, 5:6], ALU.add).then_inc(setup_step, 1)
            dve.wait_ge(setup_ps, 1)
            dve.tensor_copy(flat(pos_bias[:]), scratch[:, 0:2 * HEADS])
            dve.tensor_tensor(bias_out[:], scratch[:, 2 * HEADS:2 * HEADS + 1], vec[:, 7:8], ALU.add).then_inc(setup_step, 1)
            dve.wait_ge(setup_step, 5)

            def rotate(half, number, image, head):
                part = slice(half * HALF, (half + 1) * HALF)
                rot_chain.begin(dve, 2 * (HEADS * image + head) + half)
                dve.wait_ge(scratch_filled, number + 1)
                dve.scalar_tensor_tensor(turned[:, 0, :], scratch[:, 0:HALF], pos_bias[:, 0, head:head + 1], cos_t[:, part], ALU.add, ALU.mult)
                ins = dve.scalar_tensor_tensor(turned[:, 1, :], scratch[:, HALF:2 * HALF], pos_bias[:, 1, head:head + 1], sin_t[:, part], ALU.add, ALU.mult)
                ins.then_inc(scratch_read, 1)
                dve.wait_ge(scratch_read, number + 1)
                rot_chain.step(dve.tensor_tensor(rotated_f[:], turned[:, 0, :], turned[:, 1, :], ALU.add))
                rot_chain.step(dve.tensor_copy(rot_h[head % 2][:, part], rotated_f[:]))
                rot_chain.step(dve.tensor_tensor(rot_l[head % 2][:, part], rotated_f[:], raw(rot_h[head % 2][:, part]), ALU.subtract))
                rot_chain.end()

            def consume(item, number, image, head):
                if item[0] == "R":
                    rotate(int(item[1]), number, image, head)
                elif item[0] == "M":
                    i = int(item[1])
                    a, b = band_of_queries(i)
                    dve.wait_ge(scratch_filled, number + 1)
                    dve.tensor_reduce(neg_max[:, i:i + 1], scratch[:, 0:T + 2 * (b - a)], AX.X, ALU.max, negate=True).then_inc(scratch_read, 1)
                elif item == "TX":
                    norm_chain.begin(dve, image)
                    dve.wait_ge(scratch_filled, number + 1)
                    norm_chain.step(dve.tensor_reduce(total[:], scratch_tiles, AX.X, ALU.add))
                    norm_chain.step(dve.tensor_scalar(mean[:], total[:], 1.0 / C, None, ALU.mult))
                    dve.tensor_tensor(xc[:], scratch_tiles, col_bcast(mean[:], C), ALU.subtract).then_inc(scratch_read, 1)
                elif item == "O":
                    dve.wait_ge(scratch_filled, number + 1)
                    dve.wait_ge(xres_loaded, 16 * image + 16)
                    if not is_first(image):
                        dve.wait_ge(stored, 16 * image)
                    dve.scalar_tensor_tensor(y[:], scratch[:, 0:T], bias_out[:], xres[:], ALU.add, ALU.add).then_inc(scratch_read, 1)

            def variance(n):
                dve.wait_ge(squared, n + 1)
                norm_chain.step(dve.tensor_reduce(total[:], sq[:], AX.X, ALU.add))
                norm_chain.end()
                dve.tensor_scalar(var[:], total[:], (1.0 + 1e-5) / C, 1e-10, ALU.mult, ALU.add).then_inc(var_ready, 1)

            def normalise(n):
                dve.wait_ge(rstd_ready, n + 1)
                dve.tensor_tensor(xc[:], xc[:], col_bcast(rstd[:], C), ALU.mult).then_inc(normed, 1)

            def split_z(n):
                dve.wait_ge(scratch_read, prepared_number(n, "TN") + 1)
                dve.tensor_copy(zh[:], z[:]).then_inc(z_high, 1)
                dve.wait_ge(z_high, n + 1)
                dve.tensor_tensor(zl[:], z[:], raw(zh[:]), ALU.subtract).then_inc(z_low, 1)

            def split_q(n):
                dve.wait_ge(scratch_read, prepared_number(n, "Q") + 1)
                if not is_first(n):
                    dve.wait_ge(stack_loaded[HEADS - 1], 96 * n)
                dve.tensor_copy(qh[:], q[:]).then_inc(q_high, 1)
                dve.wait_ge(q_high, n + 1)
                dve.tensor_tensor(ql[:], q[:], raw(qh[:]), ALU.subtract).then_inc(q_low, 1)

            def split_k(n):
                dve.wait_ge(scratch_read, prepared_number(n, "K") + 1)
                dve.tensor_copy(kh[:], k[:]).then_inc(k_high, 1)
                dve.wait_ge(k_high, n + 1)
                dve.tensor_tensor(kl[:], k[:], raw(kh[:]), ALU.subtract).then_inc(k_low, 1)

            def normalise_head(hh, h):
                context_chain.begin(dve, hh)
                dve.wait_ge(sums_done, STEPS * hh + STEPS)
                context_chain.step(dve.reciprocal(recip[:], sum_ps[DH:2 * DH, :]))
                context_chain.end()
                dve.tensor_tensor(context[h * DH:(h + 1) * DH, :], sum_ps[0:DH, :], recip[:], ALU.mult).then_inc(context_ready, 1)

            def prologue(item, number):
                consume(item, number, 0, 0)
                if item == "TX":
                    variance(0)
                    normalise(0)
                elif item == "TN":
                    split_z(0)
                elif item == "Q":
                    split_q(0)
                elif item == "K":
                    split_k(0)

            later = {(0, 5): variance, (0, 7): normalise, (1, 4): split_z, (2, 1): split_q, (2, 3): split_k}

            def step(n, h, i, before, after):
                for item in before:
                    consume(*item)
                if i == 0 and not (is_first(n) and h == 0):
                    normalise_head(HEADS * n + h - 1, (h - 1) % HEADS)
                for item in after:
                    consume(*item)
                if (h, i) in later and not is_last(n):
                    later[h, i](n + 1)

            image_loop(dve, prologue, step)
            normalise_head(HEADS * NB - 1, HEADS - 1)
            consume("O", LAST_O, NB - 1, 0)

        @block.tensor
        def _(pe):
            pe.wait_ge(loaded, 17 * 16)
            pe.wait_ge(setup_step, 4)
            for s in range(2):
                pe.matmul(scratch[:, s * HEADS:(s + 1) * HEADS], wpos[:, s, :], v_less_u[:], start=True, stop=True)
            pe.matmul(scratch[:, 2 * HEADS:2 * HEADS + 1], wout[:], vec[:, 4:5], start=True, stop=True).then_inc(setup_ps, 1)
            pe.wait_ge(setup_step, 5)
            pe.wait_ge(consts_set, 7)

            def total_up(bank_of, products):
                first, last = {}, {}
                for j, (a, b, _, _) in enumerate(products):
                    first.setdefault(a // HALF, j)
                    last[a // HALF] = j
                for j, (a, b, left, right) in enumerate(products):
                    ins = pe.matmul(bank_of[:, a:b], left, right, start=(first[a // HALF] == j), stop=(last[a // HALF] == j),
                                    skip_group_check=True)
                return ins

            def by_bank(a, b):
                while a < b:
                    end = min(b, (a // HALF + 1) * HALF)
                    yield a, end
                    a = end

            def scores(h, i):
                keys = slice(i * P, (i + 1) * P)
                a, b = band_of_keys(i)
                nxt, between = T, T + b - a
                cut = a - (i * P - 2)
                rh, rl = rot_h[h % 2], rot_l[h % 2]
                products = []
                stacked = ks[:, h, keys]
                for c in (0, HALF):
                    products.append((c, c + HALF, stacked, qs[:, h, c:c + HALF]))
                products.append((nxt, nxt + b - a, stacked, qs[:, h, a:b]))
                products.append((between, between + b - a, stacked, qs[:, h, a:b]))
                for kt, r in ((keys_h, rh), (keys_h, rl), (keys_l, rh)):
                    for c, d in by_bank(a, T):
                        products.append((c, d, kt[:, 0, keys], r[:, c:d]))
                    for c, d in by_bank(0, a):
                        products.append((c, d, kt[:, 1, keys], r[:, c + 1:d + 1]))
                    products.append((nxt, nxt + b - a, kt[:, 1, keys], r[:, a + 1:b + 1]))
                for c, d in by_bank(a, b):
                    products.append((c, d, identr[:], masks[:, 0, cut + c - a:cut + d - a]))
                for kind, c in ((1, nxt), (2, between)):
                    products.append((c, c + b - a, identr[:], masks[:, kind, cut:BAND]))
                total_up(score_ps, products).then_inc(scores_done, 1)

            def maxima(h, i):
                tile = slice(i * P, (i + 1) * P)
                after_tile = slice(i * P + 1, (i + 1) * P + 1)
                a, b = band_of_queries(i)
                nxt, between = T, T + b - a
                rh = rot_h[h % 2]
                stacked = qs[0:3 * DH, h, tile]
                products = [(c, c + HALF, stacked, ks[0:3 * DH, h, c:c + HALF]) for c in (0, HALF)]
                products.append((nxt, nxt + b - a, stacked, ks[0:3 * DH, h, a:b]))
                products.append((between, between + b - a, stacked, ks[0:3 * DH, h, a:b]))
                for c, d in by_bank(0, b):
                    products.append((c, d, rh[:, tile], keys_h[:, 0, c:d]))
                for c, d in by_bank(b, T):
                    products.append((c, d, rh[:, after_tile], keys_h[:, 1, c:d]))
                products.append((nxt, nxt + b - a, rh[:, after_tile], keys_h[:, 1, a:b]))
                for c, d in by_bank(a, b):
                    products.append((c, d, identr[:], masks[:, 3, c - a:d - a]))
                for kind, c in ((4, nxt), (5, between)):
                    products.append((c, c + b - a, identr[:], masks[:, kind, 0:b - a]))
                return total_up(scratch, products)

            def fill(item, number, image, head):
                pe.wait_ge(scratch_read, number)
                if item == "TX":
                    pe.wait_ge(x_loaded, 16 * image + 16)
                    for t in range(TT):
                        last = pe.transpose(scratch[:, t * P:(t + 1) * P], x[:, t * P:(t + 1) * P], ident[:])
                elif item == "TN":
                    pe.wait_ge(normed, image + 1)
                    for t in range(TT):
                        last = pe.transpose(scratch[:, t * P:(t + 1) * P], xc[:, t, :], ident[:])
                elif item in ("Q", "K"):
                    pe.wait_ge(z_low, image + 1)
                    w = 0 if item == "Q" else 1
                    last = total_up(scratch, [(c, c + HALF, a[:, w, :], b[:, c:c + HALF])
                                              for a, b in ((wh, zh), (wl, zh), (wh, zl)) for c in (0, HALF)])
                elif item == "V":
                    last = total_up(scratch, [(t * P, (t + 1) * P, b[:, t * P:(t + 1) * P], a[:, 2, :])
                                              for a, b in ((wh, zh), (wl, zh), (wh, zl)) for t in range(TT)])
                elif item[0] == "R":
                    part = slice(int(item[1]) * HALF, (int(item[1]) + 1) * HALF)
                    pe.wait_ge(stack_loaded[head], 96 * (image + 1))
                    last = total_up(scratch, [(s * HALF, (s + 1) * HALF, posw[:, head, s, :], qs[0:3 * DH, head, part])
                                              for s in range(2)])
                elif item[0] == "M":
                    if item == "M0":
                        pe.wait_ge(rot_chain.sem, 6 * (HEADS * image + head) + 6)
                    last = maxima(head, int(item[1]))
                elif item == "X":
                    for t in range(TT):
                        last = pe.transpose(scratch[0:1, t * P:(t + 1) * P], neg_max[:, t:t + 1], ident[:])
                elif item == "O":
                    pe.wait_ge(context_ready, HEADS * (image + 1))
                    for c in (0, HALF):
                        last = pe.matmul(scratch[:, c:c + HALF], wout[:], context[:, c:c + HALF], start=True, stop=True)
                last.then_inc(scratch_filled, 1)

            def sum_values(n, h, i):
                J = HEADS * STEPS * n + STEPS * h + i
                pe.wait_ge(weights_ready, J + 1)
                if i == 0:
                    if h == 0:
                        pe.wait_ge(scratch_read, number_of(n, "V") + 1)
                    if not (is_first(n) and h == 0):
                        pe.wait_ge(context_ready, HEADS * n + h)
                for c in (0, HALF):
                    last = pe.matmul(sum_ps[0:2 * DH, c:c + HALF], vals[:, i, h, :], weights[i % 2][:, c:c + HALF],
                                     start=(i == 0), stop=(i == STEPS - 1))
                last.then_inc(sums_done, 1)

            def step(n, h, i, before, after):
                J = HEADS * STEPS * n + STEPS * h + i
                if not (is_first(n) and h == 0 and i == 0):
                    pe.wait_ge(exps_done, J)
                if i == 0:
                    if h == 0:
                        pe.wait_ge(scratch_read, number_of(n, *order[0]))
                    else:
                        pe.wait_ge(scratch_read, number_of(n, "X", h - 1) + 1)
                scores(h, i)
                for item in before:
                    fill(*item)
                if i:
                    sum_values(n, h, i - 1)
                elif h:
                    sum_values(n, h - 1, STEPS - 1)
                elif not is_first(n):
                    sum_values(n - 1, HEADS - 1, STEPS - 1)
                for item in after:
                    fill(*item)

            image_loop(pe, lambda item, number: fill(item, number, 0, 0), step)
            sum_values(NB - 1, HEADS - 1, STEPS - 1)
            fill("O", LAST_O, NB - 1, 0)


SIDE = 32
WS = 7
NW = 5
WIN = WS * WS
WINDOWS = NW * NW
SLOTS = (WINDOWS + 1) // 2
PITCH = WS + 2
QROW = PITCH * WS
EPS = 1e-5
BN = ("dw0", "ffn0_in0", "ffn0_in1", "ffn0_out", "q", "k_first", "k_second", "value", "qdw", "proj",
      "dw1", "ffn1_in0", "ffn1_in1", "ffn1_out")
AT_WINDOW_SCALE = 0.25


def conv_phase(nc, NB, x_dram, y_dram, bn_dram, taps_dram, qtaps_dram, ffn_in_dram, ffn_out_dram, qk_dram, v_dram,
               proj_dram, bias_dram, group_dram, ident_dram):
    with ExitStack() as ctx:
        def sb(name, shape, dt=F32):
            return ctx.enter_context(nc.sbuf_tensor("conv_" + name, shape, dt))

        def sem(name):
            return ctx.enter_context(nc.semaphore("conv_" + name))

        ident, group = sb("ident", [P, P]), sb("group", [P, P])
        bnp = sb("bnp", [P, 4, len(BN)])
        scale, shift, root = (sb(s, [P, len(BN)]) for s in ("scale", "shift", "root"))
        minus_half = sb("minus_half", [P, len(BN)])
        taps, qtaps = sb("taps", [P, 2, 9]), sb("qtaps", [P, 25])
        w_in, w_out = sb("w_in", [P, 2, 2 * C]), sb("w_out", [P, 2, 2, C])
        w_qk, w_v, w_proj = sb("w_qk", [P, 4, C]), sb("w_v", [P, 2, 64]), sb("w_proj", [P, C])
        bias = sb("bias", [P, HEADS * WIN])
        x, xo = sb("x", [P, T]), sb("xo", [P, T])
        stats, squares, parts = sb("stats", [P, 2, 6]), sb("squares", [P, 4]), sb("parts", [P, 2])
        gm, gsq, gshift = (sb(s, [P, 2]) for s in ("gm", "gsq", "gshift"))
        gvar, grstd = sb("gvar", [P, 1]), sb("grstd", [P, 1])
        xp = sb("xp", [P, SIDE + 2, SIDE + 2])
        x1 = sb("x1", [P, T])
        hidden = sb("hidden", [P, 2, T])
        branch = sb("branch", [P, T])
        x2 = sb("x2", [P, NW * WS, NW * WS])
        xw = sb("xw", [P, WINDOWS, WIN])
        qp = sb("qp", [P, SLOTS * PITCH + 4, WS + 4])
        q = sb("q", [P, SLOTS * QROW + 2])
        keys = [sb(f"keys{g}", [P, SLOTS, HEADS, WIN]) for g in range(2)]
        values = sb("values", [P, WINDOWS, 2, 64])
        score = sb("score", [P, SLOTS, HEADS * WIN])
        most, total, recip = (sb(s, [P, SLOTS * HEADS]) for s in ("most", "total", "recip"))
        prob = sb("prob", [P, SLOTS, HEADS, 64])
        probT = sb("probT", [P, 2 * SLOTS, P])
        mixed = sb("mixed", [P, WINDOWS * WIN])
        projected = sb("projected", [P, WINDOWS, WIN])
        x3 = sb("x3", [P, SIDE + 2, SIDE + 2])
        x4 = sb("x4", [P, T])
        branch4 = sb("branch4", [P, T])
        y = sb("y", [P, T])

        zero = [xp[:], x2[:], x3[:], qp[:], q[:, SLOTS * QROW:], keys[0][:], keys[1][:], values[:], prob[:], gshift[:, 1:2]]
        ZEROED, LOADED = len(zero), 11 * 16

        NT = 4
        tile = [ctx.enter_context(nc.psum_tensor(f"conv_tile{r}", [P, 2 * HALF], F32)) for r in range(NT)]

        loaded, const_set, zeroed, root_ready, fold_step, folded = (
            sem(s) for s in ("loaded", "const_set", "zeroed", "root_ready", "fold_step", "folded"))
        tile_filled = [sem(f"tile{r}_filled") for r in range(NT)]
        tile_used = [sem(f"tile{r}_used") for r in range(NT)]
        x_loaded, moments_ready, gvar_ready, grstd_ready, xp_ready, x1_ready = (
            sem(s) for s in ("x_loaded", "moments_ready", "gvar_ready", "grstd_ready", "xp_ready", "x1_ready"))
        x2_ready, xw_ready, q_ready, shifted, exps_ready = (
            sem(s) for s in ("x2_ready", "xw_ready", "q_ready", "shifted", "exps_ready"))
        x3_ready, x4_ready, xo_loaded, y_step, y_ready, stored = (
            sem(s) for s in ("x3_ready", "x4_ready", "xo_loaded", "y_step", "y_ready", "stored"))
        moment_chain = Chain(sem("moment_step"), 3)
        group_chain = Chain(sem("group_step"), 3)
        conv0_chain = Chain(sem("conv0_step"), 8)
        conv1_chain = Chain(sem("conv1_step"), 8)
        qconv_chain = Chain(sem("qconv_step"), 24)
        softmax_chain = Chain(sem("softmax_step"), 4)
        block = ctx.enter_context(nc.Block())

        first_items = ["G", "F0a", "F0b", "F0c"]
        main_items = (["Q", "K0", "K1", "V0", "V1"] + ["F1a", "F1b", "F1c"] + [f"S{j}" for j in range(4)] + ["G"]
                      + [f"T{j}" for j in range(4)] + ["A0", "A1", "P0", "P1", "F0a", "F0b", "F0c"])
        FIRST, F1 = len(first_items), ("F1a", "F1b", "F1c")
        NEXT = ("G", "F0a", "F0b", "F0c")
        assert len(main_items) % NT == 0 and FIRST % NT == 0

        def is_first(n):
            return isinstance(n, int) and n == 0

        def is_last(n):
            return isinstance(n, int) and n == NB - 1

        def items_of(n):
            return [m for m in main_items if not (is_first(n) and m in F1) and not (is_last(n) and m in NEXT)]

        def place(n, item):
            if n is None:
                at, whole = first_items.index(item), 0
            else:
                skipped = 0 if is_first(n) else len(F1)
                at, whole = FIRST - skipped + items_of(n).index(item), len(main_items) // NT * n
            return at % NT, whole + at // NT

        LAST_F1 = FIRST - len(F1) + len(main_items) * (NB - 1) + len(items_of(NB - 1))

        def last_place(item):
            at = LAST_F1 + F1.index(item)
            return at % NT, at // NT

        def image_loop(eng, prologue, turn, epilogue):
            prologue()
            turn(0)
            if NB > 2:
                with eng.Fori(1, NB - 1) as n:
                    turn(n)
            turn(NB - 1)
            epilogue()

        def bank_cols(j):
            return j // 10 * HALF + j % 10 * WIN

        def col(t, name):
            k = BN.index(name)
            return t[:, k:k + 1]

        def image(t):
            return t[:].rearrange("p (r c) -> p r c", c=SIDE)

        @block.sync
        def _(sp):
            for to, of in ((ident[:], ident_dram), (group[:], group_dram), (bnp[:], bn_dram), (taps[:], taps_dram),
                           (qtaps[:], qtaps_dram), (w_in[:], ffn_in_dram), (w_out[:], ffn_out_dram), (w_qk[:], qk_dram),
                           (w_v[:], v_dram), (w_proj[:], proj_dram), (bias[:], bias_dram)):
                sp.dma_start(to, of).then_inc(loaded, 16)
            sp.dma_start(x[:], x_dram[0]).then_inc(x_loaded, 16)

            def store(n):
                sp.wait_ge(y_ready, n + 1)
                sp.dma_start(y_dram[n], y[:]).then_inc(stored, 16)

            def turn(n):
                if not is_last(n):
                    sp.wait_ge(xp_ready, n + 1)
                    sp.dma_start(x[:], x_dram[n + 1]).then_inc(x_loaded, 16)
                if not is_first(n):
                    store(n - 1)
                sp.dma_start(xo[:], x_dram[n]).then_inc(xo_loaded, 16)

            image_loop(sp, lambda: None, turn, lambda: store(NB - 1))
            sp.wait_ge(stored, 16 * NB)

        def used(eng, where):
            eng.wait_ge(tile_used[where[0]], where[1] + 1)

        def filled(eng, where):
            eng.wait_ge(tile_filled[where[0]], where[1] + 1)

        def prepared(n, item):
            return place(None, item) if is_first(n) else place(n - 1, item)

        def last_ffn(n, item):
            return last_place(item) if is_last(n) else place(n + 1, item)

        @block.gpsimd
        def _(pool):
            pool.memset(minus_half[:], -0.5).then_inc(const_set, 1)
            pool.wait_ge(const_set, 1)
            pool.wait_ge(fold_step, 1)
            pool.tensor_tensor(root[:], root[:], minus_half[:], ALU.pow).then_inc(root_ready, 1)

            def group_root(n):
                pool.wait_ge(gvar_ready, n + 1)
                pool.tensor_tensor(grstd[:], gvar[:], minus_half[:, 0:1], ALU.pow).then_inc(grstd_ready, 1)

            def add_branch(n):
                used(pool, prepared(n, "F0c"))
                if not is_first(n):
                    pool.wait_ge(x3_ready, n)
                pool.tensor_tensor(x2[:, 0:SIDE, 0:SIDE], image(branch), image(x1), ALU.add).then_inc(x2_ready, 1)

            def add_last(n):
                used(pool, last_ffn(n, "F1c"))
                if not is_first(n):
                    pool.wait_ge(stored, 16 * n)
                pool.tensor_tensor(y[:], branch4[:], x4[:], ALU.add).then_inc(y_step, 1)
                pool.wait_ge(y_step, n + 1)
                pool.wait_ge(xo_loaded, 16 * n + 16)
                pool.tensor_tensor(y[:], y[:], xo[:], ALU.add).then_inc(y_ready, 1)

            def prologue():
                group_root(0)
                pool.wait_ge(zeroed, ZEROED)
                add_branch(0)

            def turn(n):
                if not is_first(n):
                    add_last(n - 1)
                if not is_last(n):
                    group_root(n + 1)
                    add_branch(n + 1)

            image_loop(pool, prologue, turn, lambda: add_last(NB - 1))

        @block.scalar
        def _(act):
            act.wait_ge(loaded, LOADED)
            act.wait_ge(folded, 1)
            act.wait_ge(zeroed, ZEROED)

            def batch_norm(where, out, source, name, func=ACT.Identity, rows=slice(0, P), last=True):
                ins = act.activation(out, source, func, bias=col(shift, name)[rows, :], scale=col(scale, name)[rows, :])
                if last:
                    ins.then_inc(tile_used[where[0]], 1)

            def ffn(where, number, out):
                for j, item in enumerate("abc"):
                    at = where(f"F{number}{item}")
                    filled(act, at)
                    if j < 2:
                        batch_norm(at, hidden[:, j, :], tile[at[0]][:], f"ffn{number}_in{j}", ACT.Relu)
                    else:
                        batch_norm(at, out[:], tile[at[0]][:], f"ffn{number}_out")

            def ffn0(n):
                if not is_first(n):
                    act.wait_ge(x2_ready, n)
                ffn(lambda item: prepared(n, item), 0, branch)

            def ffn1(n):
                if not is_first(n):
                    act.wait_ge(y_step, n)
                ffn(lambda item: last_ffn(n, item), 1, branch4)

            def turn(n):
                act.wait_ge(x2_ready, n + 1)
                for row in range(NW):
                    cut = x2[:, row * WS:(row + 1) * WS, :].rearrange("p r (w c) -> p w r c", w=NW)
                    ins = act.activation(xw[:, row * NW:(row + 1) * NW, :].rearrange("p w (r c) -> p w r c", r=WS), cut, ACT.Copy)
                ins.then_inc(xw_ready, 1)
                at = place(n, "Q")
                filled(act, at)
                if not is_first(n):
                    act.wait_ge(q_ready, n)
                inside = qp[:, 2:2 + SLOTS * PITCH, 2:2 + WS].rearrange("p (s r) c -> p s r c", r=PITCH)
                for s, k in ((0, 10), (10, SLOTS - 10)):
                    source = tile[at[0]][:, bank_cols(s):bank_cols(s) + k * WIN].rearrange("p (s r c) -> p s r c", s=k, r=WS)
                    batch_norm(at, inside[:, s:s + k, 0:WS, :], source, "q", last=(s > 0))
                for g in range(2):
                    at = place(n, f"K{g}")
                    filled(act, at)
                    for h in range(HEADS):
                        rows = slice(h * DH, (h + 1) * DH)
                        for s, k in ((0, 10), (10, SLOTS - 10)):
                            source = tile[at[0]][rows, bank_cols(s):bank_cols(s) + k * WIN].rearrange("p (s m) -> p s m", s=k)
                            batch_norm(at, keys[g][rows, s:s + k, h, :], source, ("k_first", "k_second")[g], rows=rows,
                                       last=(h == HEADS - 1 and s > 0))
                for v in range(2):
                    at = place(n, f"V{v}")
                    filled(act, at)
                    first, k = 16 * v, min(16, WINDOWS - 16 * v)
                    for low in range(2):
                        rows = slice(64 * low, 64 * low + WIN)
                        source = tile[at[0]][rows, 0:k * 64].rearrange("p (w a d) -> p w a d", w=k, a=2)
                        ins = act.activation(values[rows, first:first + k, :, low * DH:(low + 1) * DH], source, ACT.Copy)
                    ins.then_inc(tile_used[at[0]], 1)
                if not is_first(n):
                    ffn1(n - 1)
                act.wait_ge(shifted, n + 1)
                act.activation(prob[:, :, :, 0:WIN], score[:].rearrange("p s (h m) -> p s h m", h=HEADS), ACT.Exp).then_inc(exps_ready, 1)
                for j in range(4):
                    at = place(n, f"T{j}")
                    k = min(8, 2 * SLOTS - 8 * j)
                    filled(act, at)
                    act.activation(flat(probT[:, 8 * j:8 * j + k, :]), tile[at[0]][:, 0:k * P], ACT.Copy).then_inc(tile_used[at[0]], 1)
                for name, out, bn, func in (("A", mixed, "value", ACT.Relu), ("P", projected, "proj", ACT.Identity)):
                    for j, (first, k) in enumerate(((0, 20), (20, WINDOWS - 20))):
                        at = place(n, f"{name}{j}")
                        filled(act, at)
                        banks = [(w, min(10, k - w)) for w in range(0, k, 10)]
                        for w, kk in banks:
                            to = out[:, first + w:first + w + kk, :] if name == "P" else out[:, (first + w) * WIN:(first + w + kk) * WIN]
                            source = tile[at[0]][:, bank_cols(w):bank_cols(w) + kk * WIN]
                            if name == "P":
                                to = flat(to)
                            batch_norm(at, to, source, bn, func, last=(w == banks[-1][0]))
                if not is_last(n):
                    ffn0(n + 1)

            image_loop(act, lambda: ffn0(0), turn, lambda: ffn1(NB - 1))

        @block.vector
        def _(dve):
            for t in zero:
                dve.memset(t, 0.0).then_inc(zeroed, 1)
            dve.wait_ge(loaded, LOADED)
            dve.tensor_scalar(root[:], bnp[:, 3, :], EPS, None, ALU.add).then_inc(fold_step, 1)
            dve.wait_ge(root_ready, 1)
            dve.tensor_tensor(scale[:], bnp[:, 0, :], root[:], ALU.mult).then_inc(fold_step, 1)
            dve.wait_ge(fold_step, 2)
            dve.tensor_tensor(shift[:], bnp[:, 2, :], scale[:], ALU.mult).then_inc(fold_step, 1)
            dve.wait_ge(fold_step, 3)
            dve.tensor_tensor(shift[:], bnp[:, 1, :], shift[:], ALU.subtract).then_inc(fold_step, 1)
            for j, name in enumerate(("dw0", "dw1")):
                dve.tensor_scalar(taps[:, j, :], taps[:, j, :], col(scale, name), None, ALU.mult).then_inc(fold_step, 1)
            dve.wait_ge(fold_step, 6)
            dve.tensor_scalar(taps[:, :, 4:5], taps[:, :, 4:5], 1.0, None, ALU.add).then_inc(fold_step, 1)
            dve.tensor_scalar(qtaps[:], qtaps[:], col(scale, "qdw"), None, ALU.mult).then_inc(fold_step, 1)
            dve.wait_ge(fold_step, 8)
            dve.wait_ge(zeroed, ZEROED)
            dve.tensor_copy(gshift[:, 0:1], gshift[:, 1:2]).then_inc(folded, 1)

            def convolve(chain, n, out, source, weights, taps_a_side, rows, width, bn, ready):
                chain.begin(dve, n)
                steps = [(dy, dx) for dy in range(taps_a_side) for dx in range(taps_a_side)]
                for j, (dy, dx) in enumerate(steps):
                    shifted_in = source[:, dy:dy + rows, dx:dx + width]
                    tap = weights[:, j:j + 1]
                    if j == 0:
                        ins = dve.tensor_scalar(out, shifted_in, tap, col(shift, bn), ALU.mult, ALU.add)
                    else:
                        ins = dve.scalar_tensor_tensor(out, shifted_in, tap, out, ALU.mult, ALU.add)
                    if j == len(steps) - 1:
                        ins.then_inc(ready, 1)
                    else:
                        chain.step(ins)
                chain.end()

            def moments_of(n):
                moment_chain.begin(dve, n)
                dve.wait_ge(x_loaded, 16 * n + 16)
                for c in range(2):
                    ins = dve.bn_stats(stats[:, c, :], x[:, c * HALF:(c + 1) * HALF])
                moment_chain.step(ins)
                quarters = flat(stats[:]).rearrange("p (q k) -> p q k", k=3)
                means, deviations = quarters[:, :, 1], quarters[:, :, 2]
                moment_chain.step(dve.tensor_tensor(squares[:], means, means, ALU.mult))
                moment_chain.step(dve.scalar_tensor_tensor(squares[:], deviations, 4.0 / T, squares[:], ALU.mult, ALU.add))
                moment_chain.end()
                dve.tensor_reduce(parts[:, 0:1], means, AX.X, ALU.add)
                dve.tensor_reduce(parts[:, 1:2], squares[:], AX.X, ALU.add).then_inc(moments_ready, 1)

            def group_norm(n):
                group_chain.begin(dve, n)
                at = prepared(n, "G")
                filled(dve, at)
                dve.tensor_copy(gm[:], tile[at[0]][:, 0:2]).then_inc(tile_used[at[0]], 1)
                used(dve, at)
                group_chain.step(dve.tensor_tensor(gsq[:, 0:1], gm[:, 0:1], gm[:, 0:1], ALU.mult))
                group_chain.step(dve.tensor_tensor(gsq[:, 1:2], gm[:, 1:2], gsq[:, 0:1], ALU.subtract))
                dve.tensor_scalar(gvar[:], gsq[:, 1:2], EPS, None, ALU.add).then_inc(gvar_ready, 1)
                dve.wait_ge(grstd_ready, n + 1)
                group_chain.step(dve.scalar_tensor_tensor(gshift[:, 0:1], gm[:, 0:1], -1.0, grstd[:], ALU.mult, ALU.mult))
                group_chain.end()
                dve.tensor_scalar(xp[:, 1:SIDE + 1, 1:SIDE + 1], image(x), grstd[:], gshift[:, 0:1], ALU.mult, ALU.add).then_inc(xp_ready, 1)
                dve.wait_ge(xp_ready, n + 1)
                if not is_first(n):
                    dve.wait_ge(x2_ready, n)
                convolve(conv0_chain, n, image(x1), xp, taps[:, 0, :], 3, SIDE, SIDE, "dw0", x1_ready)

            def turn(n):
                used(dve, place(n, "Q"))
                convolve(qconv_chain, n, q[:, 0:SLOTS * QROW].rearrange("p (r c) -> p r c", c=WS), qp, qtaps[:], 5,
                         SLOTS * PITCH, WS, "qdw", q_ready)
                softmax_chain.begin(dve, n)
                for j in range(4):
                    at = place(n, f"S{j}")
                    filled(dve, at)
                    k = min(4, SLOTS - 4 * j)
                    for s in range(0, k, 2):
                        kk = min(2, k - s)
                        source = tile[at[0]][:, s // 2 * HALF:s // 2 * HALF + kk * HEADS * WIN].rearrange("p (s m) -> p s m", s=kk)
                        ins = dve.scalar_tensor_tensor(score[:, 4 * j + s:4 * j + s + kk, :], source, AT_WINDOW_SCALE,
                                                       bias[:].unsqueeze(1).to_broadcast([P, kk, HEADS * WIN]), ALU.mult, ALU.add)
                    ins.then_inc(tile_used[at[0]], 1)
                for j in range(4):
                    used(dve, place(n, f"S{j}"))
                by_head = score[:].rearrange("p s (h m) -> p (s h) m", h=HEADS)
                softmax_chain.step(dve.tensor_reduce(most[:], by_head, AX.X, ALU.max))
                dve.tensor_tensor(by_head, by_head, col_bcast(most[:], WIN), ALU.subtract).then_inc(shifted, 1)
                if not is_last(n):
                    moments_of(n + 1)
                dve.wait_ge(exps_ready, n + 1)
                weights = prob[:].rearrange("p s h m -> p (s h) m")[:, :, 0:WIN]
                softmax_chain.step(dve.tensor_reduce(total[:], weights, AX.X, ALU.add))
                softmax_chain.step(dve.reciprocal(recip[:], total[:]))
                softmax_chain.step(dve.tensor_tensor(weights, weights, col_bcast(recip[:], WIN), ALU.mult))
                softmax_chain.end()
                if not is_last(n):
                    group_norm(n + 1)
                for j in range(2):
                    used(dve, place(n, f"P{j}"))
                for row in range(NW):
                    k = min(WS, SIDE - row * WS)
                    for first, windows, width in ((0, NW - 1, WS), (NW - 1, 1, SIDE - (NW - 1) * WS)):
                        def cut(t, border):
                            part = t[:, border + row * WS:border + row * WS + k, border + first * WS:border + first * WS + windows * width]
                            return part.rearrange("p r (w c) -> p r w c", w=windows)
                        w = row * NW + first
                        add = projected[:, w:w + windows, :].rearrange("p w (r c) -> p r w c", r=WS)[:, 0:k, :, 0:width]
                        ins = dve.tensor_tensor(cut(x3, 1), cut(x2, 0), add, ALU.add)
                ins.then_inc(x3_ready, 1)
                dve.wait_ge(x3_ready, n + 1)
                if not is_first(n):
                    dve.wait_ge(y_step, n)
                convolve(conv1_chain, n, image(x4), x3, taps[:, 1, :], 3, SIDE, SIDE, "dw1", x4_ready)

            def prologue():
                moments_of(0)
                group_norm(0)

            image_loop(dve, prologue, turn, lambda: None)

        @block.tensor
        def _(pe):
            pe.wait_ge(loaded, LOADED)
            pe.wait_ge(zeroed, ZEROED)

            def begin(where):
                pe.wait_ge(tile_used[where[0]], where[1])
                return tile[where[0]]

            def ffn(where, number, source):
                for j in range(2):
                    at = where(f"F{number}{'ab'[j]}")
                    to = begin(at)
                    for c in (0, HALF):
                        last = pe.matmul(to[:, c:c + HALF], w_in[:, number, j * C:(j + 1) * C], source[:, c:c + HALF], start=True, stop=True)
                    last.then_inc(tile_filled[at[0]], 1)
                at = where(f"F{number}c")
                to = begin(at)
                for j in range(2):
                    used(pe, where(f"F{number}{'ab'[j]}"))
                for c in (0, HALF):
                    for j in range(2):
                        last = pe.matmul(to[:, c:c + HALF], w_out[:, number, j, :], hidden[:, j, c:c + HALF], start=(j == 0), stop=(j == 1))
                last.then_inc(tile_filled[at[0]], 1)

            def moments_mean(n):
                at = prepared(n, "G")
                to = begin(at)
                pe.wait_ge(moments_ready, n + 1)
                pe.matmul(to[:, 0:2], group[:], parts[:], start=True, stop=True).then_inc(tile_filled[at[0]], 1)

            def ffn0(n):
                pe.wait_ge(x1_ready, n + 1)
                ffn(lambda item: prepared(n, item), 0, x1)

            def ffn1(n):
                pe.wait_ge(x4_ready, n + 1)
                ffn(lambda item: last_ffn(n, item), 1, x4)

            def by_windows(to, products):
                begun = set()
                for w, first, count, slot in products:
                    while count:
                        k = min(count, 10 - slot % 10)
                        last = pe.matmul(to[:, bank_cols(slot):bank_cols(slot) + k * WIN], w, flat(xw[:, first:first + k, :]),
                                         start=slot // 10 not in begun, stop=True, skip_group_check=True)
                        begun.add(slot // 10)
                        first, slot, count = first + k, slot + k, count - k
                return last

            def prologue():
                moments_mean(0)
                ffn0(0)

            def turn(n):
                pe.wait_ge(xw_ready, n + 1)
                at = place(n, "Q")
                last = by_windows(begin(at), [(w_qk[:, 0, :], 0, SLOTS, 0), (w_qk[:, 1, :], SLOTS, WINDOWS - SLOTS, 0)])
                last.then_inc(tile_filled[at[0]], 1)
                for g in range(2):
                    at = place(n, f"K{g}")
                    first = SLOTS * g
                    last = by_windows(begin(at), [(w_qk[:, 2 + g, :], first, min(SLOTS, WINDOWS - first), 0)])
                    last.then_inc(tile_filled[at[0]], 1)
                for v in range(2):
                    at = place(n, f"V{v}")
                    to = begin(at)
                    for j in range(min(16, WINDOWS - 16 * v)):
                        for low in range(2):
                            last = pe.matmul(to[64 * low:64 * low + WIN, 64 * j:64 * j + 64], xw[:, 16 * v + j, :], w_v[:, low, :], start=True, stop=True)
                    last.then_inc(tile_filled[at[0]], 1)
                if not is_first(n):
                    ffn1(n - 1)
                pe.wait_ge(q_ready, n + 1)
                for g in range(2):
                    used(pe, place(n, f"K{g}"))
                for j in range(4):
                    at = place(n, f"S{j}")
                    to = begin(at)
                    for s in range(min(4, SLOTS - 4 * j)):
                        slot = 4 * j + s
                        c = s // 2 * HALF + s % 2 * HEADS * WIN
                        for g in range(2):
                            last = pe.matmul(to[64 * g:64 * g + 64, c:c + HEADS * WIN], q[:, slot * QROW:slot * QROW + 64],
                                             keys[g][:, slot, :, :].rearrange("p h m -> p (h m)"), start=True, stop=True)
                    last.then_inc(tile_filled[at[0]], 1)
                if not is_last(n):
                    moments_mean(n + 1)
                pe.wait_ge(softmax_chain.sem, 4 * n + 4)
                for j in range(4):
                    at = place(n, f"T{j}")
                    to = begin(at)
                    for t in range(min(8, 2 * SLOTS - 8 * j)):
                        slot, pair = divmod(8 * j + t, 2)
                        last = pe.transpose(to[:, t * P:(t + 1) * P], prob[:, slot, 2 * pair:2 * pair + 2, :].rearrange("p h m -> p (h m)"), ident[:])
                    last.then_inc(tile_filled[at[0]], 1)
                for v in range(2):
                    used(pe, place(n, f"V{v}"))
                for j in range(4):
                    used(pe, place(n, f"T{j}"))
                for j, (first, k) in enumerate(((0, 20), (20, WINDOWS - 20))):
                    at = place(n, f"A{j}")
                    to = begin(at)
                    for w in range(k):
                        group_of, slot = divmod(first + w, SLOTS)
                        for pair in range(2):
                            last = pe.matmul(to[64 * pair:64 * pair + 64, bank_cols(w):bank_cols(w) + WIN], values[:, first + w, pair, :],
                                             probT[:, 2 * slot + pair, 64 * group_of:64 * group_of + WIN], start=True, stop=True)
                    last.then_inc(tile_filled[at[0]], 1)
                for j, (first, k) in enumerate(((0, 20), (20, WINDOWS - 20))):
                    at = place(n, f"P{j}")
                    to = begin(at)
                    used(pe, place(n, f"A{j}"))
                    for w in range(0, k, 10):
                        kk = min(10, k - w)
                        last = pe.matmul(to[:, bank_cols(w):bank_cols(w) + kk * WIN], w_proj[:],
                                         mixed[:, (first + w) * WIN:(first + w + kk) * WIN], start=True, stop=True)
                    last.then_inc(tile_filled[at[0]], 1)
                if not is_last(n):
                    ffn0(n + 1)

            image_loop(pe, prologue, turn, lambda: ffn1(NB - 1))

def tables():
    rate = np.repeat(np.exp(np.arange(0, C, 2) * (-np.log(10000.0) / C)), 2)[:, None]
    place = np.arange(T)[None, :]
    odd = (np.arange(C) % 2)[:, None]
    angle = (T - 1 - place) * rate
    rot = np.stack([np.cos(angle), np.sin(angle) * (2 * odd - 1)])
    keys = np.stack([np.where(odd, np.cos(m * rate), np.sin(m * rate)) for m in (place, place - T)])
    one, other = np.arange(P)[:, None], np.arange(BAND)[None, :]
    by_key = other - 2 - one
    by_query = one - other
    masks = [np.where(keep, 0.0, NEG) for d in (by_key, by_query) for keep in (d >= 0, d <= -2, d == -1)]
    masks = np.stack(masks, 1).reshape(P, 6 * BAND)
    lower = np.broadcast_to(np.tril(np.ones((E, E)), -1).reshape(-1), (P, E * E))
    return {name: np.ascontiguousarray(a.astype(np.float32)) for name, a in
            (("heads", np.arange(C)[:, None] // DH == np.arange(HEADS)[None, :]), ("rot", rot), ("keys", keys), ("masks", masks), ("lower", lower), ("ident", np.eye(P)))}


def pos_layout(w):
    swapped = w.reshape(C // 2, 2, C)[:, ::-1].reshape(C, C)
    by_row = np.stack([w.T, swapped.T], 1)
    stack = by_row.reshape(HEADS, DH, 2, C).transpose(1, 0, 2, 3).reshape(DH, HEADS * 2 * C)
    return np.ascontiguousarray(np.concatenate([stack] * 3)), np.ascontiguousarray(by_row)


def window_bias(attn_bias):
    places = [(r, c) for r in range(WS) for c in range(WS)]
    offsets = {}
    index = np.array([[offsets.setdefault((abs(a - c), abs(b - d)), len(offsets)) for c, d in places] for a, b in places])
    out = np.zeros((2, 64, HEADS, WIN), np.float32)
    out[:, :WIN] = attn_bias[:, index].transpose(1, 0, 2)
    return out.reshape(P, HEADS * WIN)


def conv_layout(v):
    def get(name):
        return np.asarray(v["L0_conv_" + name])

    kd, dv = 16, 32
    head_channel = np.arange(C)
    from_x = head_channel % HEADS * DH + head_channel // HEADS
    rows = np.array([[h * DH + c for c in range(kd)] for h in range(HEADS)])
    qkv = get("qkv_w")
    qk = np.zeros((C, 4, C), np.float32)
    for kind in range(2):
        for g in range(2):
            for h in range(HEADS):
                block = qkv[h, kind * kd:(kind + 1) * kd, :]
                qk[from_x[h * DH:(h + 1) * DH][:, None], 2 * kind + g, (rows[h] + g * kd)[None, :]] = block.T
    value = np.zeros((C, 2, 2, dv), np.float32)
    for h in range(HEADS):
        value[from_x[h * DH:(h + 1) * DH], h % 2, h // 2] = qkv[h, 2 * kd:].T
    bn = np.zeros((C, 4, len(BN)), np.float32)
    bn[:, 3, :] = 1.0

    def put(name, params, at=slice(0, C)):
        bn[at, :, BN.index(name)] = params.T

    for name, key in (("dw0", "dw0_bn"), ("ffn0_out", "ffn0_bn2"), ("proj", "proj_bn"), ("dw1", "dw1_bn"), ("ffn1_out", "ffn1_bn2")):
        put(name, get(key))
    for number in range(2):
        for j in range(2):
            put(f"ffn{number}_in{j}", get(f"ffn{number}_bn1")[:, j * C:(j + 1) * C])
    qkv_bn, qdw = get("qkv_bn"), get("qdw_w").reshape(HEADS, kd, 25)
    qtaps = np.zeros((C, 25), np.float32)
    for h in range(HEADS):
        put("value", qkv_bn[h, :, 2 * kd:], slice(h * dv, (h + 1) * dv))
        for g in range(2):
            at = rows[h] + g * kd
            put("q", qkv_bn[h, :, :kd], at)
            put(("k_first", "k_second")[g], qkv_bn[h, :, kd:2 * kd], at)
            put("qdw", get("qdw_bn").reshape(4, HEADS, kd)[:, h], at)
            qtaps[at] = qdw[h]
    taps = np.stack([get("dw0_w").reshape(C, 9), get("dw1_w").reshape(C, 9)], 1)
    ffn_in = np.stack([get("ffn0_w1").T, get("ffn1_w1").T], 1)
    ffn_out = np.stack([get(f"ffn{n}_w2").T.reshape(2, C, C).transpose(1, 0, 2) for n in range(2)], 1)
    group = np.kron(np.eye(C // 4), np.full((4, 4), 0.25 / 4))
    return dict(bn=bn, taps=taps, qtaps=qtaps, ffn_in=ffn_in, ffn_out=ffn_out, qk=qk, value=value.reshape(C, 2, 64),
                proj=get("proj_w").T, window_bias=window_bias(get("attn_bias")), group=group)


def program(nc, NB, a, out):
    after_conv = nc.dram_tensor("after_conv", [NB, C, T], F32, kind="Internal").ap()
    after_attention = nc.dram_tensor("after_attention", [NB, C, T], F32, kind="Internal").ap()
    conv_phase(nc, NB, a["x"], after_conv, a["bn"], a["taps"], a["qtaps"], a["ffn_in"], a["ffn_out"], a["qk"], a["value"],
               a["proj"], a["window_bias"], a["group"], a["ident"])
    attention_phase(nc, NB, after_conv, after_attention, a["gamma"], a["beta"], a["w_qkv"], a["bq"], a["bk"], a["bv"],
                    a["u_bias"], a["v_bias"], a["pos_stack"], a["pos_rows"], a["w_out"], a["b_out"], a["ident"], a["rot"],
                    a["keys"], a["masks"], a["heads"])
    moe_phase(nc, NB, after_attention, out, a["wg"], a["bg"], a["w1"], a["b1"], a["w2"], a["b2"], a["ident"], a["lower"])


def kernel(**inputs):
    import concourse.bacc as bacc
    from concourse.bass_utils import run_bass_kernel_spmd

    v = {name: np.asarray(a) for name, a in inputs.items()}
    NB = v["x"].shape[0]
    arrays = dict(x=v["x"].reshape(NB, C, T), **tables(), **conv_layout(v))
    for name, key in (("gamma", "ln_gamma"), ("beta", "ln_beta"), ("bq", "bq"), ("bk", "bk"), ("bv", "bv"), ("b_out", "bout"),
                      ("u_bias", "u_bias"), ("v_bias", "v_bias")):
        arrays[name] = v["L1_attn_" + key].reshape(C, 1)
    arrays["w_qkv"] = np.stack([v["L1_attn_W" + s] for s in "qkv"], 1)
    arrays["pos_stack"], arrays["pos_rows"] = pos_layout(v["L1_attn_Wpos"])
    arrays["w_out"] = v["L1_attn_Wout"]
    for name, key in (("wg", "Wg"), ("bg", "bg"), ("w1", "W1"), ("w2", "W2"), ("b2", "b2")):
        arrays[name] = v["L1_ffn_" + key]
    arrays["b1"] = v["L1_ffn_b1"].reshape(E, MC, P).transpose(2, 0, 1)

    nc = bacc.Bacc("TRN2", target_bir_lowering=False, num_devices=1)
    sent, aps = {}, {}
    for name, a in arrays.items():
        sent[f"in_{name}"] = np.ascontiguousarray(a, np.float32)
        aps[name] = nc.dram_tensor(f"in_{name}", a.shape, F32, kind="ExternalInput").ap()
    out = nc.dram_tensor("out_0", (NB, C, T), F32, kind="ExternalOutput").ap()
    program(nc, NB, aps, out)
    result = run_bass_kernel_spmd(nc, [sent], core_ids=[0])
    return result.results[0]["out_0"].reshape(v["x"].shape)
```

```python
from contextlib import ExitStack

import numpy as np

import concourse.bass as bass
from concourse import mybir

F32 = mybir.dt.float32
F32R = mybir.dt.float32r
ALU = mybir.AluOpType
ACT = mybir.ActivationFunctionType
AX = mybir.AxisListType

C = 128
T = 1024
P = 128
TT = T // P
HALF = 512
E = 8
HID = 512
MC = HID // P


class Chain:

    def __init__(self, sem, per):
        self.sem, self.per = sem, per

    def begin(self, eng, n):
        self.eng, self.base, self.k = eng, n * self.per, 0

    def step(self, instruction):
        instruction.then_inc(self.sem, 1)
        self.k += 1
        self.eng.wait_ge(self.sem, self.base + self.k)

    def end(self):
        assert self.k == self.per, (self.k, self.per)


def flat(ap):
    return ap.rearrange("p a b -> p (a b)")


def raw(ap):
    return ap.bitcast(F32)


def col_bcast(stat, n):
    return stat.unsqueeze(2).to_broadcast([stat.shape[0], stat.shape[1], n])

def twice(ap):
    return ap.unsqueeze(1).broadcast_to((ap.shape[0], 2, ap.shape[1]))


def moe_phase(nc, NB, x_dram, out_dram, wg, bg, w1, b1, w2, b2, ident_dram, lower_dram):
    gate_rows = nc.dram_tensor("gate_rows", [NB, E, T], F32, kind="Internal").ap()
    LAG = MC
    NH, NF, NS = 3, MC, 2 * MC
    AFTER = 2 * MC
    GROUPS = 2 + 2 * E
    CHUNKS = 2 * E * MC

    with ExitStack() as ctx:
        def sb(name, shape, dt=F32):
            return ctx.enter_context(nc.sbuf_tensor("moe_" + name, shape, dt))

        def sem(name):
            return ctx.enter_context(nc.semaphore("moe_" + name))

        def psum(name, shape):
            return ctx.enter_context(nc.psum_tensor("moe_" + name, shape, F32))

        ident = sb("ident", [P, P])
        lower = sb("lower", [P, E * E])
        w1f = sb("w1f", [P, HID])
        w1h = sb("w1h", [P, E, HID], F32R)
        w1l = sb("w1l", [P, E, HID], F32R)
        w2h = sb("w2h", [P, E, MC, C], F32R)
        w2l = sb("w2l", [P, E, MC, C], F32R)
        wgf = sb("wgf", [P, E])
        wgh = sb("wgh", [P, E], F32R)
        wgl = sb("wgl", [P, E], F32R)
        bgb = sb("bgb", [P, E])
        b1s = sb("b1s", [P, E, MC])
        b2s = sb("b2s", [E, C])
        minus_half = sb("minus_half", [P, TT])
        x = [sb(f"x{k}", [P, T]) for k in range(2)]
        xc = sb("xc", [P, TT, C])
        sq = sb("sq", [P, TT, C])
        total, mean, var, rstd = (sb(s, [P, TT]) for s in ("total", "mean", "var", "rstd"))
        xnh = [sb(f"xnh{k}", [P, T], F32R) for k in range(2)]
        xnl = [sb(f"xnl{k}", [P, T], F32R) for k in range(2)]
        logit = sb("logit", [P, TT, E])
        diff = sb("diff", [P, TT, E])
        above = sb("above", [P, TT, E, E])
        equal = sb("equal", [P, TT, E, E])
        rank = sb("rank", [P, TT * E])
        best = sb("best", [P, TT])
        gate = sb("gate", [P, TT, E])
        gateT = [sb(f"gateT{k}", [E, T]) for k in range(2)]
        gate_all = sb("gate_all", [P, E, T])
        w2s = gate_all[:, 0:MC, :].rearrange("p m (e c) -> p e m c", e=E)
        hid = sb("hid", [P, NF, HALF])
        hidh = sb("hidh", [P, NS, HALF], F32R)
        hidl = sb("hidl", [P, NS, HALF], F32R)
        scaled = sb("scaled", [P, HALF])
        acc = [sb(f"acc{k}", [P, T]) for k in range(2)]

        turn_ps = psum("turn_ps", [P, 2, HALF])
        logit_ps = psum("logit_ps", [P, HALF])
        hid_ps = psum("hid_ps", [P, NH, HALF])
        out_ps = psum("out_ps", [P, 2, HALF])
        turn = flat(turn_ps[:])
        turn_tiles = turn.rearrange("p (t c) -> p t c", t=TT)
        logit_tiles = logit_ps[:, 0:TT * E].rearrange("p (t e) -> p t e", t=TT)

        w1_loaded, weights_loaded, w1_used = sem("w1_loaded"), sem("weights_loaded"), sem("w1_used")
        weights_split, consts_set = sem("weights_split"), sem("consts_set")
        x_turned, centred, squared = sem("x_turned"), sem("centred"), sem("squared")
        var_ready, rstd_ready, normed, norm_turned = sem("var_ready"), sem("rstd_ready"), sem("normed"), sem("norm_turned")
        high_ready, low_ready, logits_ready = sem("high_ready"), sem("low_ready"), sem("logits_ready")
        diff_ready, exp_ready, gates_ready = sem("diff_ready"), sem("exp_ready"), sem("gates_ready")
        gates_turned, gateT_ready, rows_stored = sem("gates_turned"), sem("gateT_ready"), sem("rows_stored")
        gate_spread = [sem(f"gate{e}_spread") for e in range(E)]
        hid_done, gelu_done, hid_high = sem("hid_done"), sem("gelu_done"), sem("hid_high")
        rest_by_pool, rest_by_vector = sem("rest_by_pool"), sem("rest_by_vector")
        out_done, out_used = sem("out_done"), sem("out_used")
        stored = sem("stored")
        x_loaded = [sem(f"x{k}_loaded") for k in range(2)]
        norm_chain = Chain(sem("norm_step"), 3)
        gate_chain = Chain(sem("gate_step"), 9)
        summed = sem("summed")
        block = ctx.enter_context(nc.Block())

        def wait_rest(eng, n, g):
            q, m = divmod(g, MC)
            if m == MC - 1:
                eng.wait_ge(rest_by_vector, 2 * E * n + q + 1)
            else:
                eng.wait_ge(rest_by_pool, 2 * E * (MC - 1) * n + (MC - 1) * q + m + 1)

        def image_loop(eng, pieces, run):
            for at in sorted(pieces):
                pieces[at](0, 0, True)

            def ahead(n, k):
                return lambda at: pieces[at](n, k, False) if at in pieces else None

            run(0, 0, ahead(1, 1))
            if NB > 4:
                with eng.Fori(1, NB - 4, 2) as n:
                    run(n, 1, ahead(n + 1, 0))
                    run(n + 1, 0, ahead(n + 2, 1))
            if NB > 2:
                run(NB - 3, 1, ahead(NB - 2, 0))
                run(NB - 2, 0, ahead(NB - 1, 1))
            run(NB - 1, 1, lambda at: None)

        @block.sync
        def _(sp):
            sp.dma_start(ident[:], ident_dram).then_inc(weights_loaded, 16)
            sp.dma_start(lower[:], lower_dram).then_inc(weights_loaded, 16)
            sp.dma_start(wgf[:], wg).then_inc(weights_loaded, 16)
            sp.dma_start(bgb[:], bg.partition_broadcast(P)).then_inc(weights_loaded, 16)
            sp.dma_start(b2s[:], b2).then_inc(weights_loaded, 16)
            sp.dma_start(b1s[:], b1).then_inc(weights_loaded, 16)
            for m in range(MC):
                sp.dma_start(w2s[:, :, m, :], w2[:, m * P:(m + 1) * P, :].rearrange("e p c -> p e c")).then_inc(weights_loaded, 16)
            for e in range(E):
                if e:
                    sp.wait_ge(w1_used, e)
                sp.dma_start(w1f[:], w1[e]).then_inc(w1_loaded, 16)

            def load(n, k):
                sp.dma_start(x[k][:], x_dram[n]).then_inc(x_loaded[k], 16)

            def store_rows(n, k, first):
                sp.wait_ge(gateT_ready, n + 1)
                sp.dma_start(gate_rows[n], gateT[k][:]).then_inc(rows_stored, 16)
                if first:
                    sp.wait_ge(rows_stored, 16)
                    for e in range(E):
                        sp.dma_start(gate_all[:, e, :], gate_rows[n, e].partition_broadcast(P)).then_inc(gate_spread[e], 16)

            def run(n, k, ahead):
                more = not (isinstance(n, int) and n == NB - 1)
                if not (isinstance(n, int) and n == 0):
                    sp.wait_ge(stored, 16 * n)
                if not (isinstance(n, int) and n >= NB - 2):
                    sp.wait_ge(out_used, GROUPS * n + 2)
                    load(n + 2, k)
                ahead(0)
                for e in range(E if more else 0):
                    sp.wait_ge(out_used, GROUPS * n + 2 + 2 * e + 2)
                    if e == 0:
                        sp.wait_ge(rows_stored, 16 * (n + 1) + 16)
                    sp.dma_start(gate_all[:, e, :], gate_rows[n + 1, e].partition_broadcast(P)).then_inc(gate_spread[e], 16)
                sp.wait_ge(summed, 2 * E * (n + 1))
                sp.dma_start(out_dram[n], acc[k][:]).then_inc(stored, 16)

            load(0, 0)
            load(1, 1)
            image_loop(sp, {0: store_rows}, run)
            sp.wait_ge(stored, 16 * NB)

        @block.gpsimd
        def _(pool):
            pool.memset(minus_half[:], -0.5).then_inc(consts_set, 1)
            pool.wait_ge(consts_set, 1)

            def powers(n, k, first):
                pool.wait_ge(var_ready, n + 1)
                pool.tensor_tensor(rstd[:], var[:], minus_half[:], ALU.pow).then_inc(rstd_ready, 1)

            def run(n, k, ahead):
                for g in range(CHUNKS):
                    if g % MC < MC - 1:
                        pool.wait_ge(hid_high, CHUNKS * n + g + 1)
                        if g < NS:
                            pool.wait_ge(out_done, GROUPS * n)
                        else:
                            pool.wait_ge(out_done, GROUPS * n + 2 + g // MC - 1)
                        pool.tensor_tensor(hidl[:, g % NS, :], hid[:, g % NF, :], raw(hidh[:, g % NS, :]), ALU.subtract).then_inc(rest_by_pool, 1)
                    ahead(g)

            image_loop(pool, {15: powers}, run)

        @block.scalar
        def _(act):
            def square(n, k, first):
                act.wait_ge(centred, n + 1)
                act.activation(flat(sq[:]), flat(xc[:]), ACT.Square).then_inc(squared, 1)

            def high(n, k, first):
                act.wait_ge(norm_turned, n + 1)
                act.activation(xnh[k][:], turn, ACT.Copy).then_inc(high_ready, 1)

            def gates(n, k, first):
                act.wait_ge(gates_turned, n + 1)
                act.activation(gateT[k][:], turn[0:E, :], ACT.Copy).then_inc(gateT_ready, 1)

            def run(n, k, ahead):
                for g in range(CHUNKS):
                    e, m = g // (2 * MC), g % MC
                    act.wait_ge(hid_done, CHUNKS * n + g + 1)
                    if g >= NF:
                        wait_rest(act, n, g - NF)
                    elif not (isinstance(n, int) and n == 0):
                        wait_rest(act, n - 1, CHUNKS + g - NF)
                    act.activation(hid[:, g % NF, :], hid_ps[:, g % NH, :], ACT.Gelu,
                                   bias=b1s[:, e, m:m + 1]).then_inc(gelu_done, 1)
                    ahead(g)

            def weigh(n, k, first):
                act.wait_ge(diff_ready, n + 1)
                act.activation(flat(gate[:]), flat(diff[:]), ACT.Exp).then_inc(exp_ready, 1)

            act.wait_ge(weights_loaded, (6 + MC) * 16)
            image_loop(act, {10: square, 28: high, 44: weigh, 58: gates}, run)

        @block.vector
        def _(dve):
            for e in range(E):
                dve.wait_ge(w1_loaded, 16 * (e + 1))
                dve.tensor_copy(w1h[:, e, :], w1f[:]).then_inc(weights_split, 1)
                dve.wait_ge(weights_split, e + 1)
                dve.tensor_tensor(w1l[:, e, :], w1f[:], raw(w1h[:, e, :]), ALU.subtract).then_inc(w1_used, 1)
            dve.wait_ge(weights_loaded, (6 + MC) * 16)
            dve.tensor_copy(wgh[:], wgf[:]).then_inc(weights_split, 1)
            dve.tensor_copy(w2h[:], w2s).then_inc(weights_split, 1)
            dve.wait_ge(weights_split, E + 2)
            dve.tensor_tensor(w2l[:], w2s, raw(w2h[:]), ALU.subtract)
            dve.tensor_tensor(wgl[:], wgf[:], raw(wgh[:]), ALU.subtract).then_inc(weights_split, 1)

            def centre(n, k, first):
                norm_chain.begin(dve, n)
                dve.wait_ge(x_turned, n + 1)
                norm_chain.step(dve.tensor_reduce(total[:], turn_tiles, AX.X, ALU.add))
                norm_chain.step(dve.tensor_scalar(mean[:], total[:], 1.0 / C, None, ALU.mult))
                dve.tensor_tensor(xc[:], turn_tiles, col_bcast(mean[:], C), ALU.subtract).then_inc(centred, 1)

            def variance(n, k, first):
                dve.wait_ge(squared, n + 1)
                norm_chain.step(dve.tensor_reduce(total[:], sq[:], AX.X, ALU.add))
                norm_chain.end()
                dve.tensor_scalar(var[:], total[:], 1.0 / C, 1e-5, ALU.mult, ALU.add).then_inc(var_ready, 1)

            def normalise(n, k, first):
                dve.wait_ge(rstd_ready, n + 1)
                dve.wait_ge(centred, n + 1)
                dve.tensor_tensor(xc[:], xc[:], col_bcast(rstd[:], C), ALU.mult).then_inc(normed, 1)

            def low(n, k, first):
                dve.wait_ge(norm_turned, n + 1)
                dve.wait_ge(high_ready, n + 1)
                dve.tensor_tensor(xnl[k][:], turn, raw(xnh[k][:]), ALU.subtract).then_inc(low_ready, 1)

            def gating(n, k, first):
                gate_chain.begin(dve, n)
                dve.wait_ge(logits_ready, n + 1)
                gate_chain.step(dve.tensor_tensor(logit[:], logit_tiles, bgb[:].unsqueeze(1).to_broadcast([P, TT, E]), ALU.add))
                other = logit[:].unsqueeze(2).to_broadcast([P, TT, E, E])
                own = logit[:].unsqueeze(3).to_broadcast([P, TT, E, E])
                dve.tensor_tensor(above[:], other, own, ALU.is_gt)
                gate_chain.step(dve.tensor_tensor(equal[:], other, own, ALU.is_equal))
                pairs = equal[:].rearrange("p t e f -> p t (e f)")
                gate_chain.step(dve.tensor_tensor(pairs, pairs, lower[:].unsqueeze(1).to_broadcast([P, TT, E * E]), ALU.mult))
                gate_chain.step(dve.tensor_tensor(above[:], above[:], equal[:], ALU.add))
                dve.tensor_reduce(rank[:], above[:].rearrange("p t e f -> p (t e) f"), AX.X, ALU.add)
                gate_chain.step(dve.tensor_reduce(best[:], logit[:], AX.X, ALU.max))
                dve.tensor_tensor(diff[:], logit[:], col_bcast(best[:], E), ALU.subtract).then_inc(diff_ready, 1)

            def gate_of_best(n, k, first):
                dve.wait_ge(exp_ready, n + 1)
                gate_chain.step(dve.scalar_tensor_tensor(flat(gate[:]), rank[:], 1.5, flat(gate[:]), ALU.is_lt, ALU.mult))
                gate_chain.step(dve.tensor_reduce(total[:], gate[:], AX.X, ALU.add))
                gate_chain.step(dve.reciprocal(mean[:], total[:]))
                gate_chain.step(dve.tensor_tensor(gate[:], gate[:], col_bcast(mean[:], E), ALU.mult))
                gate_chain.end()
                dve.tensor_copy(logit[:], gate[:]).then_inc(gates_ready, 1)

            def split_hidden(n, g):
                q, m = divmod(g, MC)
                dve.wait_ge(gelu_done, CHUNKS * n + g + 1)
                if m == 0:
                    dve.wait_ge(out_done, GROUPS * n + (2 + q - 1 if q >= 2 else 0))
                dve.tensor_copy(hidh[:, g % NS, :], hid[:, g % NF, :]).then_inc(hid_high, 1)
                if m == MC - 1:
                    dve.wait_ge(hid_high, CHUNKS * n + g + 1)
                    dve.tensor_tensor(hidl[:, g % NS, :], hid[:, g % NF, :], raw(hidh[:, g % NS, :]), ALU.subtract).then_inc(rest_by_vector, 1)

            def residual(n, k):
                dve.wait_ge(gate_spread[0], 16 * n + 16)
                for half in range(2):
                    part = slice(half * HALF, (half + 1) * HALF)
                    dve.wait_ge(out_done, GROUPS * n + half + 1)
                    dve.tensor_tensor(acc[k][:, part], out_ps[:, half, :], x[k][:, part], ALU.add).then_inc(out_used, 1)

            def add_group(n, k, q):
                e, half = divmod(q, 2)
                part = slice(half * HALF, (half + 1) * HALF)
                dve.wait_ge(out_done, GROUPS * n + 2 + q + 1)
                if half == 0:
                    dve.wait_ge(gate_spread[e], 16 * n + 16)
                if q:
                    dve.wait_ge(summed, 2 * E * n + q)
                else:
                    dve.wait_ge(out_used, GROUPS * n + 2)
                dve.tensor_tensor(scaled[:], out_ps[:, half, :], gate_all[:, e, part], ALU.mult).then_inc(out_used, 1)
                dve.wait_ge(out_used, GROUPS * n + 2 + q + 1)
                dve.tensor_tensor(acc[k][:, part], acc[k][:, part], scaled[:], ALU.add).then_inc(summed, 1)

            def run(n, k, ahead):
                for g in range(CHUNKS + AFTER):
                    if g < CHUNKS:
                        split_hidden(n, g)
                    if g == LAG - 1:
                        residual(n, k)
                    if g >= AFTER and g % MC == 0:
                        add_group(n, k, (g - AFTER) // MC)
                    ahead(g)

            image_loop(dve, {8: centre, 14: variance, 19: normalise, 30: low, 40: gating, 48: gate_of_best}, run)

        @block.tensor
        def _(pe):
            def turn_x(n, k, first):
                pe.wait_ge(x_loaded[k], 8 * (n - k) + 16)
                if not first:
                    pe.wait_ge(gateT_ready, n)
                for t in range(TT):
                    last = pe.transpose(turn[:, t * P:(t + 1) * P], x[k][:, t * P:(t + 1) * P], ident[:])
                last.then_inc(x_turned, 1)

            def turn_norm(n, k, first):
                pe.wait_ge(normed, n + 1)
                for t in range(TT):
                    last = pe.transpose(turn[:, t * P:(t + 1) * P], xc[:, t, :], ident[:])
                last.then_inc(norm_turned, 1)

            def logits(n, k, first):
                pe.wait_ge(high_ready, n + 1)
                pe.wait_ge(low_ready, n + 1)
                if not first:
                    pe.wait_ge(gates_ready, n)
                for t in range(TT):
                    cols = slice(t * P, (t + 1) * P)
                    for j, (a, w) in enumerate(((xnh[k], wgh), (xnh[k], wgl), (xnl[k], wgh))):
                        last = pe.matmul(logit_ps[:, t * E:(t + 1) * E], a[:, cols], w[:], start=(j == 0), stop=(j == 2))
                last.then_inc(logits_ready, 1)

            def turn_gates(n, k, first):
                pe.wait_ge(gates_ready, n + 1)
                for t in range(TT):
                    last = pe.transpose(turn[0:E, t * P:(t + 1) * P], logit[:, t, :], ident[:])
                last.then_inc(gates_turned, 1)

            def run(n, k, ahead):
                def biases():
                    pe.wait_ge(gateT_ready, n + 1)
                    for half in range(2):
                        part = slice(half * HALF, (half + 1) * HALF)
                        if not (isinstance(n, int) and n == 0):
                            pe.wait_ge(out_used, GROUPS * n + half - 1)
                        pe.matmul(out_ps[:, half, :], b2s[:], gateT[k][:, part], start=True, stop=True).then_inc(out_done, 1)

                def first_product(g):
                    e, half, m = g // (2 * MC), g // MC % 2, g % MC
                    part = slice(half * HALF, (half + 1) * HALF)
                    rows = slice(m * P, (m + 1) * P)
                    pe.wait_ge(gelu_done, CHUNKS * n + max(g - NH + 1, 0))
                    for j, (w, a) in enumerate(((w1h, xnh[k]), (w1l, xnh[k]), (w1h, xnl[k]))):
                        last = pe.matmul(hid_ps[:, g % NH, :], w[:, e, rows], a[:, part], start=(j == 0), stop=(j == 2))
                    last.then_inc(hid_done, 1)

                def second_product(g):
                    e, half, m = g // (2 * MC), g // MC % 2, g % MC
                    pe.wait_ge(hid_high, CHUNKS * n + g + 1)
                    if m == 0:
                        pe.wait_ge(out_used, GROUPS * n + 2 + g // MC - 1)
                    pe.matmul(out_ps[:, half, :], w2h[:, e, m, :], hidh[:, g % NS, :], start=(m == 0), stop=False)
                    pe.matmul(out_ps[:, half, :], w2l[:, e, m, :], hidh[:, g % NS, :], start=False, stop=False)
                    wait_rest(pe, n, g)
                    last = pe.matmul(out_ps[:, half, :], w2h[:, e, m, :], hidl[:, g % NS, :], start=False, stop=(m == MC - 1))
                    if m == MC - 1:
                        last.then_inc(out_done, 1)

                for g in range(CHUNKS + LAG):
                    if g < CHUNKS:
                        first_product(g)
                    if g == LAG - 1:
                        biases()
                    if g >= LAG:
                        second_product(g - LAG)
                    ahead(g)

            pe.wait_ge(weights_loaded, (6 + MC) * 16)
            pe.wait_ge(weights_split, E + 3)
            pe.wait_ge(w1_used, E)
            image_loop(pe, {6: turn_x, 26: turn_norm, 38: logits, 56: turn_gates}, run)


HEADS = 4
DH = C // HEADS
STEPS = TT
MIDDLE = 3
BAND = P + 2
NEG = -1e30


def band_of_keys(i):
    return (max(i * P - 2, 0), (i + 1) * P)


def band_of_queries(i):
    return (i * P, min((i + 1) * P + 2, T))


def attention_phase(nc, NB, x_dram, y_dram, gamma, beta, w_qkv, bq, bk, bv, u_bias, v_bias, pos_stack, pos_t,
                    w_out, b_out, ident_dram, rot_dram, keys_dram, masks_dram, heads_dram):
    SCALE = 1.0 / float(np.sqrt(C))

    with ExitStack() as ctx:
        def sb(name, shape, dt=F32):
            return ctx.enter_context(nc.sbuf_tensor("att_" + name, shape, dt))

        def sem(name):
            return ctx.enter_context(nc.semaphore("att_" + name))

        def psum(name, shape):
            return ctx.enter_context(nc.psum_tensor("att_" + name, shape, F32))

        ident = sb("ident", [P, P])
        identr = sb("identr", [P, P], F32R)
        masks = sb("masks", [P, 6, BAND], F32R)
        cos_t, sin_t = sb("cos_t", [P, T]), sb("sin_t", [P, T])
        keys_h = sb("keys_h", [P, 2, T], F32R)
        keys_l = sb("keys_l", [P, 2, T], F32R)
        wh, wl = sb("wh", [P, 3, C], F32R), sb("wl", [P, 3, C], F32R)
        posw = sb("posw", [3 * DH, HEADS, 2, C], F32R)
        wpos = sb("wpos", [P, 2, C])
        wout = sb("wout", [P, C])
        vec = sb("vec", [P, 8])
        bias_q, bias_out = sb("bias_q", [P, 1]), sb("bias_out", [P, 1])
        head_of, v_less_u = sb("head_of", [P, HEADS]), sb("v_less_u", [P, HEADS])
        mask_u = sb("mask_u", [P, HEADS])
        pos_bias = sb("pos_bias", [P, 2, HEADS])
        minus_half = sb("minus_half", [P, TT])
        x, y = sb("x", [P, T]), sb("y", [P, T])
        xc = sb("xc", [P, TT, C])
        sq = sb("sq", [P, TT, C])
        total, mean, var, rstd = (sb(s, [P, TT]) for s in ("total", "mean", "var", "rstd"))
        z = flat(sq[:])
        zh, zl = sb("zh", [P, T], F32R), sb("zl", [P, T], F32R)
        qk = sb("qk", [P, T])
        qh, ql, kh, kl = (sb(s, [P, T], F32R) for s in ("qh", "ql", "kh", "kl"))
        qs = sb("qs", [3 * DH + 1, HEADS, T], F32R)
        ks = sb("ks", [3 * DH + 1, HEADS, T], F32R)
        vals = sb("vals", [P, TT, HEADS, 3, DH], F32R)
        turned = sb("turned", [P, 2, HALF])
        rotated_f = sb("rotated_f", [P, HALF])
        rot_h = [sb(f"rot_h{j}", [P, T + 2], F32R) for j in range(2)]
        rot_l = [sb(f"rot_l{j}", [P, T + 2], F32R) for j in range(2)]
        neg_max = sb("neg_max", [P, TT])
        weights = [sb(f"weights{j}", [P, T + 2 * BAND]) for j in range(2)]
        weights_h = [sb(f"weights_h{j}", [P, T], F32R) for j in range(2)]
        weights_l = [sb(f"weights_l{j}", [P, T], F32R) for j in range(2)]
        sums, sums_rest = sb("sums", [2 * DH, T]), sb("sums_rest", [DH, T])
        by_block, recip = sb("by_block", [2 * DH, T // DH, DH]), sb("recip", [2 * DH, T // DH])
        recip_all = sb("recip_all", [DH, T])
        context = sb("context", [P, T])

        score_ps = psum("score_ps", [P, 3 * HALF])
        scratch = psum("scratch", [P, 3 * HALF])
        sum_ps = psum("sum_ps", [P, T])
        values_in_scratch = scratch[:, 0:T].rearrange("p (t h d) -> p t h d", t=TT, h=HEADS)
        scratch_tiles = scratch[:, 0:T].rearrange("p (t c) -> p t c", t=TT)

        consts_set, loaded, staged, split_step, setup_ps, setup_step = (
            sem(s) for s in ("consts_set", "loaded", "staged", "split_step", "setup_ps", "setup_step"))
        keys_staged = sem("keys_staged")
        x_loaded, squared, var_ready, rstd_ready, normed = (
            sem(s) for s in ("x_loaded", "squared", "var_ready", "rstd_ready", "normed"))
        z_high, q_high, k_high = sem("z_high"), sem("q_high"), sem("k_high")
        z_low, q_low, k_low = sem("z_low"), sem("q_low"), sem("k_low")
        stack_loaded = [sem(f"stack{h}_loaded") for h in range(HEADS)]
        scratch_filled, scratch_read = sem("scratch_filled"), sem("scratch_read")
        scores_done, exps_done, band_step, band_done, high_done, weights_ready = (
            sem(s) for s in ("scores_done", "exps_done", "band_step", "band_done", "high_done", "weights_ready"))
        sums_done, sums_read, context_ready, y_loaded, stored, values_high = (
            sem(s) for s in ("sums_done", "sums_read", "context_ready", "y_loaded", "stored", "values_high"))
        norm_chain = Chain(sem("norm_step"), 3)
        turned_back = sem("turned_back")
        rot_chain = Chain(sem("rot_step"), 3)
        context_chain = Chain(sem("context_step"), 4)
        block = ctx.enter_context(nc.Block())

        amid = {2: ["M0"], 6: ["M5"], 7: ["M7"]}
        before = {0: ["R0"], 1: ["R1"], 2: ["M1"], 3: ["M2"], 4: ["M3"], 5: ["M4"], 6: ["M6"], 7: ["X"]}
        amid_of_image = {(0, 4): "TX", (1, 1): "O", (1, 4): "TN", (2, 1): "Q", (2, 3): "K"}
        after_of_image = {(0, 1): "V"}
        first_items = ["TX", "TN", "Q", "K", "R0", "R1"] + [f"M{i}" for i in range(TT)] + ["X"]

        order = []
        for h in range(HEADS):
            for i in range(STEPS):
                order += [(name, h) for name in amid.get(i, [])]
                order += [(name, None) for name in (amid_of_image.get((h, i)),) if name]
                order += [(name, h) for name in before[i]]
                order += [(name, None) for name in (after_of_image.get((h, i)),) if name]
        OF_NEXT_IMAGE = ("TX", "TN", "Q", "K")
        FIRST = len(first_items)

        def is_first(n):
            return isinstance(n, int) and n == 0

        def is_last(n):
            return isinstance(n, int) and n == NB - 1

        def number_of(n, name, h=None):
            ahead = order[:order.index((name, h))]
            if is_first(n):
                return FIRST + sum(other != "O" for other, _ in ahead)
            if is_last(n):
                ahead = [other for other in ahead if other[0] not in OF_NEXT_IMAGE]
            return FIRST - 1 + len(order) * n + len(ahead)

        def prepared_number(n, name):
            return first_items.index(name) if is_first(n) else number_of(n - 1, name)

        left_out = len(OF_NEXT_IMAGE) + 2 + TT + 1
        LAST_O = FIRST - 1 + len(order) * NB - left_out

        def image_loop(eng, prologue, step):
            for number, item in enumerate(first_items):
                prologue(item, number)

            def image(n):
                number = number_of(n, *order[0])
                for h in range(HEADS):
                    for i in range(STEPS):
                        placed = []
                        for names in (amid.get(i, []) + [amid_of_image.get((h, i))], before[i], [after_of_image.get((h, i))]):
                            numbered = []
                            for name in names:
                                if name is None:
                                    continue
                                by_head = name not in ("V", "O") + OF_NEXT_IMAGE
                                if is_last(n) and (name in OF_NEXT_IMAGE or (by_head and h == HEADS - 1)):
                                    continue
                                if is_first(n) and name == "O":
                                    continue
                                image_of = n - 1 if name == "O" else n + 1 if name in OF_NEXT_IMAGE or (by_head and h == HEADS - 1) else n
                                numbered.append((name, number, image_of, (h + 1) % HEADS))
                                number = number + 1
                            placed.append(numbered)
                        step(n, h, i, *placed)

            image(0)
            if NB > 2:
                with eng.Fori(1, NB - 1) as n:
                    image(n)
            image(NB - 1)

        @block.sync
        def _(sp):
            sp.dma_start(ident[:], ident_dram).then_inc(loaded, 16)
            sp.dma_start(cos_t[:], rot_dram[0]).then_inc(loaded, 16)
            sp.dma_start(sin_t[:], rot_dram[1]).then_inc(loaded, 16)
            sp.dma_start(context[:, 0:6 * BAND], masks_dram).then_inc(loaded, 16)
            sp.dma_start(sq[:, 0:3, :], w_qkv).then_inc(loaded, 16)
            sp.dma_start(flat(xc[0:3 * DH, :, :]), pos_stack).then_inc(loaded, 16)
            sp.dma_start(wpos[:], pos_t).then_inc(loaded, 16)
            sp.dma_start(wout[:], w_out).then_inc(loaded, 16)
            sp.dma_start(head_of[:], heads_dram).then_inc(loaded, 16)
            for j, v in enumerate((gamma, beta, bq, bk, bv, u_bias, v_bias, b_out)):
                sp.dma_start(vec[:, j:j + 1], v).then_inc(loaded, 16)
            sp.dma_start(qk[:], keys_dram[0]).then_inc(keys_staged, 16)
            sp.dma_start(y[:], keys_dram[1]).then_inc(keys_staged, 16)

            def load_stack(h):
                rows = slice(h * DH, (h + 1) * DH)
                for j, (a, b) in enumerate(((qh, kh), (ql, kh), (qh, kl))):
                    to = slice(j * DH, (j + 1) * DH)
                    sp.dma_start(raw(qs[to, h, :]), raw(a[rows, :])).then_inc(stack_loaded[h], 16)
                    sp.dma_start(raw(ks[to, h, :]), raw(b[rows, :])).then_inc(stack_loaded[h], 16)

            sp.dma_start(x[:], x_dram[0]).then_inc(x_loaded, 16)
            sp.wait_ge(q_low, 1)
            sp.wait_ge(k_low, 1)
            for h in range(HEADS):
                load_stack(h)

            def image(n):
                if not is_last(n):
                    sp.wait_ge(scratch_filled, prepared_number(n, "TX") + 1)
                    sp.dma_start(x[:], x_dram[n + 1]).then_inc(x_loaded, 16)
                if not is_first(n):
                    sp.wait_ge(scores_done, HEADS * STEPS * n)
                    load_stack(HEADS - 1)
                    sp.wait_ge(scratch_read, number_of(n, "O") + 1)
                    sp.dma_start(y_dram[n - 1], y[:]).then_inc(stored, 16)
                    sp.wait_ge(stored, 16 * n)
                sp.dma_start(y[:], x_dram[n]).then_inc(y_loaded, 16)
                if not is_last(n):
                    sp.wait_ge(k_low, n + 2)
                    for h in range(HEADS - 1):
                        if h:
                            sp.wait_ge(scores_done, HEADS * STEPS * n + STEPS * (h + 1))
                        load_stack(h)

            image(0)
            if NB > 2:
                with sp.Fori(1, NB - 1) as n:
                    image(n)
            image(NB - 1)
            sp.wait_ge(scratch_read, LAST_O + 1)
            sp.dma_start(y_dram[NB - 1], y[:]).then_inc(stored, 16)
            sp.wait_ge(stored, 16 * NB)

        @block.gpsimd
        def _(pool):
            pool.memset(minus_half[:], -0.5).then_inc(consts_set, 1)
            pool.memset(raw(vals[:, :, :, 1, :]), 1.0).then_inc(consts_set, 1)
            pool.wait_ge(consts_set, 2)
            pool.memset(raw(ks[3 * DH:3 * DH + 1, :, :]), 1.0).then_inc(consts_set, 1)
            pool.wait_ge(consts_set, 3)
            for j in range(2):
                pool.memset(raw(rot_h[j][:, T:T + 2]), 0.0).then_inc(consts_set, 1)
                pool.memset(raw(rot_l[j][:, T:T + 2]), 0.0).then_inc(consts_set, 1)
            pool.wait_ge(consts_set, 7)

            def rstd_of(n):
                pool.wait_ge(var_ready, n + 1)
                pool.tensor_tensor(rstd[:], var[:], minus_half[:], ALU.pow).then_inc(rstd_ready, 1)

            def prologue(item, number):
                if item == "TX":
                    rstd_of(0)

            def rest_of(J, i):
                w = i % 2
                pool.wait_ge(high_done, J + 1)
                pool.tensor_tensor(weights_l[w][:], weights[w][:, 0:T], raw(weights_h[w][:]), ALU.subtract).then_inc(weights_ready, 1)

            def step(n, h, i, amid, before, after):
                J = HEADS * STEPS * n + STEPS * h + i
                w = weights[i % 2]
                a, b = band_of_keys(i)
                pool.wait_ge(exps_done, J + 1)
                pool.tensor_tensor(w[:, a:b], w[:, a:b], w[:, T:T + b - a], ALU.add).then_inc(band_step, 1)
                pool.wait_ge(band_step, J + 1)
                pool.tensor_tensor(w[:, a:b], w[:, a:b], w[:, T + b - a:T + 2 * (b - a)], ALU.add).then_inc(band_done, 1)
                if not (is_first(n) and h == 0 and i == 0):
                    rest_of(J - 1, i - 1)
                if (h, i) == (0, 5) and not is_last(n):
                    rstd_of(n + 1)

            image_loop(pool, prologue, step)
            rest_of(HEADS * STEPS * NB - 1, STEPS - 1)

        @block.scalar
        def _(act):
            act.wait_ge(loaded, 17 * 16)
            act.wait_ge(setup_step, 5)
            act.wait_ge(consts_set, 7)

            def consume(item, number, image, head):
                if item in ("V", "TN", "Q", "K"):
                    act.wait_ge(scratch_filled, number + 1)
                if item == "V":
                    act.activation(vals[:, :, :, 0, :], values_in_scratch, ACT.Copy).then_inc(values_high, 1)
                elif item == "TN":
                    act.activation(z, scratch[:, 0:T], ACT.Identity, bias=vec[:, 1:2], scale=vec[:, 0:1]).then_inc(scratch_read, 1)
                elif item == "Q":
                    act.activation(qk[:], scratch[:, 0:T], ACT.Identity, bias=bias_q[:]).then_inc(scratch_read, 1)
                elif item == "K":
                    act.wait_ge(q_low, image + 1)
                    act.activation(qk[:], scratch[:, 0:T], ACT.Identity, bias=vec[:, 3:4]).then_inc(scratch_read, 1)

            def square(n):
                act.wait_ge(scratch_read, prepared_number(n, "TX") + 1)
                act.activation(flat(sq[:]), flat(xc[:]), ACT.Square).then_inc(squared, 1)

            def prologue(item, number):
                consume(item, number, 0, 0)
                if item == "TX":
                    square(0)

            def high_of(J, i, early=False):
                w = i % 2
                act.wait_ge(band_done, J + 1)
                if not early:
                    act.wait_ge(sums_done, J - 1)
                act.activation(weights_h[w][:], weights[w][:, 0:T], ACT.Copy).then_inc(high_done, 1)

            def take_sums(hh):
                act.wait_ge(sums_done, STEPS * hh + STEPS)
                if not is_first(hh):
                    act.wait_ge(context_ready, hh)
                act.activation(sums[:], sum_ps[0:2 * DH, :], ACT.Copy)
                act.activation(sums_rest[:], sum_ps[2 * DH:3 * DH, :], ACT.Copy).then_inc(sums_read, 1)

            def step(n, h, i, amid, before, after):
                J = HEADS * STEPS * n + STEPS * h + i
                for item in amid:
                    consume(*item)
                act.wait_ge(scores_done, J + 1)
                if not is_first(n) or STEPS * h + i >= 2:
                    act.wait_ge(weights_ready, J - 1)
                a, b = band_of_keys(i)
                width = T + 2 * (b - a)
                act.activation(weights[i % 2][:, 0:width], score_ps[:, 0:width], ACT.Exp, scale=SCALE).then_inc(exps_done, 1)
                if not (is_first(n) and h == 0 and i == 0):
                    high_of(J - 1, i - 1, early=is_first(n) and h == 0 and i < 3)
                for item in before:
                    consume(*item)
                if i == 1 and not (is_first(n) and h == 0):
                    take_sums(HEADS * n + h - 1)
                for item in after:
                    consume(*item)
                if (h, i) == (0, 4) and not is_last(n):
                    square(n + 1)

            image_loop(act, prologue, step)
            high_of(HEADS * STEPS * NB - 1, STEPS - 1)
            take_sums(HEADS * NB - 1)

        @block.vector
        def _(dve):
            dve.wait_ge(loaded, 17 * 16)
            dve.tensor_copy(identr[:], ident[:])
            dve.tensor_copy(flat(masks[:]), context[:, 0:6 * BAND])
            dve.tensor_copy(wh[:], sq[:, 0:3, :]).then_inc(split_step, 1)
            dve.wait_ge(split_step, 1)
            dve.tensor_tensor(wl[:], sq[:, 0:3, :], raw(wh[:]), ALU.subtract).then_inc(split_step, 1)
            pos_flat = posw[:].rearrange("p h s c -> p (h s c)")
            part_flat = zh
            source = flat(xc[0:3 * DH, :, :])
            low_rows = slice(2 * DH, 3 * DH)
            dve.tensor_copy(pos_flat[0:2 * DH, :], source[0:2 * DH, :])
            dve.tensor_copy(part_flat[low_rows, :], source[low_rows, :]).then_inc(split_step, 1)
            dve.wait_ge(split_step, 3)
            dve.tensor_tensor(pos_flat[low_rows, :], source[low_rows, :], raw(part_flat[low_rows, :]), ALU.subtract).then_inc(split_step, 1)
            dve.wait_ge(keys_staged, 32)
            for j, source_of in enumerate((qk, y)):
                dve.tensor_copy(keys_h[:, j, :], source_of[:]).then_inc(split_step, 1)
                dve.wait_ge(split_step, 5 + j)
                dve.tensor_tensor(keys_l[:, j, :], source_of[:], raw(keys_h[:, j, :]), ALU.subtract).then_inc(setup_step, 1)
            dve.tensor_scalar(v_less_u[:], head_of[:], vec[:, 6:7], None, ALU.mult).then_inc(split_step, 1)
            dve.tensor_scalar(mask_u[:], head_of[:], vec[:, 5:6], None, ALU.mult).then_inc(split_step, 1)
            dve.wait_ge(split_step, 8)
            dve.tensor_tensor(v_less_u[:], v_less_u[:], mask_u[:], ALU.subtract).then_inc(setup_step, 1)
            dve.tensor_tensor(bias_q[:], vec[:, 2:3], vec[:, 5:6], ALU.add).then_inc(setup_step, 1)
            dve.wait_ge(setup_ps, 1)
            dve.tensor_copy(flat(pos_bias[:]), scratch[:, 0:2 * HEADS])
            dve.tensor_tensor(bias_out[:], scratch[:, 2 * HEADS:2 * HEADS + 1], vec[:, 7:8], ALU.add).then_inc(setup_step, 1)
            dve.wait_ge(setup_step, 5)

            def rotate(half, number, image, head):
                part = slice(half * HALF, (half + 1) * HALF)
                rot_chain.begin(dve, 2 * (HEADS * image + head) + half)
                dve.wait_ge(scratch_filled, number + 1)
                dve.scalar_tensor_tensor(turned[:, 0, :], scratch[:, 0:HALF], pos_bias[:, 0, head:head + 1], cos_t[:, part], ALU.add, ALU.mult)
                ins = dve.scalar_tensor_tensor(turned[:, 1, :], scratch[:, HALF:2 * HALF], pos_bias[:, 1, head:head + 1], sin_t[:, part], ALU.add, ALU.mult)
                ins.then_inc(scratch_read, 1)
                dve.wait_ge(scratch_read, number + 1)
                rot_chain.step(dve.tensor_tensor(rotated_f[:], turned[:, 0, :], turned[:, 1, :], ALU.add))
                rot_chain.step(dve.tensor_copy(rot_h[head % 2][:, part], rotated_f[:]))
                rot_chain.step(dve.tensor_tensor(rot_l[head % 2][:, part], rotated_f[:], raw(rot_h[head % 2][:, part]), ALU.subtract))
                rot_chain.end()

            def consume(item, number, image, head):
                if item[0] == "R":
                    rotate(int(item[1]), number, image, head)
                elif item[0] == "M":
                    i = int(item[1])
                    a, b = band_of_queries(i)
                    dve.wait_ge(scratch_filled, number + 1)
                    dve.tensor_reduce(neg_max[:, i:i + 1], scratch[:, 0:T + 2 * (b - a)], AX.X, ALU.max, negate=True).then_inc(scratch_read, 1)
                elif item == "TX":
                    norm_chain.begin(dve, image)
                    dve.wait_ge(scratch_filled, number + 1)
                    norm_chain.step(dve.tensor_reduce(total[:], scratch_tiles, AX.X, ALU.add))
                    norm_chain.step(dve.tensor_scalar(mean[:], total[:], 1.0 / C, None, ALU.mult))
                    dve.tensor_tensor(xc[:], scratch_tiles, col_bcast(mean[:], C), ALU.subtract).then_inc(scratch_read, 1)
                elif item == "X":
                    dve.wait_ge(scratch_filled, number + 1)
                    dve.tensor_copy(qs[3 * DH:3 * DH + 1, head, :], scratch[0:1, 0:T]).then_inc(scratch_read, 1)
                elif item == "V":
                    dve.wait_ge(values_high, image + 1)
                    dve.tensor_tensor(vals[:, :, :, 2, :], values_in_scratch, raw(vals[:, :, :, 0, :]), ALU.subtract).then_inc(scratch_read, 1)
                elif item == "O":
                    dve.wait_ge(scratch_filled, number + 1)
                    dve.wait_ge(y_loaded, 16 * image + 16)
                    dve.scalar_tensor_tensor(y[:], scratch[:, 0:T], bias_out[:], y[:], ALU.add, ALU.add).then_inc(scratch_read, 1)

            def variance(n):
                dve.wait_ge(squared, n + 1)
                norm_chain.step(dve.tensor_reduce(total[:], sq[:], AX.X, ALU.add))
                norm_chain.end()
                dve.tensor_scalar(var[:], total[:], (1.0 + 1e-5) / C, 1e-10, ALU.mult, ALU.add).then_inc(var_ready, 1)

            def normalise(n):
                dve.wait_ge(rstd_ready, n + 1)
                dve.tensor_tensor(xc[:], xc[:], col_bcast(rstd[:], C), ALU.mult).then_inc(normed, 1)

            def split_z(n):
                dve.wait_ge(scratch_read, prepared_number(n, "TN") + 1)
                dve.tensor_copy(zh[:], z).then_inc(z_high, 1)
                dve.wait_ge(z_high, n + 1)
                dve.tensor_tensor(zl[:], z, raw(zh[:]), ALU.subtract).then_inc(z_low, 1)

            def split_q(n):
                dve.wait_ge(scratch_read, prepared_number(n, "Q") + 1)
                if not is_first(n):
                    dve.wait_ge(stack_loaded[HEADS - 1], 96 * n)
                dve.tensor_copy(qh[:], qk[:]).then_inc(q_high, 1)
                dve.wait_ge(q_high, n + 1)
                dve.tensor_tensor(ql[:], qk[:], raw(qh[:]), ALU.subtract).then_inc(q_low, 1)

            def split_k(n):
                dve.wait_ge(scratch_read, prepared_number(n, "K") + 1)
                dve.tensor_copy(kh[:], qk[:]).then_inc(k_high, 1)
                dve.wait_ge(k_high, n + 1)
                dve.tensor_tensor(kl[:], qk[:], raw(kh[:]), ALU.subtract).then_inc(k_low, 1)

            def divide_sums(hh, h, stage):
                low = slice(DH, 2 * DH)
                if stage == 0:
                    context_chain.begin(dve, hh)
                    dve.wait_ge(sums_read, hh + 1)
                    context_chain.step(dve.transpose(flat(by_block[low, :, :]), sums[low, :]))
                    context_chain.step(dve.reciprocal(recip[low, :], by_block[low, :, 0]))
                elif stage == 1:
                    context_chain.step(dve.tensor_copy(by_block[low, :, :], col_bcast(recip[low, :], DH)))
                    dve.transpose(recip_all[:], flat(by_block[low, :, :])).then_inc(turned_back, 1)
                elif stage == 2:
                    context_chain.step(dve.tensor_tensor(sums_rest[:], sums_rest[:], sums[0:DH, :], ALU.add))
                    context_chain.end()
                else:
                    dve.wait_ge(turned_back, hh + 1)
                    dve.tensor_tensor(context[h * DH:(h + 1) * DH, :], sums_rest[:], recip_all[:], ALU.mult).then_inc(context_ready, 1)

            def prologue(item, number):
                consume(item, number, 0, 0)
                if item == "TX":
                    variance(0)
                    normalise(0)
                elif item == "TN":
                    split_z(0)
                elif item == "Q":
                    split_q(0)
                elif item == "K":
                    split_k(0)

            later = {(0, 6): variance, (1, 0): normalise, (1, 5): split_z, (2, 2): split_q, (2, 4): split_k}

            def step(n, h, i, amid, before, after):
                for item in amid:
                    consume(*item)
                if 3 <= i < 7 and not (is_first(n) and h == 0):
                    divide_sums(HEADS * n + h - 1, (h - 1) % HEADS, i - 3)
                if (h, i) in later and not is_last(n):
                    later[h, i](n + 1)
                for item in before + after:
                    consume(*item)

            image_loop(dve, prologue, step)
            for stage in range(4):
                divide_sums(HEADS * NB - 1, HEADS - 1, stage)
            consume("O", LAST_O, NB - 1, 0)

        @block.tensor
        def _(pe):
            pe.wait_ge(loaded, 17 * 16)
            pe.wait_ge(setup_step, 4)
            for s in range(2):
                pe.matmul(scratch[:, s * HEADS:(s + 1) * HEADS], wpos[:, s, :], v_less_u[:], start=True, stop=True)
            pe.matmul(scratch[:, 2 * HEADS:2 * HEADS + 1], wout[:], vec[:, 4:5], start=True, stop=True).then_inc(setup_ps, 1)
            pe.wait_ge(setup_step, 5)
            pe.wait_ge(consts_set, 7)

            def total_up(bank_of, products, amid=()):
                first, last = {}, {}
                for j, (a, b, _, _) in enumerate(products):
                    first.setdefault(a // HALF, j)
                    last[a // HALF] = j
                for j, (a, b, left, right) in enumerate(products):
                    if j == len(products) * MIDDLE // 8:
                        for item in amid:
                            fill(*item)
                    ins = pe.matmul(bank_of[:, a:b], left, right, start=(first[a // HALF] == j), stop=(last[a // HALF] == j),
                                    skip_group_check=True)
                return ins

            def by_bank(a, b):
                while a < b:
                    end = min(b, (a // HALF + 1) * HALF)
                    yield a, end
                    a = end

            def scores(h, i, amid):
                keys = slice(i * P, (i + 1) * P)
                a, b = band_of_keys(i)
                nxt = T
                cut = a - (i * P - 2)
                rh, rl = rot_h[h % 2], rot_l[h % 2]
                products = []
                stacked = ks[:, h, keys]
                for c in (0, HALF):
                    products.append((c, c + HALF, stacked, qs[:, h, c:c + HALF]))
                products.append((nxt, nxt + 2 * (b - a), stacked, twice(qs[:, h, a:b])))
                for kt, r in ((keys_h, rh), (keys_h, rl), (keys_l, rh)):
                    for c, d in by_bank(a, T):
                        products.append((c, d, kt[:, 0, keys], r[:, c:d]))
                    for c, d in by_bank(0, a):
                        products.append((c, d, kt[:, 1, keys], r[:, c + 1:d + 1]))
                    products.append((nxt, nxt + b - a, kt[:, 1, keys], r[:, a + 1:b + 1]))
                for c, d in by_bank(a, b):
                    products.append((c, d, identr[:], masks[:, 0, cut + c - a:cut + d - a]))
                products.append((nxt, nxt + 2 * (b - a), identr[:], masks[:, 1:3, cut:BAND]))
                total_up(score_ps, products, amid).then_inc(scores_done, 1)

            def maxima(h, i):
                tile = slice(i * P, (i + 1) * P)
                after_tile = slice(i * P + 1, (i + 1) * P + 1)
                a, b = band_of_queries(i)
                nxt = T
                rh = rot_h[h % 2]
                stacked = qs[0:3 * DH, h, tile]
                products = [(c, c + HALF, stacked, ks[0:3 * DH, h, c:c + HALF]) for c in (0, HALF)]
                products.append((nxt, nxt + 2 * (b - a), stacked, twice(ks[0:3 * DH, h, a:b])))
                for c, d in by_bank(0, b):
                    products.append((c, d, rh[:, tile], keys_h[:, 0, c:d]))
                for c, d in by_bank(b, T):
                    products.append((c, d, rh[:, after_tile], keys_h[:, 1, c:d]))
                products.append((nxt, nxt + b - a, rh[:, after_tile], keys_h[:, 1, a:b]))
                for c, d in by_bank(a, b):
                    products.append((c, d, identr[:], masks[:, 3, c - a:d - a]))
                products.append((nxt, nxt + 2 * (b - a), identr[:], masks[:, 4:6, 0:b - a]))
                return total_up(scratch, products)

            def fill(item, number, image, head):
                pe.wait_ge(scratch_read, number)
                if item == "TX":
                    pe.wait_ge(x_loaded, 16 * image + 16)
                    for t in range(TT):
                        last = pe.transpose(scratch[:, t * P:(t + 1) * P], x[:, t * P:(t + 1) * P], ident[:])
                elif item == "TN":
                    pe.wait_ge(normed, image + 1)
                    for t in range(TT):
                        last = pe.transpose(scratch[:, t * P:(t + 1) * P], xc[:, t, :], ident[:])
                elif item in ("Q", "K"):
                    pe.wait_ge(z_low, image + 1)
                    w = 0 if item == "Q" else 1
                    last = total_up(scratch, [(c, c + HALF, a[:, w, :], b[:, c:c + HALF])
                                              for a, b in ((wh, zh), (wl, zh), (wh, zl)) for c in (0, HALF)])
                elif item == "V":
                    last = total_up(scratch, [(t * P, (t + 1) * P, b[:, t * P:(t + 1) * P], a[:, 2, :])
                                              for a, b in ((wh, zh), (wl, zh), (wh, zl)) for t in range(TT)])
                elif item[0] == "R":
                    part = slice(int(item[1]) * HALF, (int(item[1]) + 1) * HALF)
                    pe.wait_ge(stack_loaded[head], 96 * (image + 1))
                    last = total_up(scratch, [(s * HALF, (s + 1) * HALF, posw[:, head, s, :], qs[0:3 * DH, head, part])
                                              for s in range(2)])
                elif item[0] == "M":
                    if item == "M0":
                        pe.wait_ge(rot_chain.sem, 6 * (HEADS * image + head) + 3)
                    if item == "M3":
                        pe.wait_ge(rot_chain.sem, 6 * (HEADS * image + head) + 6)
                    last = maxima(head, int(item[1]))
                elif item == "X":
                    for t in range(TT):
                        last = pe.transpose(scratch[0:1, t * P:(t + 1) * P], neg_max[:, t:t + 1], ident[:])
                elif item == "O":
                    pe.wait_ge(context_ready, HEADS * (image + 1))
                    for c in (0, HALF):
                        last = pe.matmul(scratch[:, c:c + HALF], wout[:], context[:, c:c + HALF], start=True, stop=True)
                last.then_inc(scratch_filled, 1)

            def sum_values(n, h, i):
                J = HEADS * STEPS * n + STEPS * h + i
                pe.wait_ge(weights_ready, J + 1)
                if i == 0:
                    if h == 0:
                        pe.wait_ge(scratch_read, number_of(n, "V") + 1)
                    if not (is_first(n) and h == 0):
                        pe.wait_ge(sums_read, HEADS * n + h)
                both = vals[:, i, h, :, :].rearrange("p a d -> p (a d)")
                for part in (weights_h[i % 2], weights_l[i % 2]):
                    for c in (0, HALF):
                        last = pe.matmul(sum_ps[0:3 * DH, c:c + HALF], both, part[:, c:c + HALF],
                                         start=(i == 0 and part is weights_h[i % 2]), stop=(i == STEPS - 1 and part is weights_l[i % 2]))
                last.then_inc(sums_done, 1)

            def step(n, h, i, amid, before, after):
                J = HEADS * STEPS * n + STEPS * h + i
                if not (is_first(n) and h == 0 and i == 0):
                    pe.wait_ge(exps_done, J)
                if i == 0:
                    if h == 0:
                        pe.wait_ge(scratch_read, number_of(n, *order[0]))
                    else:
                        pe.wait_ge(scratch_read, number_of(n, "X", h - 1) + 1)
                scores(h, i, amid)
                for item in before:
                    fill(*item)
                if i >= 2:
                    sum_values(n, h, i - 2)
                elif h:
                    sum_values(n, h - 1, STEPS - 2 + i)
                elif not is_first(n):
                    sum_values(n - 1, HEADS - 1, STEPS - 2 + i)
                for item in after:
                    fill(*item)

            image_loop(pe, lambda item, number: fill(item, number, 0, 0), step)
            for i in (STEPS - 2, STEPS - 1):
                sum_values(NB - 1, HEADS - 1, i)
            fill("O", LAST_O, NB - 1, 0)


SIDE = 32
WS = 7
NW = 5
WIN = WS * WS
WINDOWS = NW * NW
SLOTS = (WINDOWS + 1) // 2
PITCH = WS + 2
QROW = PITCH * WS
SLOTS_HALF = 8
SOFTMAX_HALVES = (slice(0, SLOTS_HALF * HEADS), slice(SLOTS_HALF * HEADS, SLOTS * HEADS))
QTAPS_PE = 11
EPS = 1e-5
BN = ("dw0", "ffn0_in0", "ffn0_in1", "ffn0_out", "q", "k_first", "k_second", "value", "qdw", "proj",
      "dw1", "ffn1_in0", "ffn1_in1", "ffn1_out")
AT_WINDOW_SCALE = 0.25


def conv_phase(nc, NB, x_dram, y_dram, bn_dram, taps_dram, qtaps_dram, ffn_in_dram, ffn_out_dram, qk_dram, v_dram,
               proj_dram, bias_dram, group_dram, ident_dram):
    with ExitStack() as ctx:
        def sb(name, shape, dt=F32):
            return ctx.enter_context(nc.sbuf_tensor("conv_" + name, shape, dt))

        def sem(name):
            return ctx.enter_context(nc.semaphore("conv_" + name))

        ident, group = sb("ident", [P, P]), sb("group", [P, P])
        bnp = sb("bnp", [P, 4, len(BN)])
        scale, shift, root = (sb(s, [P, len(BN)]) for s in ("scale", "shift", "root"))
        minus_half = sb("minus_half", [P, len(BN)])
        taps, qtaps = sb("taps", [P, 2, 9]), sb("qtaps", [P, 25])
        w_in, w_out = sb("w_in", [P, 2, 2 * C]), sb("w_out", [P, 2, 2, C])
        w_qk, w_v, w_proj = sb("w_qk", [P, 4, C]), sb("w_v", [P, 2, 64]), sb("w_proj", [P, C])
        bias = sb("bias", [P, HEADS * WIN])
        x, xo = sb("x", [P, T]), sb("xo", [P, T])
        stats, squares, parts = sb("stats", [P, 2, 6]), sb("squares", [P, 4]), sb("parts", [P, 2])
        gm, gsq, gshift = (sb(s, [P, 2]) for s in ("gm", "gsq", "gshift"))
        gvar, grstd = sb("gvar", [P, 1]), sb("grstd", [P, 1])
        xp = sb("xp", [P, SIDE + 2, SIDE + 2])
        x1 = sb("x1", [P, T])
        hidden = sb("hidden", [P, 2, T])
        branch = sb("branch", [P, T])
        x2 = sb("x2", [P, NW * WS, NW * WS])
        xw = sb("xw", [P, WINDOWS, WIN])
        qp = sb("qp", [P, SLOTS * PITCH + 4, WS + 4])
        tap_products = sb("tap_products", [P, QTAPS_PE, P])
        q = sb("q", [P, SLOTS * QROW + 2])
        keys = [sb(f"keys{g}", [P, SLOTS, HEADS, WIN]) for g in range(2)]
        values = sb("values", [P, WINDOWS, 2, 64])
        score = sb("score", [P, SLOTS, HEADS * WIN])
        most, total, recip = (sb(s, [P, SLOTS * HEADS]) for s in ("most", "total", "recip"))
        prob = sb("prob", [P, SLOTS, HEADS, 64])
        probT = sb("probT", [P, 2 * SLOTS, P])
        mixed = sb("mixed", [P, WINDOWS * WIN])
        projected = sb("projected", [P, WINDOWS, WIN])
        x3 = sb("x3", [P, SIDE + 2, SIDE + 2])
        x4 = sb("x4", [P, T])
        branch4 = sb("branch4", [P, T])
        y = sb("y", [P, T])

        zero = [xp[:], x2[:], x3[:], qp[:], q[:, SLOTS * QROW:], keys[0][:], keys[1][:], values[:], prob[:], gshift[:, 1:2]]
        ZEROED, LOADED = len(zero), 11 * 16

        NT = 4
        tile = [ctx.enter_context(nc.psum_tensor(f"conv_tile{r}", [P, 2 * HALF], F32)) for r in range(NT)]

        loaded, const_set, zeroed, root_ready, fold_step, folded = (
            sem(s) for s in ("loaded", "const_set", "zeroed", "root_ready", "fold_step", "folded"))
        tile_filled = [sem(f"tile{r}_filled") for r in range(NT)]
        tile_used = [sem(f"tile{r}_used") for r in range(NT)]
        x_loaded, moments_ready, gvar_ready, grstd_ready, xp_ready, x1_ready = (
            sem(s) for s in ("x_loaded", "moments_ready", "gvar_ready", "grstd_ready", "xp_ready", "x1_ready"))
        x2_ready, xw_ready, shifted, exps_ready = (
            sem(s) for s in ("x2_ready", "xw_ready", "shifted", "exps_ready"))
        x3_ready, x4_ready, xo_loaded, y_step, y_ready, stored = (
            sem(s) for s in ("x3_ready", "x4_ready", "xo_loaded", "y_step", "y_ready", "stored"))
        moment_chain = Chain(sem("moment_step"), 3)
        group_chain = Chain(sem("group_step"), 3)
        x1_added = sem("x1_added")
        conv0_chain = Chain(sem("conv0_step"), 8)
        conv1_chain = Chain(sem("conv1_step"), 8)
        qconv_chain = Chain(sem("qconv_step"), 25 - QTAPS_PE)
        softmax_chain = Chain(sem("softmax_step"), 8)
        block = ctx.enter_context(nc.Block())

        first_items = ["G", "G1", "F0a", "F0b", "F0c"]
        F0, F1 = ["F0a", "F0b", "F0c"], ["F1a", "F1b", "F1c"]
        main_items = (["Q", "K0", "K1"] + [f"C{j}" for j in range(4)] + ["G"] + [f"S{j}" for j in range(4)] + ["V0", "V1"]
                      + F0 + [f"T{j}" for j in range(4)] + ["A0", "A1", "P0", "P1"] + F1)
        FIRST = len(first_items)
        assert len(main_items) % NT == 0

        def is_first(n):
            return isinstance(n, int) and n == 0

        def is_last(n):
            return isinstance(n, int) and n == NB - 1

        def has_after_next(n):
            return not (isinstance(n, int) and n >= NB - 2)

        def items_of(n):
            left_out = (F1 if is_first(n) else []) + (F0 if is_last(n) else []) + ([] if has_after_next(n) else ["G"])
            return [m for m in main_items if m not in left_out]

        def place(n, item):
            if n is None:
                at, whole = first_items.index(item), 0
            elif is_last(n):
                at, whole = FIRST + sum(len(items_of(m)) for m in range(n)) + items_of(n).index(item), 0
            else:
                skipped = 0 if is_first(n) else len(F1)
                at, whole = FIRST - skipped + items_of(n).index(item), len(main_items) // NT * n
            return at % NT, whole + at // NT

        LAST_F1 = FIRST + sum(len(items_of(m)) for m in range(NB))

        def last_place(item):
            at = LAST_F1 + F1.index(item)
            return at % NT, at // NT

        def image_loop(eng, prologue, turn, epilogue):
            prologue()
            turn(0)
            if NB > 3:
                with eng.Fori(1, NB - 2) as n:
                    turn(n)
            if NB > 2:
                turn(NB - 2)
            turn(NB - 1)
            epilogue()

        def bank_cols(j):
            return j // 10 * HALF + j % 10 * WIN

        def col(t, name):
            k = BN.index(name)
            return t[:, k:k + 1]

        def image(t):
            return t[:].rearrange("p (r c) -> p r c", c=SIDE)

        @block.sync
        def _(sp):
            for to, of in ((ident[:], ident_dram), (group[:], group_dram), (bnp[:], bn_dram), (taps[:], taps_dram),
                           (qtaps[:], qtaps_dram), (w_in[:], ffn_in_dram), (w_out[:], ffn_out_dram), (w_qk[:], qk_dram),
                           (w_v[:], v_dram), (w_proj[:], proj_dram), (bias[:], bias_dram)):
                sp.dma_start(to, of).then_inc(loaded, 16)
            sp.dma_start(x[:], x_dram[0]).then_inc(x_loaded, 16)
            for n in range(1, min(3, NB)):
                sp.wait_ge(xp_ready, n)
                sp.dma_start(x[:], x_dram[n]).then_inc(x_loaded, 16)

            def store(n):
                sp.wait_ge(y_ready, n + 1)
                sp.dma_start(y_dram[n], y[:]).then_inc(stored, 16)

            def turn(n):
                if not (isinstance(n, int) and n >= NB - 3):
                    sp.wait_ge(xp_ready, n + 3)
                    sp.dma_start(x[:], x_dram[n + 3]).then_inc(x_loaded, 16)
                if not is_first(n):
                    store(n - 1)
                sp.dma_start(xo[:], x_dram[n]).then_inc(xo_loaded, 16)

            turn(0)
            if NB > 4:
                with sp.Fori(1, NB - 3) as n:
                    turn(n)
            for n in range(max(NB - 3, 1), NB):
                turn(n)
            store(NB - 1)
            sp.wait_ge(stored, 16 * NB)

        def used(eng, where):
            eng.wait_ge(tile_used[where[0]], where[1] + 1)

        def filled(eng, where):
            eng.wait_ge(tile_filled[where[0]], where[1] + 1)

        def prepared(n, item):
            if item == "G" and isinstance(n, int) and n < 2:
                return place(None, ("G", "G1")[n])
            return place(None, item) if is_first(n) else place(n - (2 if item == "G" else 1), item)

        def last_ffn(n, item):
            return last_place(item) if is_last(n) else place(n + 1, item)

        @block.gpsimd
        def _(pool):
            pool.memset(minus_half[:], -0.5).then_inc(const_set, 1)
            pool.wait_ge(const_set, 1)
            pool.wait_ge(fold_step, 1)
            pool.tensor_tensor(root[:], root[:], minus_half[:], ALU.pow).then_inc(root_ready, 1)

            def group_root(n):
                pool.wait_ge(gvar_ready, n + 1)
                pool.tensor_tensor(grstd[:], gvar[:], minus_half[:, 0:1], ALU.pow).then_inc(grstd_ready, 1)

            def add_branch(n):
                used(pool, prepared(n, "F0c"))
                pool.tensor_tensor(branch[:], branch[:], x1[:], ALU.add).then_inc(x1_added, 1)

            def add_last(n):
                used(pool, last_ffn(n, "F1c"))
                if not is_first(n):
                    pool.wait_ge(stored, 16 * n)
                pool.tensor_tensor(y[:], branch4[:], x4[:], ALU.add).then_inc(y_step, 1)
                pool.wait_ge(y_step, n + 1)
                pool.wait_ge(xo_loaded, 16 * n + 16)
                pool.tensor_tensor(y[:], y[:], xo[:], ALU.add).then_inc(y_ready, 1)

            def prologue():
                group_root(0)
                group_root(1)
                add_branch(0)

            def turn(n):
                if has_after_next(n):
                    group_root(n + 2)
                if not is_last(n):
                    add_branch(n + 1)
                if not is_first(n):
                    add_last(n - 1)

            image_loop(pool, prologue, turn, lambda: add_last(NB - 1))

        @block.scalar
        def _(act):
            act.wait_ge(loaded, LOADED)
            act.wait_ge(folded, 1)
            act.wait_ge(zeroed, ZEROED)

            def batch_norm(where, out, source, name, func=ACT.Identity, rows=slice(0, P), last=True):
                ins = act.activation(out, source, func, bias=col(shift, name)[rows, :], scale=col(scale, name)[rows, :])
                if last:
                    ins.then_inc(tile_used[where[0]], 1)

            def into_windows(n):
                act.wait_ge(x1_added, n + 1)
                if not is_first(n):
                    act.wait_ge(x3_ready, n)
                act.activation(x2[:, 0:SIDE, 0:SIDE], image(branch), ACT.Copy).then_inc(x2_ready, 1)
                act.wait_ge(x2_ready, n + 1)
                for row in range(NW):
                    cut = x2[:, row * WS:(row + 1) * WS, :].rearrange("p r (w c) -> p w r c", w=NW)
                    ins = act.activation(xw[:, row * NW:(row + 1) * NW, :].rearrange("p w (r c) -> p w r c", r=WS), cut, ACT.Copy)
                ins.then_inc(xw_ready, 1)

            def ffn(where, number, out, parts="abc"):
                for j, item in enumerate("abc"):
                    if item not in parts:
                        continue
                    at = where(f"F{number}{item}")
                    filled(act, at)
                    if j < 2:
                        batch_norm(at, hidden[:, j, :], tile[at[0]][:], f"ffn{number}_in{j}", ACT.Relu)
                    else:
                        batch_norm(at, out[:], tile[at[0]][:], f"ffn{number}_out")

            def ffn0(n):
                if not is_first(n):
                    act.wait_ge(x2_ready, n)
                ffn(lambda item: prepared(n, item), 0, branch)

            def ffn1(n, parts):
                if "c" in parts and not is_first(n):
                    act.wait_ge(y_step, n)
                ffn(lambda item: last_ffn(n, item), 1, branch4, parts)

            def turn(n):
                at = place(n, "Q")
                filled(act, at)
                inside = qp[:, 2:2 + SLOTS * PITCH, 2:2 + WS].rearrange("p (s r) c -> p s r c", r=PITCH)
                for s, k in ((0, 10), (10, SLOTS - 10)):
                    source = tile[at[0]][:, bank_cols(s):bank_cols(s) + k * WIN].rearrange("p (s r c) -> p s r c", s=k, r=WS)
                    batch_norm(at, inside[:, s:s + k, 0:WS, :], source, "q", last=(s > 0))
                for g in range(2):
                    at = place(n, f"K{g}")
                    filled(act, at)
                    for h in range(HEADS):
                        rows = slice(h * DH, (h + 1) * DH)
                        for s, k in ((0, 10), (10, SLOTS - 10)):
                            source = tile[at[0]][rows, bank_cols(s):bank_cols(s) + k * WIN].rearrange("p (s m) -> p s m", s=k)
                            batch_norm(at, keys[g][rows, s:s + k, h, :], source, ("k_first", "k_second")[g], rows=rows,
                                       last=(h == HEADS - 1 and s > 0))
                for v, slots in enumerate((slice(0, SLOTS_HALF), slice(SLOTS_HALF, SLOTS))):
                    at = place(n, f"V{v}")
                    filled(act, at)
                    first, k = 16 * v, min(16, WINDOWS - 16 * v)
                    for low in range(2):
                        rows = slice(64 * low, 64 * low + WIN)
                        source = tile[at[0]][rows, 0:k * 64].rearrange("p (w a d) -> p w a d", w=k, a=2)
                        ins = act.activation(values[rows, first:first + k, :, low * DH:(low + 1) * DH], source, ACT.Copy)
                    ins.then_inc(tile_used[at[0]], 1)
                    act.wait_ge(shifted, 2 * n + v + 1)
                    act.activation(prob[:, slots, :, 0:WIN], score[:, slots, :].rearrange("p s (h m) -> p s h m", h=HEADS),
                                   ACT.Exp).then_inc(exps_ready, 1)
                if not is_last(n):
                    ffn0(n + 1)
                for j in range(4):
                    at = place(n, f"T{j}")
                    k = min(8, 2 * SLOTS - 8 * j)
                    filled(act, at)
                    act.activation(flat(probT[:, 8 * j:8 * j + k, :]), tile[at[0]][:, 0:k * P], ACT.Copy).then_inc(tile_used[at[0]], 1)
                for name, out, bn, func in (("A", mixed, "value", ACT.Relu), ("P", projected, "proj", ACT.Identity)):
                    for j, (first, k) in enumerate(((0, 20), (20, WINDOWS - 20))):
                        at = place(n, f"{name}{j}")
                        filled(act, at)
                        banks = [(w, min(10, k - w)) for w in range(0, k, 10)]
                        for w, kk in banks:
                            to = out[:, first + w:first + w + kk, :] if name == "P" else out[:, (first + w) * WIN:(first + w + kk) * WIN]
                            source = tile[at[0]][:, bank_cols(w):bank_cols(w) + kk * WIN]
                            if name == "P":
                                to = flat(to)
                            batch_norm(at, to, source, bn, func, last=(w == banks[-1][0]))
                if not is_first(n):
                    ffn1(n - 1, "ab")
                if not is_last(n):
                    into_windows(n + 1)
                if not is_first(n):
                    ffn1(n - 1, "c")

            def prologue():
                ffn0(0)
                into_windows(0)

            image_loop(act, prologue, turn, lambda: ffn1(NB - 1, "abc"))

        @block.vector
        def _(dve):
            for t in zero:
                dve.memset(t, 0.0).then_inc(zeroed, 1)
            dve.wait_ge(loaded, LOADED)
            dve.tensor_scalar(root[:], bnp[:, 3, :], EPS, None, ALU.add).then_inc(fold_step, 1)
            dve.wait_ge(root_ready, 1)
            dve.tensor_tensor(scale[:], bnp[:, 0, :], root[:], ALU.mult).then_inc(fold_step, 1)
            dve.wait_ge(fold_step, 2)
            dve.tensor_tensor(shift[:], bnp[:, 2, :], scale[:], ALU.mult).then_inc(fold_step, 1)
            dve.wait_ge(fold_step, 3)
            dve.tensor_tensor(shift[:], bnp[:, 1, :], shift[:], ALU.subtract).then_inc(fold_step, 1)
            for j, name in enumerate(("dw0", "dw1")):
                dve.tensor_scalar(taps[:, j, :], taps[:, j, :], col(scale, name), None, ALU.mult).then_inc(fold_step, 1)
            dve.wait_ge(fold_step, 6)
            dve.tensor_scalar(taps[:, :, 4:5], taps[:, :, 4:5], 1.0, None, ALU.add).then_inc(fold_step, 1)
            dve.tensor_scalar(qtaps[:], qtaps[:], col(scale, "qdw"), None, ALU.mult).then_inc(fold_step, 1)
            dve.wait_ge(fold_step, 8)
            dve.wait_ge(zeroed, ZEROED)
            of_channel = qtaps[:, 25 - QTAPS_PE:25].unsqueeze(2).to_broadcast([P, QTAPS_PE, P])
            dve.tensor_tensor(tap_products[:], ident[:].unsqueeze(1).to_broadcast([P, QTAPS_PE, P]), of_channel, ALU.mult)
            dve.tensor_copy(gshift[:, 0:1], gshift[:, 1:2]).then_inc(folded, 1)

            def convolve(chain, n, out, source, weights, taps_a_side, rows, width, bn, ready, meanwhile=None):
                chain.begin(dve, n)
                steps = [(dy, dx) for dy in range(taps_a_side) for dx in range(taps_a_side)]
                if ready is None:
                    steps = steps[:chain.per]
                for j, (dy, dx) in enumerate(steps):
                    if meanwhile is not None and j == len(steps) // 2:
                        meanwhile()
                    shifted_in = source[:, dy:dy + rows, dx:dx + width]
                    tap = weights[:, j:j + 1]
                    if j == 0:
                        ins = dve.tensor_scalar(out, shifted_in, tap, col(shift, bn), ALU.mult, ALU.add)
                    else:
                        ins = dve.scalar_tensor_tensor(out, shifted_in, tap, out, ALU.mult, ALU.add)
                    if ready is not None and j == len(steps) - 1:
                        ins.then_inc(ready, 1)
                    else:
                        chain.step(ins)
                chain.end()

            def moments_of(n):
                moment_chain.begin(dve, n)
                dve.wait_ge(x_loaded, 16 * n + 16)
                for c in range(2):
                    ins = dve.bn_stats(stats[:, c, :], x[:, c * HALF:(c + 1) * HALF])
                moment_chain.step(ins)
                quarters = flat(stats[:]).rearrange("p (q k) -> p q k", k=3)
                means, deviations = quarters[:, :, 1], quarters[:, :, 2]
                moment_chain.step(dve.tensor_tensor(squares[:], means, means, ALU.mult))
                moment_chain.step(dve.scalar_tensor_tensor(squares[:], deviations, 4.0 / T, squares[:], ALU.mult, ALU.add))
                moment_chain.end()
                dve.tensor_reduce(parts[:, 0:1], means, AX.X, ALU.add)
                dve.tensor_reduce(parts[:, 1:2], squares[:], AX.X, ALU.add).then_inc(moments_ready, 1)

            def group_moments(n):
                group_chain.begin(dve, n)
                at = prepared(n, "G")
                filled(dve, at)
                dve.tensor_copy(gm[:], tile[at[0]][:, 0:2]).then_inc(tile_used[at[0]], 1)
                used(dve, at)
                group_chain.step(dve.tensor_tensor(gsq[:, 0:1], gm[:, 0:1], gm[:, 0:1], ALU.mult))
                group_chain.step(dve.tensor_tensor(gsq[:, 1:2], gm[:, 1:2], gsq[:, 0:1], ALU.subtract))
                dve.tensor_scalar(gvar[:], gsq[:, 1:2], EPS, None, ALU.add).then_inc(gvar_ready, 1)

            def group_norm(n):
                dve.wait_ge(grstd_ready, n + 1)
                group_chain.step(dve.scalar_tensor_tensor(gshift[:, 0:1], gm[:, 0:1], -1.0, grstd[:], ALU.mult, ALU.mult))
                group_chain.end()
                dve.tensor_scalar(xp[:, 1:SIDE + 1, 1:SIDE + 1], image(x), grstd[:], gshift[:, 0:1], ALU.mult, ALU.add).then_inc(xp_ready, 1)

            def first_convolution(n, meanwhile=None):
                dve.wait_ge(xp_ready, n + 1)
                if not is_first(n):
                    dve.wait_ge(x1_added, n)
                convolve(conv0_chain, n, image(x1), xp, taps[:, 0, :], 3, SIDE, SIDE, "dw0", x1_ready, meanwhile)

            def last_convolution(n):
                dve.wait_ge(x3_ready, n + 1)
                if isinstance(n, int) and n:
                    dve.wait_ge(y_step, n)
                convolve(conv1_chain, n, image(x4), x3, taps[:, 1, :], 3, SIDE, SIDE, "dw1", x4_ready)

            def add_attention(n):
                if not is_first(n):
                    dve.wait_ge(x4_ready, n)
                for j in range(2):
                    used(dve, place(n, f"P{j}"))
                for row in range(NW):
                    k = min(WS, SIDE - row * WS)
                    for first, windows, width in ((0, NW - 1, WS), (NW - 1, 1, SIDE - (NW - 1) * WS)):
                        def cut(t, border):
                            part = t[:, border + row * WS:border + row * WS + k, border + first * WS:border + first * WS + windows * width]
                            return part.rearrange("p r (w c) -> p r w c", w=windows)
                        w = row * NW + first
                        add = projected[:, w:w + windows, :].rearrange("p w (r c) -> p r w c", r=WS)[:, 0:k, :, 0:width]
                        ins = dve.tensor_tensor(cut(x3, 1), cut(x2, 0), add, ALU.add)
                ins.then_inc(x3_ready, 1)

            def turn(n):
                if has_after_next(n):
                    moments_of(n + 2)
                used(dve, place(n, "Q"))
                convolve(qconv_chain, n, q[:, 0:SLOTS * QROW].rearrange("p (r c) -> p r c", c=WS), qp, qtaps[:], 5,
                         SLOTS * PITCH, WS, "qdw", None)
                for j in range(4):
                    at = place(n, f"C{j}")
                    filled(dve, at)
                    part = slice(4 * j * QROW, min(4 * j + 4, SLOTS) * QROW)
                    dve.tensor_tensor(q[:, part], q[:, part], tile[at[0]][:, 0:part.stop - part.start], ALU.add).then_inc(tile_used[at[0]], 1)
                if has_after_next(n):
                    group_moments(n + 2)
                softmax_chain.begin(dve, n)
                by_head = score[:].rearrange("p s (h m) -> p (s h) m", h=HEADS)
                for part, tiles in zip(SOFTMAX_HALVES, ((0, 1), (2, 3))):
                    for j in tiles:
                        at = place(n, f"S{j}")
                        filled(dve, at)
                        k = min(4, SLOTS - 4 * j)
                        for s in range(0, k, 2):
                            kk = min(2, k - s)
                            source = tile[at[0]][:, s // 2 * HALF:s // 2 * HALF + kk * HEADS * WIN].rearrange("p (s m) -> p s m", s=kk)
                            ins = dve.scalar_tensor_tensor(score[:, 4 * j + s:4 * j + s + kk, :], source, AT_WINDOW_SCALE,
                                                           bias[:].unsqueeze(1).to_broadcast([P, kk, HEADS * WIN]), ALU.mult, ALU.add)
                        ins.then_inc(tile_used[at[0]], 1)
                    for j in tiles:
                        used(dve, place(n, f"S{j}"))
                    softmax_chain.step(dve.tensor_reduce(most[:, part], by_head[:, part, :], AX.X, ALU.max))
                    dve.tensor_tensor(by_head[:, part, :], by_head[:, part, :], col_bcast(most[:, part], WIN), ALU.subtract).then_inc(shifted, 1)
                if has_after_next(n):
                    group_norm(n + 2)
                weights = prob[:].rearrange("p s h m -> p (s h) m")[:, :, 0:WIN]
                for j, part in enumerate(SOFTMAX_HALVES):
                    dve.wait_ge(exps_ready, 2 * n + j + 1)
                    softmax_chain.step(dve.tensor_reduce(total[:, part], weights[:, part, :], AX.X, ALU.add))
                    softmax_chain.step(dve.reciprocal(recip[:, part], total[:, part]))
                    softmax_chain.step(dve.tensor_tensor(weights[:, part, :], weights[:, part, :], col_bcast(recip[:, part], WIN), ALU.mult))
                softmax_chain.end()
                if not is_first(n):
                    last_convolution(n - 1)
                if has_after_next(n):
                    first_convolution(n + 2, lambda: add_attention(n))
                else:
                    add_attention(n)

            def prologue():
                moments_of(0)
                group_moments(0)
                group_norm(0)
                first_convolution(0)
                moments_of(1)
                group_moments(1)
                group_norm(1)
                first_convolution(1)

            image_loop(dve, prologue, turn, lambda: last_convolution(NB - 1))

        @block.tensor
        def _(pe):
            pe.wait_ge(loaded, LOADED)
            pe.wait_ge(zeroed, ZEROED)

            def begin(where):
                pe.wait_ge(tile_used[where[0]], where[1])
                return tile[where[0]]

            def ffn(where, number, source):
                for j in range(2):
                    at = where(f"F{number}{'ab'[j]}")
                    to = begin(at)
                    for c in (0, HALF):
                        last = pe.matmul(to[:, c:c + HALF], w_in[:, number, j * C:(j + 1) * C], source[:, c:c + HALF], start=True, stop=True)
                    last.then_inc(tile_filled[at[0]], 1)
                at = where(f"F{number}c")
                to = begin(at)
                for j in range(2):
                    used(pe, where(f"F{number}{'ab'[j]}"))
                for c in (0, HALF):
                    for j in range(2):
                        last = pe.matmul(to[:, c:c + HALF], w_out[:, number, j, :], hidden[:, j, c:c + HALF], start=(j == 0), stop=(j == 1))
                last.then_inc(tile_filled[at[0]], 1)

            def moments_mean(n):
                at = prepared(n, "G")
                to = begin(at)
                pe.wait_ge(moments_ready, n + 1)
                pe.matmul(to[:, 0:2], group[:], parts[:], start=True, stop=True).then_inc(tile_filled[at[0]], 1)

            def ffn0(n):
                pe.wait_ge(x1_ready, n + 1)
                ffn(lambda item: prepared(n, item), 0, x1)

            def ffn1(n):
                pe.wait_ge(x4_ready, n + 1)
                ffn(lambda item: last_ffn(n, item), 1, x4)

            def by_windows(to, products):
                begun = set()
                for w, first, count, slot in products:
                    while count:
                        k = min(count, 10 - slot % 10)
                        last = pe.matmul(to[:, bank_cols(slot):bank_cols(slot) + k * WIN], w, flat(xw[:, first:first + k, :]),
                                         start=slot // 10 not in begun, stop=True, skip_group_check=True)
                        begun.add(slot // 10)
                        first, slot, count = first + k, slot + k, count - k
                return last

            def prologue():
                moments_mean(0)
                moments_mean(1)
                ffn0(0)

            def turn(n):
                pe.wait_ge(xw_ready, n + 1)
                at = place(n, "Q")
                last = by_windows(begin(at), [(w_qk[:, 0, :], 0, SLOTS, 0), (w_qk[:, 1, :], SLOTS, WINDOWS - SLOTS, 0)])
                last.then_inc(tile_filled[at[0]], 1)
                for g in range(2):
                    at = place(n, f"K{g}")
                    first = SLOTS * g
                    last = by_windows(begin(at), [(w_qk[:, 2 + g, :], first, min(SLOTS, WINDOWS - first), 0)])
                    last.then_inc(tile_filled[at[0]], 1)
                used(pe, place(n, "Q"))
                for j in range(4):
                    at = place(n, f"C{j}")
                    to = begin(at)
                    rows, end = 4 * j * PITCH, min(4 * j + 4, SLOTS) * PITCH
                    for t in range(QTAPS_PE):
                        dy, dx = divmod(25 - QTAPS_PE + t, 5)
                        last = pe.matmul(to[:, 0:(end - rows) * WS], tap_products[:, t, :], qp[:, rows + dy:end + dy, dx:dx + WS],
                                         start=(t == 0), stop=(t == QTAPS_PE - 1))
                    last.then_inc(tile_filled[at[0]], 1)
                if has_after_next(n):
                    moments_mean(n + 2)
                for g in range(2):
                    used(pe, place(n, f"K{g}"))
                for j in range(4):
                    at = place(n, f"S{j}")
                    to = begin(at)
                    for c in {0: (0, 1), 1: (2,), 2: (3,), 3: ()}[j]:
                        used(pe, place(n, f"C{c}"))
                    for s in range(min(4, SLOTS - 4 * j)):
                        slot = 4 * j + s
                        c = s // 2 * HALF + s % 2 * HEADS * WIN
                        for g in range(2):
                            last = pe.matmul(to[64 * g:64 * g + 64, c:c + HEADS * WIN], q[:, slot * QROW:slot * QROW + 64],
                                             keys[g][:, slot, :, :].rearrange("p h m -> p (h m)"), start=True, stop=True)
                    last.then_inc(tile_filled[at[0]], 1)
                for v in range(2):
                    at = place(n, f"V{v}")
                    to = begin(at)
                    for j in range(min(16, WINDOWS - 16 * v)):
                        for low in range(2):
                            last = pe.matmul(to[64 * low:64 * low + WIN, 64 * j:64 * j + 64], xw[:, 16 * v + j, :], w_v[:, low, :], start=True, stop=True)
                    last.then_inc(tile_filled[at[0]], 1)
                if not is_last(n):
                    ffn0(n + 1)
                for j in range(4):
                    if j % 2 == 0:
                        pe.wait_ge(softmax_chain.sem, 8 * n + (5 if j == 0 else 8))
                    at = place(n, f"T{j}")
                    to = begin(at)
                    for t in range(min(8, 2 * SLOTS - 8 * j)):
                        slot, pair = divmod(8 * j + t, 2)
                        last = pe.transpose(to[:, t * P:(t + 1) * P], prob[:, slot, 2 * pair:2 * pair + 2, :].rearrange("p h m -> p (h m)"), ident[:])
                    last.then_inc(tile_filled[at[0]], 1)
                for j in range(4):
                    used(pe, place(n, f"T{j}"))
                for j, (first, k) in enumerate(((0, 20), (20, WINDOWS - 20))):
                    at = place(n, f"A{j}")
                    to = begin(at)
                    for w in range(k):
                        group_of, slot = divmod(first + w, SLOTS)
                        for pair in range(2):
                            last = pe.matmul(to[64 * pair:64 * pair + 64, bank_cols(w):bank_cols(w) + WIN], values[:, first + w, pair, :],
                                             probT[:, 2 * slot + pair, 64 * group_of:64 * group_of + WIN], start=True, stop=True)
                    last.then_inc(tile_filled[at[0]], 1)
                for j, (first, k) in enumerate(((0, 20), (20, WINDOWS - 20))):
                    at = place(n, f"P{j}")
                    to = begin(at)
                    used(pe, place(n, f"A{j}"))
                    for w in range(0, k, 10):
                        kk = min(10, k - w)
                        last = pe.matmul(to[:, bank_cols(w):bank_cols(w) + kk * WIN], w_proj[:],
                                         mixed[:, (first + w) * WIN:(first + w + kk) * WIN], start=True, stop=True)
                    last.then_inc(tile_filled[at[0]], 1)
                if not is_first(n):
                    ffn1(n - 1)

            image_loop(pe, prologue, turn, lambda: ffn1(NB - 1))

def tables():
    rate = np.repeat(np.exp(np.arange(0, C, 2) * (-np.log(10000.0) / C)), 2)[:, None]
    place = np.arange(T)[None, :]
    odd = (np.arange(C) % 2)[:, None]
    angle = (T - 1 - place) * rate
    rot = np.stack([np.cos(angle), np.sin(angle) * (2 * odd - 1)])
    keys = np.stack([np.where(odd, np.cos(m * rate), np.sin(m * rate)) for m in (place, place - T)])
    one, other = np.arange(P)[:, None], np.arange(BAND)[None, :]
    by_key = other - 2 - one
    by_query = one - other
    masks = [np.where(keep, 0.0, NEG) for d in (by_key, by_query) for keep in (d >= 0, d <= -2, d == -1)]
    masks = np.stack(masks, 1).reshape(P, 6 * BAND)
    lower = np.broadcast_to(np.tril(np.ones((E, E)), -1).reshape(-1), (P, E * E))
    return {name: np.ascontiguousarray(a.astype(np.float32)) for name, a in
            (("heads", np.arange(C)[:, None] // DH == np.arange(HEADS)[None, :]), ("rot", rot), ("keys", keys), ("masks", masks), ("lower", lower), ("ident", np.eye(P)))}


def pos_layout(w):
    swapped = w.reshape(C // 2, 2, C)[:, ::-1].reshape(C, C)
    by_row = np.stack([w.T, swapped.T], 1)
    stack = by_row.reshape(HEADS, DH, 2, C).transpose(1, 0, 2, 3).reshape(DH, HEADS * 2 * C)
    return np.ascontiguousarray(np.concatenate([stack] * 3)), np.ascontiguousarray(by_row)


def window_bias(attn_bias):
    places = [(r, c) for r in range(WS) for c in range(WS)]
    offsets = {}
    index = np.array([[offsets.setdefault((abs(a - c), abs(b - d)), len(offsets)) for c, d in places] for a, b in places])
    out = np.zeros((2, 64, HEADS, WIN), np.float32)
    out[:, :WIN] = attn_bias[:, index].transpose(1, 0, 2)
    return out.reshape(P, HEADS * WIN)


def conv_layout(v):
    def get(name):
        return np.asarray(v["L0_conv_" + name])

    kd, dv = 16, 32
    head_channel = np.arange(C)
    from_x = head_channel % HEADS * DH + head_channel // HEADS
    rows = np.array([[h * DH + c for c in range(kd)] for h in range(HEADS)])
    qkv = get("qkv_w")
    qk = np.zeros((C, 4, C), np.float32)
    for kind in range(2):
        for g in range(2):
            for h in range(HEADS):
                block = qkv[h, kind * kd:(kind + 1) * kd, :]
                qk[from_x[h * DH:(h + 1) * DH][:, None], 2 * kind + g, (rows[h] + g * kd)[None, :]] = block.T
    value = np.zeros((C, 2, 2, dv), np.float32)
    for h in range(HEADS):
        value[from_x[h * DH:(h + 1) * DH], h % 2, h // 2] = qkv[h, 2 * kd:].T
    bn = np.zeros((C, 4, len(BN)), np.float32)
    bn[:, 3, :] = 1.0

    def put(name, params, at=slice(0, C)):
        bn[at, :, BN.index(name)] = params.T

    for name, key in (("dw0", "dw0_bn"), ("ffn0_out", "ffn0_bn2"), ("proj", "proj_bn"), ("dw1", "dw1_bn"), ("ffn1_out", "ffn1_bn2")):
        put(name, get(key))
    for number in range(2):
        for j in range(2):
            put(f"ffn{number}_in{j}", get(f"ffn{number}_bn1")[:, j * C:(j + 1) * C])
    qkv_bn, qdw = get("qkv_bn"), get("qdw_w").reshape(HEADS, kd, 25)
    qtaps = np.zeros((C, 25), np.float32)
    for h in range(HEADS):
        put("value", qkv_bn[h, :, 2 * kd:], slice(h * dv, (h + 1) * dv))
        for g in range(2):
            at = rows[h] + g * kd
            put("q", qkv_bn[h, :, :kd], at)
            put(("k_first", "k_second")[g], qkv_bn[h, :, kd:2 * kd], at)
            put("qdw", get("qdw_bn").reshape(4, HEADS, kd)[:, h], at)
            qtaps[at] = qdw[h]
    taps = np.stack([get("dw0_w").reshape(C, 9), get("dw1_w").reshape(C, 9)], 1)
    ffn_in = np.stack([get("ffn0_w1").T, get("ffn1_w1").T], 1)
    ffn_out = np.stack([get(f"ffn{n}_w2").T.reshape(2, C, C).transpose(1, 0, 2) for n in range(2)], 1)
    group = np.kron(np.eye(C // 4), np.full((4, 4), 0.25 / 4))
    return dict(bn=bn, taps=taps, qtaps=qtaps, ffn_in=ffn_in, ffn_out=ffn_out, qk=qk, value=value.reshape(C, 2, 64),
                proj=get("proj_w").T, window_bias=window_bias(get("attn_bias")), group=group)


def program(nc, NB, a, out):
    after_conv = nc.dram_tensor("after_conv", [NB, C, T], F32, kind="Internal").ap()
    after_attention = nc.dram_tensor("after_attention", [NB, C, T], F32, kind="Internal").ap()
    conv_phase(nc, NB, a["x"], after_conv, a["bn"], a["taps"], a["qtaps"], a["ffn_in"], a["ffn_out"], a["qk"], a["value"],
               a["proj"], a["window_bias"], a["group"], a["ident"])
    attention_phase(nc, NB, after_conv, after_attention, a["gamma"], a["beta"], a["w_qkv"], a["bq"], a["bk"], a["bv"],
                    a["u_bias"], a["v_bias"], a["pos_stack"], a["pos_rows"], a["w_out"], a["b_out"], a["ident"], a["rot"],
                    a["keys"], a["masks"], a["heads"])
    moe_phase(nc, NB, after_attention, out, a["wg"], a["bg"], a["w1"], a["b1"], a["w2"], a["b2"], a["ident"], a["lower"])


def kernel(**inputs):
    import concourse.bacc as bacc
    from concourse.bass_utils import run_bass_kernel_spmd

    v = {name: np.asarray(a) for name, a in inputs.items()}
    NB = v["x"].shape[0]
    arrays = dict(x=v["x"].reshape(NB, C, T), **tables(), **conv_layout(v))
    for name, key in (("gamma", "ln_gamma"), ("beta", "ln_beta"), ("bq", "bq"), ("bk", "bk"), ("bv", "bv"), ("b_out", "bout"),
                      ("u_bias", "u_bias"), ("v_bias", "v_bias")):
        arrays[name] = v["L1_attn_" + key].reshape(C, 1)
    arrays["w_qkv"] = np.stack([v["L1_attn_W" + s] for s in "qkv"], 1)
    arrays["pos_stack"], arrays["pos_rows"] = pos_layout(v["L1_attn_Wpos"])
    arrays["w_out"] = v["L1_attn_Wout"]
    for name, key in (("wg", "Wg"), ("bg", "bg"), ("w1", "W1"), ("w2", "W2"), ("b2", "b2")):
        arrays[name] = v["L1_ffn_" + key]
    arrays["b1"] = v["L1_ffn_b1"].reshape(E, MC, P).transpose(2, 0, 1)

    nc = bacc.Bacc("TRN2", target_bir_lowering=False, num_devices=1)
    sent, aps = {}, {}
    for name, a in arrays.items():
        sent[f"in_{name}"] = np.ascontiguousarray(a, np.float32)
        aps[name] = nc.dram_tensor(f"in_{name}", a.shape, F32, kind="ExternalInput").ap()
    out = nc.dram_tensor("out_0", (NB, C, T), F32, kind="ExternalOutput").ap()
    program(nc, NB, aps, out)
    result = run_bass_kernel_spmd(nc, [sent], core_ids=[0])
    return result.results[0]["out_0"].reshape(v["x"].shape)
```
